# Optimizing a Trainium2 kernel written in Bass

```python
import numpy as np
import jax
import jax.numpy as jnp

def _softmax(x, axis=-1):
    return jax.nn.softmax(x, axis=axis)

def _gelu(x):
    return jax.nn.gelu(x, approximate=True)

def _silu(x):
    return jax.nn.silu(x)

def _sigmoid(x):
    return jax.nn.sigmoid(x)

def _layernorm(x, axis=-1, eps=1e-05):
    m = jnp.mean(x, axis=axis, keepdims=True)
    v = jnp.var(x, axis=axis, keepdims=True)
    return (x - m) / jnp.sqrt(v + eps)

def _scatter_add(tgt, idx, src, axis=0):
    return tgt.at[idx].add(src)

def _segment_sum(src, seg, n):
    return jax.ops.segment_sum(src, seg, n)
kernel_name = 'mk_xattn_ffn_d4_seqx_r4_2afb4a'

def setup_inputs(seed: int=0):
    np.random.seed(seed)
    _w = jnp.asarray

    def _rec_inputs():
        import jax
        import jax.numpy as jnp
        _rk = jax.random.key(seed)
        x = -0.0002928 + 1 * jax.random.normal(jax.random.fold_in(_rk, 1), (16, 112, 256), jnp.float32)
        _lenS = 112 - jax.random.randint(jax.random.fold_in(_rk, 7), (16,), 0, max(1, 112 // 4) + 1, jnp.int32)
        _lenS2 = 375 - jax.random.randint(jax.random.fold_in(_rk, 8), (16,), 0, max(1, 375 // 4) + 1, jnp.int32)
        _ctx_1024P = jax.random.normal(jax.random.fold_in(_rk, 11), (16, 16, 256), jnp.float32)
        _ctx_1024c = jax.random.dirichlet(jax.random.fold_in(_rk, 511), 0.3 * jnp.ones((16,), jnp.float32), (16, 375))
        _ctx_1024t = jnp.einsum('bsk,bkd->bsd', _ctx_1024c, _ctx_1024P)
        _ctx_1024t = _ctx_1024t * jax.lax.rsqrt(jnp.mean(jnp.square(_ctx_1024t)) + 1e-12) * 0.953939
        ctx_1024 = -1.39393e-06 + 0.999914 * (_ctx_1024t + 0.3 * jax.random.normal(jax.random.fold_in(_rk, 611), (16, 375, 256), jnp.float32))
        _validS = jnp.arange(112)[None, :] < _lenS[:, None]
        _validS2 = jnp.arange(375)[None, :] < _lenS2[:, None]
        _causal = jnp.tril(jnp.ones((112, 112), dtype=bool))
        mask_1x1xSxS2_ik0 = jnp.where(jnp.broadcast_to(_validS2[0:1, None, None, :], (1, 1, 112, 375)), 0, 1).astype(jnp.int32)
        mask_SxS2_bk0 = jnp.logical_not(jnp.broadcast_to(_validS2[0:1, :], (112, 375)))
        return (x, ctx_1024, mask_1x1xSxS2_ik0, mask_SxS2_bk0)
    x, ctx_1024, mask_1x1xSxS2_ik0, mask_SxS2_bk0 = _rec_inputs()

    def _L0_xattn_setup():
        import jax, jax.numpy as jnp
        import numpy as np
        import math
        D_MODEL = 256
        NUM_HEADS = 16
        B, S = (2, 512)
        key = jax.random.key(seed)
        ks = jax.random.split(key, 12)
        s = 0.02
        inp = {'q': jax.random.normal(ks[0], (B, S, D_MODEL), jnp.float32), 'k': jax.random.normal(ks[1], (B, S, D_MODEL), jnp.float32), 'v': jax.random.normal(ks[2], (B, S, D_MODEL), jnp.float32), 'W_q': jax.random.normal(ks[3], (D_MODEL, D_MODEL), jnp.float32) * s, 'b_q': jnp.zeros((D_MODEL,), jnp.float32), 'W_k': jax.random.normal(ks[4], (D_MODEL, D_MODEL), jnp.float32) * s, 'b_k': jnp.zeros((D_MODEL,), jnp.float32), 'W_v': jax.random.normal(ks[5], (D_MODEL, D_MODEL), jnp.float32) * s, 'b_v': jnp.zeros((D_MODEL,), jnp.float32), 'W_o': jax.random.normal(ks[6], (D_MODEL, D_MODEL), jnp.float32) * s, 'b_o': jnp.zeros((D_MODEL,), jnp.float32), 'mask': jnp.tril(jnp.ones((S, S), jnp.int32))[None, None, :, :]}
        return inp
    _L0_xattn_all = _L0_xattn_setup()
    _L0_xattn_in = {k: v for k, v in _L0_xattn_all.items() if k in ('W_q', 'b_q', 'W_k', 'b_k', 'W_v', 'b_v', 'W_o', 'b_o')}
    del _L0_xattn_all

    def _L0_ffn_setup():
        import jax, jax.numpy as jnp
        import numpy as np
        B, S, D, E, F, K = (4, 256, 256, 8, 704, 1)
        key = jax.random.key(seed)
        ks = jax.random.split(key, 8)
        sc = 0.02
        return {'x_bsD': jax.random.normal(ks[0], (B, S, D), jnp.float32), 'router_DE': jax.random.normal(ks[1], (D, E), jnp.float32) * sc, 'w1_eDF': jax.random.normal(ks[2], (E, D, F), jnp.float32) * sc, 'w3_eDF': jax.random.normal(ks[3], (E, D, F), jnp.float32) * sc, 'w2_eFD': jax.random.normal(ks[4], (E, F, D), jnp.float32) * sc, 'ws1_DF': jax.random.normal(ks[5], (D, F), jnp.float32) * sc, 'ws3_DF': jax.random.normal(ks[6], (D, F), jnp.float32) * sc, 'ws2_FD': jax.random.normal(ks[7], (F, D), jnp.float32) * sc}
    _L0_ffn_all = _L0_ffn_setup()
    _L0_ffn_in = {k: v for k, v in _L0_ffn_all.items() if k in ('router_DE', 'w1_eDF', 'w3_eDF', 'w2_eFD', 'ws1_DF', 'ws3_DF', 'ws2_FD')}
    del _L0_ffn_all

    def _L1_xattn_setup():
        import jax, jax.numpy as jnp
        import numpy as np
        DIM = 256
        key = jax.random.key(seed)
        ks = jax.random.split(key, 8)
        B, Sx, Sy, D = (4, 512, 512, DIM)
        s = 1.0 / np.sqrt(D)
        return {'x': jax.random.normal(ks[0], (B, Sx, D), jnp.float32), 'y': jax.random.normal(ks[1], (B, Sy, D), jnp.float32), 'Wq': jax.random.normal(ks[2], (D, D), jnp.float32) * s, 'bq': jnp.zeros((D,), jnp.float32), 'Wk': jax.random.normal(ks[3], (D, D), jnp.float32) * s, 'bk': jnp.zeros((D,), jnp.float32), 'Wv': jax.random.normal(ks[4], (D, D), jnp.float32) * s, 'bv': jnp.zeros((D,), jnp.float32)}
    _L1_xattn_all = _L1_xattn_setup()
    _L1_xattn_in = {k: v for k, v in _L1_xattn_all.items() if k in ('Wq', 'bq', 'Wk', 'bk', 'Wv', 'bv')}
    del _L1_xattn_all

    def _L1_ffn_setup():
        import jax, jax.numpy as jnp
        import numpy as np
        D = 256
        H = 192
        E = 8
        K = 2
        NS = 2
        ROUTE_SCALE = 1.0

        def _gated_mlp(x, w1, w2):
            h = x @ w1.T
            y, g = jnp.split(h, 2, axis=-1)
            return y * jax.nn.silu(g) @ w2.T
        key = jax.random.key(seed)
        ks = jax.random.split(key, 6)
        s = 0.02
        return {'x': jax.random.normal(ks[0], (2, 256, D), jnp.float32), 'gate_w': jax.random.normal(ks[1], (E, D), jnp.float32) * s, 'W1': jax.random.normal(ks[2], (E, 2 * H, D), jnp.float32) * s, 'W2': jax.random.normal(ks[3], (E, D, H), jnp.float32) * s, 'Ws1': jax.random.normal(ks[4], (2 * NS * H, D), jnp.float32) * s, 'Ws2': jax.random.normal(ks[5], (D, NS * H), jnp.float32) * s}
    _L1_ffn_all = _L1_ffn_setup()
    _L1_ffn_in = {k: v for k, v in _L1_ffn_all.items() if k in ('gate_w', 'W1', 'W2', 'Ws1', 'Ws2')}
    del _L1_ffn_all

    def _L2_xattn_setup():
        import jax, jax.numpy as jnp
        import numpy as np
        B, NQ, NK = (4, 512, 512)
        QDIM = CDIM = 256
        H, DH = (16, 64)
        SCALE = DH ** (-0.5)
        WSTD = 0.02
        key = jax.random.key(seed)
        ks = jax.random.split(key, 6)
        inner = H * DH
        return {'x': jax.random.normal(ks[0], (B, NQ, QDIM), dtype=jnp.float32), 'context': jax.random.normal(ks[1], (B, NK, CDIM), dtype=jnp.float32), 'Wq': jax.random.normal(ks[2], (inner, QDIM), dtype=jnp.float32) * WSTD, 'Wk': jax.random.normal(ks[3], (inner, CDIM), dtype=jnp.float32) * WSTD, 'Wv': jax.random.normal(ks[4], (inner, CDIM), dtype=jnp.float32) * WSTD, 'Wo': jax.random.normal(ks[5], (QDIM, inner), dtype=jnp.float32) * WSTD, 'bo': jnp.zeros((QDIM,), dtype=jnp.float32)}
    _L2_xattn_all = _L2_xattn_setup()
    _L2_xattn_in = {k: v for k, v in _L2_xattn_all.items() if k in ('Wq', 'Wk', 'Wv', 'Wo', 'bo')}
    del _L2_xattn_all

    def _L2_ffn_setup():
        import jax, jax.numpy as jnp
        import numpy as np
        HIDDEN = 256
        NUM_EXPERTS = 8
        TOP_K = 2
        B, S = (4, 256)
        key = jax.random.key(seed)
        ks = jax.random.split(key, 8)
        H, E = (HIDDEN, NUM_EXPERTS)
        sc = lambda fan_in: 1.0 / np.sqrt(fan_in)
        x = jax.random.normal(ks[0], (B, S, H), dtype=jnp.float32)
        Wr = jax.random.uniform(ks[1], (H, E), minval=-sc(H), maxval=sc(H), dtype=jnp.float32)
        br = jax.random.uniform(ks[2], (E,), minval=-sc(H), maxval=sc(H), dtype=jnp.float32)
        W1 = jax.random.uniform(ks[3], (E, H, 2 * H), minval=-sc(H), maxval=sc(H), dtype=jnp.float32)
        b1 = jax.random.uniform(ks[4], (E, 2 * H), minval=-sc(H), maxval=sc(H), dtype=jnp.float32)
        W2 = jax.random.uniform(ks[5], (E, 2 * H, H), minval=-sc(2 * H), maxval=sc(2 * H), dtype=jnp.float32)
        b2 = jax.random.uniform(ks[6], (E, H), minval=-sc(2 * H), maxval=sc(2 * H), dtype=jnp.float32)
        return {'x': x, 'Wr': Wr, 'br': br, 'W1': W1, 'b1': b1, 'W2': W2, 'b2': b2}
    _L2_ffn_all = _L2_ffn_setup()
    _L2_ffn_in = {k: v for k, v in _L2_ffn_all.items() if k in ('Wr', 'br', 'W1', 'b1', 'W2', 'b2')}
    del _L2_ffn_all

    def _L3_xattn_setup():
        import jax, jax.numpy as jnp
        import numpy as np
        B, S, DIM, H = (4, 512, 256, 16)
        HD = DIM // H
        SCALE = HD ** (-0.5)

        def _heads(x):
            b, s, _ = x.shape
            return x.reshape(b, s, H, HD).transpose(0, 2, 1, 3)
        key = jax.random.key(seed)
        ks = jax.random.split(key, 7)
        init = 0.02
        return {'query': jax.random.normal(ks[0], (B, S, DIM), dtype=jnp.float32), 'key': jax.random.normal(ks[1], (B, S, DIM), dtype=jnp.float32), 'value': jax.random.normal(ks[2], (B, S, DIM), dtype=jnp.float32), 'attn_mask': jnp.tril(jnp.ones((S, S), dtype=bool)), 'Wq': jax.random.normal(ks[3], (DIM, DIM), dtype=jnp.float32) * init, 'Wk': jax.random.normal(ks[4], (DIM, DIM), dtype=jnp.float32) * init, 'Wv': jax.random.normal(ks[5], (DIM, DIM), dtype=jnp.float32) * init, 'Wo': jax.random.normal(ks[6], (DIM, DIM), dtype=jnp.float32) * init}
    _L3_xattn_all = _L3_xattn_setup()
    _L3_xattn_in = {k: v for k, v in _L3_xattn_all.items() if k in ('Wq', 'Wk', 'Wv', 'Wo')}
    del _L3_xattn_all

    def _L3_ffn_setup():
        import jax, jax.numpy as jnp
        import numpy as np
        B, S, D, F, E = (2, 512, 256, 1024, 8)
        LN_EPS = 1e-05

        def _xavier(key, shape, fan_in, fan_out):
            a = np.sqrt(6.0 / (fan_in + fan_out))
            return jax.random.uniform(key, shape, jnp.float32, -a, a)
        key = jax.random.key(seed)
        ks = jax.random.split(key, 8)
        tgt = jax.random.normal(ks[0], (B, S, D), jnp.float32)
        router_w = _xavier(ks[1], (E, D), D, E)
        router_b = jnp.zeros((E,), jnp.float32)
        w1 = _xavier(ks[2], (E, D, F), D, F)
        b1 = jnp.zeros((E, F), jnp.float32)
        w2 = _xavier(ks[3], (E, F, D), F, D)
        b2 = jnp.zeros((E, D), jnp.float32)
        gamma = jnp.ones((D,), jnp.float32)
        beta = jnp.zeros((D,), jnp.float32)
        return {'tgt': tgt, 'router_w': router_w, 'router_b': router_b, 'w1': w1, 'b1': b1, 'w2': w2, 'b2': b2, 'gamma': gamma, 'beta': beta}
    _L3_ffn_all = _L3_ffn_setup()
    _L3_ffn_in = {k: v for k, v in _L3_ffn_all.items() if k in ('router_w', 'router_b', 'w1', 'b1', 'w2', 'b2', 'gamma', 'beta')}
    del _L3_ffn_all
    return {'x': x, 'ctx_1024': ctx_1024, 'mask_1x1xSxS2_ik0': mask_1x1xSxS2_ik0, 'mask_SxS2_bk0': mask_SxS2_bk0, 'L0_xattn_W_q': _L0_xattn_in['W_q'], 'L0_xattn_b_q': _L0_xattn_in['b_q'], 'L0_xattn_W_k': _L0_xattn_in['W_k'], 'L0_xattn_b_k': _L0_xattn_in['b_k'], 'L0_xattn_W_v': _L0_xattn_in['W_v'], 'L0_xattn_b_v': _L0_xattn_in['b_v'], 'L0_xattn_W_o': _L0_xattn_in['W_o'], 'L0_xattn_b_o': _L0_xattn_in['b_o'], 'L0_ffn_router_DE': _L0_ffn_in['router_DE'], 'L0_ffn_w1_eDF': _L0_ffn_in['w1_eDF'], 'L0_ffn_w3_eDF': _L0_ffn_in['w3_eDF'], 'L0_ffn_w2_eFD': _L0_ffn_in['w2_eFD'], 'L0_ffn_ws1_DF': _L0_ffn_in['ws1_DF'], 'L0_ffn_ws3_DF': _L0_ffn_in['ws3_DF'], 'L0_ffn_ws2_FD': _L0_ffn_in['ws2_FD'], 'L1_xattn_Wq': _L1_xattn_in['Wq'], 'L1_xattn_bq': _L1_xattn_in['bq'], 'L1_xattn_Wk': _L1_xattn_in['Wk'], 'L1_xattn_bk': _L1_xattn_in['bk'], 'L1_xattn_Wv': _L1_xattn_in['Wv'], 'L1_xattn_bv': _L1_xattn_in['bv'], 'L1_ffn_gate_w': _L1_ffn_in['gate_w'], 'L1_ffn_W1': _L1_ffn_in['W1'], 'L1_ffn_W2': _L1_ffn_in['W2'], 'L1_ffn_Ws1': _L1_ffn_in['Ws1'], 'L1_ffn_Ws2': _L1_ffn_in['Ws2'], 'L2_xattn_Wq': _L2_xattn_in['Wq'], 'L2_xattn_Wk': _L2_xattn_in['Wk'], 'L2_xattn_Wv': _L2_xattn_in['Wv'], 'L2_xattn_Wo': _L2_xattn_in['Wo'], 'L2_xattn_bo': _L2_xattn_in['bo'], 'L2_ffn_Wr': _L2_ffn_in['Wr'], 'L2_ffn_br': _L2_ffn_in['br'], 'L2_ffn_W1': _L2_ffn_in['W1'], 'L2_ffn_b1': _L2_ffn_in['b1'], 'L2_ffn_W2': _L2_ffn_in['W2'], 'L2_ffn_b2': _L2_ffn_in['b2'], 'L3_xattn_Wq': _L3_xattn_in['Wq'], 'L3_xattn_Wk': _L3_xattn_in['Wk'], 'L3_xattn_Wv': _L3_xattn_in['Wv'], 'L3_xattn_Wo': _L3_xattn_in['Wo'], 'L3_ffn_router_w': _L3_ffn_in['router_w'], 'L3_ffn_router_b': _L3_ffn_in['router_b'], 'L3_ffn_w1': _L3_ffn_in['w1'], 'L3_ffn_b1': _L3_ffn_in['b1'], 'L3_ffn_w2': _L3_ffn_in['w2'], 'L3_ffn_b2': _L3_ffn_in['b2'], 'L3_ffn_gamma': _L3_ffn_in['gamma'], 'L3_ffn_beta': _L3_ffn_in['beta']}

def reference(x, ctx_1024, mask_1x1xSxS2_ik0, mask_SxS2_bk0, L0_xattn_W_q, L0_xattn_b_q, L0_xattn_W_k, L0_xattn_b_k, L0_xattn_W_v, L0_xattn_b_v, L0_xattn_W_o, L0_xattn_b_o, L0_ffn_router_DE, L0_ffn_w1_eDF, L0_ffn_w3_eDF, L0_ffn_w2_eFD, L0_ffn_ws1_DF, L0_ffn_ws3_DF, L0_ffn_ws2_FD, L1_xattn_Wq, L1_xattn_bq, L1_xattn_Wk, L1_xattn_bk, L1_xattn_Wv, L1_xattn_bv, L1_ffn_gate_w, L1_ffn_W1, L1_ffn_W2, L1_ffn_Ws1, L1_ffn_Ws2, L2_xattn_Wq, L2_xattn_Wk, L2_xattn_Wv, L2_xattn_Wo, L2_xattn_bo, L2_ffn_Wr, L2_ffn_br, L2_ffn_W1, L2_ffn_b1, L2_ffn_W2, L2_ffn_b2, L3_xattn_Wq, L3_xattn_Wk, L3_xattn_Wv, L3_xattn_Wo, L3_ffn_router_w, L3_ffn_router_b, L3_ffn_w1, L3_ffn_b1, L3_ffn_w2, L3_ffn_b2, L3_ffn_gamma, L3_ffn_beta):
    import jax
    import jax.numpy as jnp

    def _L0_xattn_ref(q, k, v, W_q, b_q, W_k, b_k, W_v, b_v, W_o, b_o, mask):
        import jax, jax.numpy as jnp
        import numpy as np
        import math
        D_MODEL = 256
        NUM_HEADS = 16
        B, S = (2, 512)
        H, d_k = (NUM_HEADS, D_MODEL // NUM_HEADS)
        Bq, Sq, D = q.shape
        Sk = k.shape[1]
        qh = (q @ W_q.T + b_q).reshape(Bq, Sq, H, d_k).transpose(0, 2, 1, 3)
        kh = (k @ W_k.T + b_k).reshape(Bq, Sk, H, d_k).transpose(0, 2, 1, 3)
        vh = (v @ W_v.T + b_v).reshape(Bq, Sk, H, d_k).transpose(0, 2, 1, 3)
        scores = jnp.einsum('bhqd,bhkd->bhqk', qh, kh) / math.sqrt(d_k)
        scores = jnp.where(mask == 0, jnp.float32(-jnp.inf), scores)
        attn = jax.nn.softmax(scores, axis=-1)
        context = jnp.einsum('bhqk,bhkd->bhqd', attn, vh)
        context = context.transpose(0, 2, 1, 3).reshape(Bq, Sq, D)
        return context @ W_o.T + b_o

    def _L0_ffn_ref(x_bsD, router_DE, w1_eDF, w3_eDF, w2_eFD, ws1_DF, ws3_DF, ws2_FD):
        import jax, jax.numpy as jnp
        import numpy as np
        B, S, D, E, F, K = (4, 256, 256, 8, 704, 1)
        b, s, d = x_bsD.shape
        a = b * s
        x_aD = x_bsD.reshape(a, d)
        scores_aE = x_aD @ router_DE
        vals_aK, idx_aK = jax.lax.top_k(scores_aE, K)
        masked_aE = jnp.full_like(scores_aE, -jnp.inf).at[jnp.arange(a)[:, None], idx_aK].set(vals_aK)
        gates_Ea = jax.nn.sigmoid(masked_aE).T
        routed_in_EaD = jax.lax.stop_gradient(gates_Ea[:, :, None] * x_aD[None, :, :])
        mid_EaF = jax.nn.silu(jnp.einsum('ead,edf->eaf', routed_in_EaD, w1_eDF)) * jnp.einsum('ead,edf->eaf', routed_in_EaD, w3_eDF)
        routed_out_EaD = jnp.einsum('eaf,efd->ead', mid_EaF, w2_eFD)
        shared_aD = jax.nn.silu(x_aD @ ws1_DF) * (x_aD @ ws3_DF) @ ws2_FD
        out_aD = shared_aD + routed_out_EaD.sum(axis=0)
        return out_aD.reshape(b, s, d)

    def _L1_xattn_ref(x, y, Wq, bq, Wk, bk, Wv, bv):
        import jax, jax.numpy as jnp
        import numpy as np
        DIM = 256
        D = x.shape[-1]
        scale = jnp.sqrt(jnp.asarray(D, x.dtype))
        Q = jnp.einsum('bsd,de->bse', x, Wq) + bq
        K = jnp.einsum('btd,de->bte', y, Wk) + bk
        V = jnp.einsum('btd,de->bte', y, Wv) + bv
        scores = jnp.einsum('bse,bte->bst', Q, K) / scale
        probs = jax.nn.softmax(scores, axis=-1)
        out = jnp.einsum('bst,bte->bse', probs, V)
        return out

    def _L1_ffn_ref(x, gate_w, W1, W2, Ws1, Ws2):
        import jax, jax.numpy as jnp
        import numpy as np
        D = 256
        H = 192
        E = 8
        K = 2
        NS = 2
        ROUTE_SCALE = 1.0

        def _gated_mlp(x, w1, w2):
            h = x @ w1.T
            y, g = jnp.split(h, 2, axis=-1)
            return y * jax.nn.silu(g) @ w2.T
        x_shape = x.shape
        xf = x.reshape(-1, D)
        T = xf.shape[0]
        scores = jax.nn.softmax((xf @ gate_w.T).astype(jnp.float32), axis=-1)
        top_vals, top_idx = jax.lax.top_k(scores, K)
        weights = (top_vals * ROUTE_SCALE).astype(x.dtype)
        w_dense = jnp.zeros((T, E), x.dtype).at[jnp.arange(T)[:, None], top_idx].set(weights)
        h = jnp.einsum('td,ehd->teh', xf, W1)
        y, g = jnp.split(h, 2, axis=-1)
        eo = jnp.einsum('teh,edh->ted', y * jax.nn.silu(g), W2)
        z = jnp.einsum('te,ted->td', w_dense, eo)
        z = z + _gated_mlp(xf, Ws1, Ws2)
        return z.reshape(x_shape)

    def _L2_xattn_ref(x, context, Wq, Wk, Wv, Wo, bo):
        import jax, jax.numpy as jnp
        import numpy as np
        B, NQ, NK = (4, 512, 512)
        QDIM = CDIM = 256
        H, DH = (16, 64)
        SCALE = DH ** (-0.5)
        WSTD = 0.02
        b, nq, _ = x.shape
        nk = context.shape[1]
        q = (x @ Wq.T).reshape(b, nq, H, DH)
        k = (context @ Wk.T).reshape(b, nk, H, DH)
        v = (context @ Wv.T).reshape(b, nk, H, DH)
        sim = jnp.einsum('bihd,bjhd->bhij', q, k) * SCALE
        attn = jax.nn.softmax(sim, axis=-1)
        out = jnp.einsum('bhij,bjhd->bihd', attn, v).reshape(b, nq, H * DH)
        return out @ Wo.T + bo

    def _L2_ffn_ref(x, Wr, br, W1, b1, W2, b2):
        import jax, jax.numpy as jnp
        import numpy as np
        HIDDEN = 256
        NUM_EXPERTS = 8
        TOP_K = 2
        B, S = (4, 256)
        B_, S_, H = x.shape
        xf = x.reshape(-1, H)
        logits = xf @ Wr + br
        topk_w, topk_idx = jax.lax.top_k(logits, TOP_K)
        topk_w = jax.nn.softmax(topk_w, axis=-1)
        gate = jnp.sum(jax.nn.one_hot(topk_idx, NUM_EXPERTS, dtype=xf.dtype) * topk_w[..., None], axis=1)
        h = jax.nn.relu(jnp.einsum('th,ehf->etf', xf, W1) + b1[:, None, :])
        y = jnp.einsum('etf,efh->eth', h, W2) + b2[:, None, :]
        out = jnp.einsum('te,eth->th', gate, y)
        return out.reshape(B_, S_, H)

    def _L3_xattn_ref(query, key, value, attn_mask, Wq, Wk, Wv, Wo):
        import jax, jax.numpy as jnp
        import numpy as np
        B, S, DIM, H = (4, 512, 256, 16)
        HD = DIM // H
        SCALE = HD ** (-0.5)

        def _heads(x):
            b, s, _ = x.shape
            return x.reshape(b, s, H, HD).transpose(0, 2, 1, 3)
        q = _heads(query @ Wq.T)
        k = _heads(key @ Wk.T)
        v = _heads(value @ Wv.T)
        logits = jnp.einsum('bhqd,bhkd->bhqk', q, k) * SCALE
        mask = attn_mask[None, None, :, :]
        masked = jnp.where(mask, logits, -1000000000.0)
        weights = jax.nn.softmax(masked, axis=-1)
        weights = weights * mask.astype(weights.dtype)
        denom = jnp.maximum(weights.sum(axis=-1, keepdims=True), 1e-09)
        weights = weights / denom
        out = jnp.einsum('bhqk,bhkd->bhqd', weights, v)
        out = out.transpose(0, 2, 1, 3).reshape(query.shape[0], query.shape[1], -1)
        return out @ Wo.T

    def _L3_ffn_ref(tgt, router_w, router_b, w1, b1, w2, b2, gamma, beta):
        import jax, jax.numpy as jnp
        import numpy as np
        B, S, D, F, E = (2, 512, 256, 1024, 8)
        LN_EPS = 1e-05

        def _xavier(key, shape, fan_in, fan_out):
            a = np.sqrt(6.0 / (fan_in + fan_out))
            return jax.random.uniform(key, shape, jnp.float32, -a, a)
        logits = jnp.einsum('bsd,ed->bse', tgt, router_w) + router_b
        rw = jax.nn.softmax(logits, axis=-1)
        rw = jnp.zeros_like(rw).at[..., 0].set(1.0)
        h = jax.nn.relu(jnp.einsum('bsd,edf->besf', tgt, w1) + b1[None, :, None, :])
        eo = jnp.einsum('besf,efd->besd', h, w2) + b2[None, :, None, :]
        tgt2 = jnp.einsum('besd,bse->bsd', eo, rw)
        x = tgt + tgt2
        mean = jnp.mean(x, axis=-1, keepdims=True)
        var = jnp.mean(jnp.square(x - mean), axis=-1, keepdims=True)
        return (x - mean) * jax.lax.rsqrt(var + LN_EPS) * gamma + beta
    x = x + _L0_xattn_ref(_layernorm(x, axis=-1), ctx_1024, ctx_1024, L0_xattn_W_q, L0_xattn_b_q, L0_xattn_W_k, L0_xattn_b_k, L0_xattn_W_v, L0_xattn_b_v, L0_xattn_W_o, L0_xattn_b_o, mask_1x1xSxS2_ik0)
    x = x + _L0_ffn_ref(_layernorm(x, axis=-1), L0_ffn_router_DE, L0_ffn_w1_eDF, L0_ffn_w3_eDF, L0_ffn_w2_eFD, L0_ffn_ws1_DF, L0_ffn_ws3_DF, L0_ffn_ws2_FD)
    x = x + _L1_xattn_ref(_layernorm(x, axis=-1), ctx_1024, L1_xattn_Wq, L1_xattn_bq, L1_xattn_Wk, L1_xattn_bk, L1_xattn_Wv, L1_xattn_bv)
    x = x + _L1_ffn_ref(_layernorm(x, axis=-1), L1_ffn_gate_w, L1_ffn_W1, L1_ffn_W2, L1_ffn_Ws1, L1_ffn_Ws2)
    x = x + _L2_xattn_ref(_layernorm(x, axis=-1), ctx_1024, L2_xattn_Wq, L2_xattn_Wk, L2_xattn_Wv, L2_xattn_Wo, L2_xattn_bo)
    x = x + _L2_ffn_ref(_layernorm(x, axis=-1), L2_ffn_Wr, L2_ffn_br, L2_ffn_W1, L2_ffn_b1, L2_ffn_W2, L2_ffn_b2)
    x = x + _L3_xattn_ref(_layernorm(x, axis=-1), ctx_1024, ctx_1024, mask_SxS2_bk0, L3_xattn_Wq, L3_xattn_Wk, L3_xattn_Wv, L3_xattn_Wo)
    x = x + _L3_ffn_ref(_layernorm(x, axis=-1), L3_ffn_router_w, L3_ffn_router_b, L3_ffn_w1, L3_ffn_b1, L3_ffn_w2, L3_ffn_b2, L3_ffn_gamma, L3_ffn_beta)
    return x

_drawn_inputs = setup_inputs


def setup_inputs(seed=0):
    import zlib

    import numpy as np

    out = dict(_drawn_inputs(seed))
    spreads = {'L0_xattn_b_q': (0.0, 0.8),
     'L0_xattn_b_k': (0.0, 2.0),
     'L0_xattn_b_v': (0.0, 0.1),
     'L0_xattn_b_o': (0.0, 0.1),
     'L1_xattn_bq': (0.0, 0.281),
     'L1_xattn_bk': (0.0, 2.0),
     'L1_xattn_bv': (0.0, 0.1),
     'L2_xattn_bo': (0.0, 0.482),
     'L3_ffn_router_b': (0.0, 0.1),
     'L3_ffn_b1': (0.0, 2.0),
     'L3_ffn_b2': (0.0, 1.732),
     'L3_ffn_gamma': (1.0, 0.6),
     'L3_ffn_beta': (0.0, 0.592)}
    factors = {'L0_xattn_W_q': 8.0,
     'L0_xattn_W_k': 8.0,
     'L0_ffn_router_DE': 3.973,
     'L0_ffn_w1_eDF': 4.153,
     'L0_ffn_w3_eDF': 4.019,
     'L0_ffn_w2_eFD': 4.139,
     'L1_ffn_gate_w': 7.959,
     'L1_ffn_W1': 7.323,
     'L1_ffn_W2': 8.0,
     'L2_xattn_Wq': 29.066,
     'L2_xattn_Wk': 32.993,
     'L2_ffn_b1': 94.289,
     'L2_ffn_b2': 18.651,
     'L3_xattn_Wq': 33.348,
     'L3_xattn_Wk': 33.114,
     'L1_ffn_Ws1': 8.0,
     'L1_ffn_Ws2': 8.0,
     'L2_ffn_br': 22.282,
     'L3_xattn_Wv': 3.482,
     'L3_xattn_Wo': 3.46,
     'L2_xattn_Wv': 3.617,
     'L2_xattn_Wo': 3.638,
     'L2_ffn_W1': 4.973}
    for name, (base, spread) in spreads.items():
        noise = np.random.default_rng([zlib.crc32(name.encode()), seed]).standard_normal(out[name].shape)
        drawn = base * np.exp(spread * noise) if base else spread * noise
        out[name] = jnp.asarray(drawn.astype(out[name].dtype))
    for name, factor in factors.items():
        out[name] = (out[name] * factor).astype(out[name].dtype)
    return out
```

```python
from contextlib import ExitStack

import concourse.bass as bass
import numpy as np
from concourse import mybir

F32 = mybir.dt.float32
I32 = mybir.dt.int32
U8 = mybir.dt.uint8
ALU = mybir.AluOpType
ACT = mybir.ActivationFunctionType
AX_X = mybir.AxisListType.X

P = 128
B = 16
S = 112
SK = 375
KT = 125
NKT = SK // KT
D = 256
ND = D // P
E = 8
CHUNK = 4
NCH = B // CHUNK
TOK = CHUNK * S
CREDIT = 8
EPS = 1e-5
BIG = 1e30

ATT = {
    0: dict(H=16, dh=16, scale=0.25, fill=1e30, bq=True, bk=True, bv=True, wo=True, bo=True),
    1: dict(H=1, dh=256, scale=1 / 16, fill=None, bq=True, bk=True, bv=True, wo=False, bo=False),
    2: dict(H=16, dh=64, scale=0.125, fill=None, bq=False, bk=False, bv=False, wo=True, bo=True),
    3: dict(H=16, dh=16, scale=0.25, fill=1e9, bq=False, bk=False, bv=False, wo=True, bo=False),
}
FFN = {
    0: dict(F=704, NE=9, gated=True),
    1: dict(F=192, NE=10, gated=True),
    2: dict(F=512, NE=8, gated=False),
    3: dict(F=1024, NE=1, gated=False),
}


def ftiles(F):
    return [(o, min(P, F - o)) for o in range(0, F, P)]


class Att:

    def __init__(self, L, sem):
        a = ATT[L]
        self.L, self.H, self.dh = L, a["H"], a["dh"]
        self.a = a
        self.W = self.H * self.dh
        self.NO = self.W // P
        self.per = max(1, P // self.dh)
        self.KH = max(1, self.dh // P)
        self.VH = max(1, self.W // 512)
        self.VW = self.W // self.VH
        self.masked = a["fill"] is not None
        self.plan = self.steps()
        self.gens = [s for s in self.plan if s[0] == "gen"]
        self.NG = len(self.gens)
        assert self.NG % 2 == 0
        n = lambda s: sem(f"l{L}a_{s}")
        self.ctx_landed = [n(f"ctx_landed{k}") for k in range(2)]
        self.gen_ready = n("gen_ready")
        self.gen_free = [n(f"gen_evacuated{k}") for k in range(2)]
        self.scores = n("scores_ready")
        self.maxed = n("max_ready")
        self.probs = n("probs_ready")
        self.pt_psum = n("probsT_in_psum")
        self.pt_sbuf = n("probsT_in_sbuf")
        self.pv = n("pv_ready")
        self.norm = n("heads_normalised")
        self.chain = n("dve_chain")

    def steps(self):
        H = self.H
        proj = lambda bb: ([("gen", "q", bb, o, 0) for o in range(self.NO)]
                           + [("gen", "k", bb, o, 0) for o in range(self.NO)]
                           + [("gen", "v", bb, kt, h) for kt in range(NKT) for h in range(self.VH)])
        late = lambda bb: ([("gen", "t", bb, o, 0) for o in range(0, self.NO, 4)] + [("gen", "o", bb, 0, 0)]
                           if self.a["wo"] else [])
        plan = proj(0)
        nxt, done = proj(1), []
        for g in range(2 * H + 3):
            if g == H:
                plan += nxt
                nxt = []
            if g < 2 * H:
                plan.append(("scores", g))
            if 2 <= g < 2 * H + 2:
                plan.append(("turn", g - 2))
            if g >= 3:
                plan.append(("pv", g - 3))
                if (g - 3) % H == H - 1:
                    bb = (g - 3) // H
                    plan.append(("norm", bb))
                    done = late(bb)
            if 2 <= g < H and nxt:
                k = -(-len(nxt) // max(1, H - g - 1))
                plan += nxt[:k]
                nxt = nxt[k:]
            if done and ((g - 3) % H == 2 or g == 2 * H + 2):
                plan += done
                done = []
        out, n = [], 0
        for s in plan + done:
            if s[0] == "gen":
                s = s + (n,)
                n += 1
            out.append(s)
        return out

    def gen_index(self, kind, bb, o=0, h=0):
        return next(s[5] for s in self.gens if s[1:5] == (kind, bb, o, h))


class Ffn:
    def __init__(self, L, sem):
        f = FFN[L]
        self.L, self.gated, self.NE, self.F = L, f["gated"], f["NE"], f["F"]
        self.tiles = ftiles(f["F"])
        self.NF = len(self.tiles)
        self.loop = self.NE // 2
        self.NU = 2 if self.gated else 1
        n = lambda s: sem(f"l{L}f_{s}")
        self.w_landed = [n(f"weights_landed{k}") for k in range(2)]
        self.hid = n("hidden_ready")
        self.act = n("activation_done")
        self.mid = n("mid_ready")
        self.out = n("out_ready")
        self.added = n("out_added")
        self.r_ps = n("router_psum")
        self.r_act = n("router_act")
        self.r_dve = n("router_dve")
        self.r_in = n("router_input")
        self.r_out = n("router_scaledT")
        if not self.gated:
            self.act = self.mid


class Ln:

    def __init__(self, sem):
        self.dve = sem("ln_dve")
        self.act = sem("ln_std")
        self.xn = sem("ln_xn")
        self.ps = sem("ln_psum")
        self.xT = sem("ln_xT")

    def at(self, k):
        return k * (2 * B + 2), k * B + CREDIT


def build(nc, A):
    ctx = ExitStack()
    with ctx:
        sb = lambda name, shape, dt=F32: ctx.enter_context(nc.sbuf_tensor(name, shape, dt))
        sem = lambda name: ctx.enter_context(nc.semaphore(name))
        bank = [ctx.enter_context(nc.psum_tensor(f"bank{k}", [P, 512], F32)) for k in range(8)]

        x = sb("x", [S, B * D])
        xnT = sb("xnT", [P, ND, B * S])
        ident = sb("ident", [P, P])
        sel = {16: sb("sel16", [P, 8]), 64: sb("sel64", [P, 2])}
        stats = sb("stats", [S, B, 6])
        mv = sb("mv", [S, B, 2])
        std = sb("std", [S, B])
        rstd = sb("rstd", [S, B])
        nmr = sb("nmr", [S, B])
        xn = sb("xn", [S, 2, D])
        epsc = sb("epsc", [P, 1])

        ctxT = sb("ctxT", [P, 2, ND, SK])
        kT = sb("kT", [P, 2, 8 * SK])
        V = sb("V", [KT, 2, NKT * 1024])
        qm = sb("qm", [P, 2, 16 * S])
        sm = sb("sm", [S, 2, SK])
        pr = sb("pr", [S, 2, SK])
        pT = sb("pT", [KT, 2, NKT * S])
        on = sb("on", [S, 1024])
        oT = sb("oT", [P, 8 * S])
        mx = sb("mx", [S, 2])
        sums = sb("sums", [S, 2, 16])
        rinv = sb("rinv", [S, 2, 16])
        maskf = sb("maskf", [S, SK])
        maski = sb("maski", [S, SK], I32)
        maskb = sb("maskb", [S, SK], U8)
        flag = sb("flag", [S, 2])
        fac = sb("fac", [S, 1])
        wA = sb("wA", [P, 4, ND * D])
        w2A = sb("w2A", [P, 4, 2048])
        biasA = sb("biasA", [P, 3, ND])
        bvB = sb("bvB", [P, D])
        boB = sb("boB", [P, D])

        wF = sb("wF", [P, 2, 2 * 704 * 2 + 6 * D])
        hg = sb("hg", [P, 2, TOK])
        mid = sb("mid", [P, 2, TOK])
        wR = sb("wR", [P, ND, E])
        brB = sb("brB", [S, E])
        tab = [a[:, :, :].rearrange("p b t -> p (b t)") for a in (sm, pr)]
        t8 = [tab[k // 5][:, k % 5 * B * E:(k % 5 + 1) * B * E].rearrange("p (b e) -> p b e", e=E)
              for k in range(6)]
        lg = tab[1][:, B * E:2 * B * E].rearrange("p (b e) -> p b e", e=E)
        t1 = [sb(f"t1_{k}", [S, B]) for k in range(6)]
        gate = sb("gate", [S, 10 * B])
        b1 = sb("b1", [P, 40])
        b2 = sb("b2", [E, D])
        gB = on[:, 0:2 * D].rearrange("p (k d) -> p k d", d=D)

        consts = sem("constants_ready")
        loaded = {k: sem(f"loaded_{k}") for k in ["x", "w0", "w1", "w2", "w3", "mask", "bias0", "bias1", "bo2",
                                                  "r0", "r1", "r2", "b12", "b13", "b2", "b23", "gb", "seed"]}
        stage_done = sem("stage_done")
        stored = sem("stored")
        settled = sem("settled")
        att = [Att(L, sem) for L in range(4)]
        ffn = [Ffn(L, sem) for L in range(4)]
        ln = Ln(sem)
        fin = sem("final_chain")

        kTv = lambda p, NO: kT[:, p, 0:NO * SK].rearrange("p (o t) -> p o t", t=SK)
        Vv = lambda p, W: V[:, p, 0:NKT * W].rearrange("p (k w) -> p k w", w=W)
        qmv = qm[:, :, :].rearrange("p b (h t) -> p b h t", t=S)
        prv = pr
        pTv = pT[:, :, :].rearrange("p b (k t) -> p b k t", t=S)
        oTv = oT[:, :].rearrange("p (o t) -> p o t", t=S)
        gxT = kT[:, :, :].rearrange("p b n -> p (b n)")[:, 0:ND * B * S].rearrange("p (k t) -> p k t", k=ND)
        gateT = qm[0:E, 0, :]
        xb = lambda b: x[:, b * D:(b + 1) * D]
        xd = lambda i, bb: x[:, bass.ds(i * (2 * D) + bb * D, D)]

        def w_att(L, k):
            if L == 2:
                return w2A[:, k, :].rearrange("p (k n) -> p k n", k=ND if k < 3 else 8)
            return wA[:, k, :].rearrange("p (k n) -> p k n", k=ND)

        def w_ffn(f, slot):
            F = f.F
            n = ND * F
            up = [wF[:, slot, u * n:(u + 1) * n].rearrange("p (k f) -> p k f", k=ND) for u in range(f.NU)]
            w2 = wF[:, slot, f.NU * n:f.NU * n + f.NF * D]
            return up, w2.rearrange("p (t n) -> p t n", n=D)

        block = ctx.enter_context(nc.Block())

        def finish(eng, n):
            eng.drain().then_inc(stage_done, 1)
            eng.wait_ge(stage_done, 3 * (n + 1))

        def settle(eng):
            eng.sem_inc(settled, 1)

        def ln_stats(dve, k, of):
            at, _ = ln.at(k)
            for b in range(B):
                dve.bn_stats(stats[:, b, :], of(b)).then_inc(ln.dve, 1)
            for b in range(B):
                dve.wait_ge(ln.dve, at + b + 1)
                dve.bn_aggr(mv[:, b, :], stats[:, b, :]).then_inc(ln.dve, 1)
            dve.wait_ge(ln.act, k + 1)
            dve.reciprocal(rstd[:, :], std[:, :]).then_inc(ln.dve, 1)
            dve.wait_ge(ln.dve, at + 2 * B + 1)
            dve.scalar_tensor_tensor(out=nmr[:, :], in0=mv[:, :, 0], scalar=-1.0, in1=rstd[:, :],
                                     op0=ALU.mult, op1=ALU.mult).then_inc(ln.dve, 1)
            dve.wait_ge(ln.dve, at + 2 * B + 2)

        def ln_std(act, k):
            act.wait_ge(ln.dve, ln.at(k)[0] + 2 * B)
            act.activation(std[:, :], mv[:, :, 1], ACT.Sqrt, bias=epsc[0:S, :]).then_inc(ln.act, 1)

        def ln_vector(dve, k):
            ln_stats(dve, k, xb)
            _, at = ln.at(k)
            with dve.Fori(0, B // 2) as i:
                for bb in range(2):
                    dve.wait_ge(ln.ps, i * 2 + bb + at - 1)
                    dve.tensor_scalar(xn[:, bb, :], xd(i, bb), rstd[:, bass.ds(i * 2 + bb, 1)],
                                      nmr[:, bass.ds(i * 2 + bb, 1)], ALU.mult, ALU.add).then_inc(ln.xn, 1)

        def ln_scalar(act, k):
            ln_std(act, k)
            _, at = ln.at(k)
            with act.Fori(0, B // 2) as i:
                for bb in range(2):
                    act.wait_ge(ln.ps, i * 2 + bb + at + 1)
                    settle(act)
                    act.activation(xnT[:, :, bass.ds((i * 2 + bb) * S, S)],
                                   bank[bb][:, 0:ND * S].rearrange("p (k t) -> p k t", k=ND),
                                   ACT.Copy).then_inc(ln.xT, 1)

        def ln_tensor(pe, k):
            _, at = ln.at(k)
            with pe.Fori(0, B // 2) as i:
                for bb in range(2):
                    pe.wait_ge(ln.xn, i * 2 + bb + at + 1)
                    pe.wait_ge(ln.xT, i * 2 + bb + at - 1)
                    for c in range(ND):
                        t = pe.transpose(bank[bb][:, c * S:(c + 1) * S], xn[:, bb, c * P:(c + 1) * P],
                                         ident[0:S, 0:S])
                    t.then_inc(ln.ps, 1)

        def att_sync(sp, t):
            with sp.Fori(0, B // 2) as i:
                for bb in range(2):
                    last = t.gen_index("v", bb, NKT - 1, t.VH - 1)
                    sp.wait_ge(t.gen_ready, i * t.NG + last + 1 - t.NG + 64)
                    sp.dma_start(ctxT[:, bb, :, :],
                                 A["ctxT"][bass.ds(i * 2 + bb, 1), :, :, :].rearrange("a p k t -> (a p) k t"))\
                        .then_inc(t.ctx_landed[bb], 16)

        def att_tensor(pe, t):
            L, H, dh, per = t.L, t.H, t.dh, t.per
            w = [w_att(L, k) for k in range(4)]
            pe.sem_inc(t.gen_ready, 64)
            for s in (t.scores, t.pt_psum, t.pv):
                pe.sem_inc(s, CREDIT)
            pe.wait_ge(loaded[f"w{L}"], 16 * (4 if t.a["wo"] else 3))
            with pe.Fori(0, B // 2) as i:
                def gen(kind, bb, o, h, n):
                    k = n % 2
                    dst = bank[6 + k]
                    pe.wait_ge(t.gen_free[k], i * (t.NG // 2) + n // 2 + CREDIT)
                    if kind == "q":
                        for c in range(ND):
                            m = pe.matmul(dst[:, 0:S], w[0][:, c, o * P:(o + 1) * P],
                                          xnT[:, c, bass.ds((i * 2 + bb) * S, S)],
                                          start=(c == 0), stop=(c == ND - 1))
                    elif kind == "k":
                        if o == 0:
                            pe.wait_ge(t.ctx_landed[bb], i * 16 + 16)
                        for c in range(ND):
                            m = pe.matmul(dst[:, 0:SK], w[1][:, c, o * P:(o + 1) * P], ctxT[:, bb, c, :],
                                          start=(c == 0), stop=(c == ND - 1))
                    elif kind == "v":
                        for c in range(ND):
                            m = pe.matmul(dst[0:KT, 0:t.VW], ctxT[:, bb, c, o * KT:(o + 1) * KT],
                                          w[2][:, c, h * t.VW:(h + 1) * t.VW],
                                          start=(c == 0), stop=(c == ND - 1))
                    elif kind == "t":
                        if o == 0:
                            pe.wait_ge(t.norm, i * 2 + bb + 1 + CREDIT)
                        for j in range(min(4, t.NO)):
                            m = pe.transpose(dst[:, j * S:(j + 1) * S], on[:, (o + j) * P:(o + j + 1) * P],
                                             ident[0:S, 0:S])
                    else:
                        last = t.gen_index("t", bb, (t.NO - 1) // 4 * 4)
                        pe.wait_ge(t.gen_free[last % 2], i * (t.NG // 2) + last // 2 + 1 + CREDIT)
                        for j in range(t.NO):
                            m = pe.matmul(dst[0:S, 0:D], oTv[:, j, :], w[3][:, j, :],
                                          start=(j == 0), stop=(j == t.NO - 1))
                    m.then_inc(t.gen_ready, 1)

                for s in t.plan:
                    if s[0] == "gen":
                        gen(*s[1:])
                        continue
                    g = s[1]
                    if s[0] == "norm":
                        continue
                    bb, h = g // H, g % H
                    at = i * (2 * H) + CREDIT
                    if s[0] == "scores":
                        if h == 0:
                            for o in range(t.NO - 2, t.NO):
                                n = t.gen_index("k", bb, o)
                                pe.wait_ge(t.gen_free[n % 2], i * (t.NG // 2) + n // 2 + 1 + CREDIT)
                        pe.wait_ge(t.maxed if t.masked else t.probs, at + g - 1)
                        for c in range(t.KH):
                            m = pe.matmul(bank[g % 2][0:S, 0:SK], qmv[:, bb, h * t.KH + c, :],
                                          kTv(bb, t.NO)[:, h // per * t.KH + c, :],
                                          start=(c == 0), stop=(c == t.KH - 1))
                        m.then_inc(t.scores, 1)
                    elif s[0] == "turn":
                        pe.wait_ge(t.probs, at + g + 1)
                        pe.wait_ge(t.pt_sbuf, at + g - 1)
                        for k in range(NKT):
                            m = pe.transpose(bank[2 + g % 2][0:KT, k * S:(k + 1) * S],
                                             prv[:, g % 2, k * KT:(k + 1) * KT], ident[0:S, 0:S])
                        m.then_inc(t.pt_psum, 1)
                    else:
                        pe.wait_ge(t.pt_sbuf, at + g + 1)
                        if h == 0:
                            for n in range(2):
                                o, hh = divmod(NKT * t.VH - 1 - n, t.VH)
                                v = t.gen_index("v", bb, o, hh)
                                pe.wait_ge(t.gen_free[v % 2], i * (t.NG // 2) + v // 2 + 1 + CREDIT)
                            pe.wait_ge(t.norm, i * 2 + bb + CREDIT - (0 if L == 2 else 1))
                        ob, col = (4 + h // 8, h % 8 * dh) if L == 2 else (4 + bb, h * dh)
                        for k in range(NKT):
                            m = pe.matmul(bank[ob][0:S, col:col + dh], pTv[:, g % 2, k, :],
                                          Vv(bb, t.W)[:, k, h * dh:(h + 1) * dh],
                                          start=(k == 0), stop=(k == NKT - 1))
                        m.then_inc(t.pv, 1)

        def att_vector(dve, t):
            L, H, dh, per = t.L, t.H, t.dh, t.per
            for s in (t.maxed, t.pt_sbuf, t.norm, *t.gen_free):
                dve.sem_inc(s, CREDIT)
            n_chain = 0
            if t.masked:
                dve.wait_ge(loaded["mask"], 32)
                m = maski if L == 0 else maskb
                dve.tensor_scalar(maskf[:, :], m[:, :], 0.0, t.a["fill"], ALU.is_equal, ALU.mult)\
                    .then_inc(t.chain, 1)
                dve.tensor_scalar(sm[:, 0, :], m[:, :], 0.0, None, ALU.not_equal).then_inc(t.chain, 1)
                dve.wait_ge(t.chain, 2)
                dve.tensor_reduce(flag[:, 0:1], sm[:, 0, :], AX_X, ALU.max).then_inc(t.chain, 1)
                dve.wait_ge(t.chain, 3)
                if L == 0:
                    dve.reciprocal(flag[:, 1:2], flag[:, 0:1]).then_inc(t.chain, 1)
                else:
                    dve.tensor_scalar(flag[:, 1:2], flag[:, 0:1], 1e-9, None, ALU.max).then_inc(t.chain, 1)
                    dve.wait_ge(t.chain, 4)
                    dve.reciprocal(flag[:, 1:2], flag[:, 1:2]).then_inc(t.chain, 1)
                n_chain = 4 if L == 0 else 5
                dve.wait_ge(t.chain, n_chain)
                dve.tensor_tensor(fac[:, :], flag[:, 0:1], flag[:, 1:2], ALU.mult).then_inc(t.chain, 1)
                n_chain += 1
                dve.wait_ge(t.chain, n_chain)
            if L == 1:
                dve.wait_ge(loaded["bias1"], 48)
            if t.a["bo"]:
                dve.wait_ge(loaded["bias0"] if L == 0 else loaded["bo2"], 16 * (4 if L == 0 else 1))
                dve.tensor_tensor(x[:, :].rearrange("p (b d) -> p b d", d=D),
                                  x[:, :].rearrange("p (b d) -> p b d", d=D),
                                  boB[0:S, :].unsqueeze(1).broadcast_to([S, B, D]), ALU.add)\
                    .then_inc(t.chain, 1)
                n_chain += 1
                dve.wait_ge(t.chain, n_chain)
            NC = 2 if t.masked else 1
            qscale = -t.a["scale"]
            with dve.Fori(0, B // 2) as i:
                def gen(kind, bb, o, h, n):
                    k = n % 2
                    src = bank[6 + k]
                    if kind in ("k", "t") or (kind == "v" and not t.a["bv"]):
                        return
                    dve.wait_ge(t.gen_ready, i * t.NG + n + 1 + 64)
                    if kind == "q":
                        if H == 1:
                            ins = dve.tensor_scalar(qmv[:, bb, o, :], src[:, 0:S], biasA[:, 0, o:o + 1],
                                                    qscale, ALU.add, ALU.mult)
                        elif t.a["bq"]:
                            ins = dve.scalar_tensor_tensor(
                                out=qmv[:, bb, o * per:(o + 1) * per, :],
                                in0=src[:, 0:S].unsqueeze(1).broadcast_to([P, per, S]),
                                scalar=biasA[:, 0, o:o + 1],
                                in1=sel[dh][:, :].unsqueeze(2).broadcast_to([P, per, S]),
                                op0=ALU.add, op1=ALU.mult)
                        else:
                            ins = dve.tensor_tensor(
                                qmv[:, bb, o * per:(o + 1) * per, :],
                                src[:, 0:S].unsqueeze(1).broadcast_to([P, per, S]),
                                sel[dh][:, :].unsqueeze(2).broadcast_to([P, per, S]), ALU.mult)
                    elif kind == "v":
                        ins = dve.tensor_tensor(Vv(bb, t.W)[:, o, h * t.VW:(h + 1) * t.VW],
                                                src[0:KT, 0:t.VW], bvB[0:KT, :], ALU.add)
                    else:
                        ins = dve.tensor_tensor(xd(i, bb), src[0:S, 0:D], xd(i, bb), ALU.add)
                    ins.then_inc(t.gen_free[k], 1)

                for s in t.plan:
                    if s[0] == "gen":
                        gen(*s[1:])
                        continue
                    at = i * (2 * H) + CREDIT
                    if s[0] == "scores":
                        g = s[1]
                        dve.wait_ge(t.scores, at + g + 1)
                        dve.wait_ge(t.probs, at + g - 1)
                        if t.masked:
                            settle(dve)
                            dve.tensor_tensor_reduce(sm[:, g % 2, :], bank[g % 2][0:S, 0:SK], maskf[:, :],
                                                     1.0, 3e38, ALU.add, ALU.min, mx[:, g % 2:g % 2 + 1])\
                                .then_inc(t.maxed, 1)
                        else:
                            dve.tensor_reduce(mx[:, g % 2:g % 2 + 1], bank[g % 2][0:S, 0:SK], AX_X, ALU.min)\
                                .then_inc(t.maxed, 1)
                    elif s[0] == "turn":
                        g = s[1]
                        dve.wait_ge(t.pt_psum, at + g + 1)
                        dve.wait_ge(t.pv, at + g - 1)
                        dve.tensor_copy(pT[:, g % 2, :], bank[2 + g % 2][0:KT, 0:NKT * S])\
                            .then_inc(t.pt_sbuf, 1)
                    elif s[0] == "norm":
                        bb = s[1]
                        c0 = i * (2 * NC) + bb * NC + n_chain
                        dve.wait_ge(t.pv, at + (bb + 1) * H)
                        dve.reciprocal(rinv[:, bb, 0:H], sums[:, bb, 0:H]).then_inc(t.chain, 1)
                        dve.wait_ge(t.chain, c0 + 1)
                        if t.masked:
                            dve.tensor_scalar(rinv[:, bb, 0:H], rinv[:, bb, 0:H], fac[:, 0:1], None, ALU.mult)\
                                .then_inc(t.chain, 1)
                            dve.wait_ge(t.chain, c0 + 2)
                        if L == 1:
                            dve.scalar_tensor_tensor(out=xd(i, bb), in0=bank[4 + bb][0:S, 0:D],
                                                     scalar=rinv[:, bb, 0:1], in1=xd(i, bb),
                                                     op0=ALU.mult, op1=ALU.add).then_inc(t.norm, 1)
                            continue
                        halves = 2 if L == 2 else 1
                        hh = H // halves
                        for q in range(halves):
                            ob = 4 + q if L == 2 else 4 + bb
                            ins = dve.tensor_tensor(
                                on[:, q * hh * dh:(q + 1) * hh * dh].rearrange("p (h d) -> p h d", d=dh),
                                bank[ob][0:S, 0:hh * dh].rearrange("p (h d) -> p h d", d=dh),
                                rinv[:, bb, q * hh:(q + 1) * hh].unsqueeze(2).broadcast_to([S, hh, dh]),
                                ALU.mult)
                        ins.then_inc(t.norm, 1)

        def att_scalar(act, t):
            H = t.H
            act.sem_inc(t.probs, CREDIT)
            if t.a["bk"]:
                act.wait_ge(loaded[f"bias{t.L}"], 16 * (4 if t.L == 0 else 3))
            with act.Fori(0, B // 2) as i:
                for s in t.plan:
                    if s[0] == "gen":
                        _, kind, bb, o, h, n = s
                        if kind in ("q", "o") or (kind == "v" and t.a["bv"]):
                            continue
                        k = n % 2
                        src = bank[6 + k]
                        act.wait_ge(t.gen_ready, i * t.NG + n + 1 + 64)
                        if kind == "k":
                            if t.a["bk"]:
                                ins = act.activation(kTv(bb, t.NO)[:, o, :], src[:, 0:SK], ACT.Identity,
                                                     bias=biasA[:, 1, o:o + 1])
                            else:
                                ins = act.activation(kTv(bb, t.NO)[:, o, :], src[:, 0:SK], ACT.Copy)
                        elif kind == "v":
                            ins = act.activation(Vv(bb, t.W)[:, o, h * t.VW:(h + 1) * t.VW],
                                                 src[0:KT, 0:t.VW], ACT.Copy)
                        else:
                            m = min(4, t.NO)
                            ins = act.activation(oTv[:, o:o + m, :],
                                                 src[:, 0:m * S].rearrange("p (o t) -> p o t", t=S), ACT.Copy)
                        ins.then_inc(t.gen_free[k], 1)
                    elif s[0] == "scores":
                        g = s[1]
                        bb, h = g // H, g % H
                        at = i * (2 * H) + CREDIT
                        act.wait_ge(t.maxed, at + g + 1)
                        act.wait_ge(t.pt_psum, at + g - 1)
                        if h == 0:
                            act.wait_ge(t.norm, i * 2 + bb - 1 + CREDIT)
                        src = sm[:, g % 2, :] if t.masked else bank[g % 2][0:S, 0:SK]
                        act.activation(pr[:, g % 2, :], src, ACT.Exp, bias=mx[:, g % 2:g % 2 + 1], scale=-1.0,
                                       accum_out=sums[:, bb, h:h + 1]).then_inc(t.probs, 1)

        def ffn_sync(sp, f):
            L = f.L
            n_up = ND * f.F

            def load(slot, e):
                up, w2 = w_ffn(f, slot)
                src = [A[f"f{L}_in{u}"] for u in range(f.NU)]
                pick = (lambda a: a[e]) if isinstance(e, int) else \
                    (lambda a: a[bass.ds(e, 1)].rearrange("a p k n -> (a p) k n"))
                for u in range(f.NU):
                    sp.dma_start(up[u], pick(src[u])).then_inc(f.w_landed[slot], 16)
                sp.dma_start(w2, pick(A[f"f{L}_out"])).then_inc(f.w_landed[slot], 16)

            if f.loop:
                with sp.Fori(0, f.loop) as i:
                    for q in range(2):
                        sp.wait_ge(f.out, i * (2 * NCH) + (q - 1) * NCH + CREDIT)
                        load(q, i * 2 + q)
            if f.NE % 2:
                if f.loop:
                    sp.wait_ge(f.out, (f.NE - 2) * NCH + CREDIT)
                load(0, f.NE - 1)

        def ffn_tensor(pe, f):
            L, NF, NU = f.L, f.NF, f.NU
            for s in (f.hid, f.out, f.r_ps):
                pe.sem_inc(s, CREDIT)
            pe.sem_inc(f.used, NF * CREDIT)
            if L < 3:
                pe.wait_ge(loaded[f"r{L}"], 16 * (2 if L == 2 else 1))
                for b in range(B):
                    for c in range(ND):
                        m = pe.matmul(bank[7][0:S, b * E:(b + 1) * E], xnT[:, c, b * S:(b + 1) * S], wR[:, c, :],
                                      start=(c == 0), stop=(c == ND - 1))
                m.then_inc(f.r_ps, 1)
            if L == 0:
                with pe.Fori(0, B // 2) as i:
                    for bb in range(2):
                        pe.wait_ge(f.r_in, i * 2 + bb + CREDIT + 1)
                        pe.wait_ge(f.r_out, i * 2 + bb + CREDIT - 1)
                        for k in range(ND):
                            t = pe.transpose(bank[bb][:, k * S:(k + 1) * S], xn[:, bb, k * P:(k + 1) * P],
                                             ident[0:S, 0:S])
                        t.then_inc(f.r_ps, 1)
                pe.wait_ge(f.r_out, B + CREDIT)
            if L == 1:
                pe.wait_ge(f.r_dve, 1)
            if L == 2:
                for c in range(NCH):
                    pe.wait_ge(f.r_dve, f.n_gate)
                    for j in range(CHUNK):
                        b = c * CHUNK + j
                        t = pe.transpose(bank[c][0:E, j * S:(j + 1) * S], t8[5][:, b, :], ident[0:S, 0:S])
                    t.then_inc(f.r_ps, 1)
                pe.wait_ge(f.r_out, NCH)
                pe.wait_ge(loaded["b2"], 16)
                for b in range(B):
                    m = pe.matmul(bank[4 + b // 2 % 4][0:S, b % 2 * D:(b % 2 + 1) * D],
                                  gateT[:, b * S:(b + 1) * S], b2[:, :], start=True, stop=True)
                    if b % 2:
                        m.then_inc(f.r_ps, 1)
                        if b == 7:
                            pe.wait_ge(f.r_in, 8)
                pe.wait_ge(f.r_in, B)

            def experts(i, n_e, first):
                steps = [(q, c, t) for q in range(n_e) for c in range(NCH) for t in range(NF)]
                s0 = first + i * (2 * NCH * NF)
                q0 = (first // NF) + i * (2 * NCH)

                def hidden(s):
                    q, c, t = steps[s]
                    up, _ = w_ffn(f, q)
                    src = gxT if (L == 0 and not first) else xnT
                    o, w = f.tiles[t]
                    if c == 0 and t == 0:
                        trips = (f.loop if first else i)
                        pe.wait_ge(f.w_landed[q], trips * (16 * (NU + 1)) + 16 * (NU + 1))
                    for u in range(NU):
                        bk = (s * NU + u) % 4
                        lag = 4 // NU
                        pe.wait_ge(f.mid if u == NU - 1 else f.act, s0 + s - lag + 1 + CREDIT)
                        for k in range(ND):
                            m = pe.matmul(bank[bk][0:w, 0:TOK], up[u][:, k, o:o + w],
                                          src[:, k, c * TOK:(c + 1) * TOK], start=(k == 0), stop=(k == ND - 1))
                        m.then_inc(f.hid, 1)

                hidden(0)
                for s in range(len(steps)):
                    if s + 1 < len(steps):
                        hidden(s + 1)
                    q, c, t = steps[s]
                    _, w2 = w_ffn(f, q)
                    w = f.tiles[t][1]
                    if t == 0:
                        pe.wait_ge(f.added, q0 + (q * NCH + c) - 1 + CREDIT)
                    pe.wait_ge(f.mid, s0 + s + 1 + CREDIT)
                    for j in range(CHUNK):
                        bk = 4 + c % 2 * 2 + j // 2
                        m = pe.matmul(bank[bk][0:S, j % 2 * D:(j % 2 + 1) * D], mid[0:w, s % 2, j * S:(j + 1) * S],
                                      w2[0:w, t, :], start=(t == 0 and j % 2 == 0), stop=(t == NF - 1),
                                      skip_group_check=True)
                    if t == NF - 1:
                        m.then_inc(f.out, 1)
                    else:
                        m.then_inc(f.used, 1)

            if f.loop:
                with pe.Fori(0, f.loop) as i:
                    experts(i, 2, 0)
            if f.NE % 2:
                experts(0, 1, (f.NE - 1) * NCH * NF)

        def mid_free(eng, f, n, s0, q0, s):
            NF = f.NF
            if s < 2:
                pos = (s - 2) % NF
                chunks = (s - 2) // NF
            else:
                pos, chunks = (s - 2) % NF, (s - 2) // NF
            if pos == NF - 1:
                eng.wait_ge(f.out, q0 + chunks + 1 + CREDIT)
            else:
                eng.wait_ge(f.used, (q0 + chunks) * (NF - 1) + pos + 1 + NF * CREDIT)

        def ffn_scalar(act, f):
            L, NF, NU = f.L, f.NF, f.NU
            act.sem_inc(f.act, CREDIT)
            if L < 3:
                act.wait_ge(f.r_dve, f.n_act)
                if L == 0:
                    act.activation(t1[1][:, :], t1[0][:, :], ACT.Sigmoid).then_inc(f.r_act, 1)
                elif L == 1:
                    act.activation(t8[1][:, :, :], t8[0][:, :, :], ACT.Exp).then_inc(f.r_act, 1)
                else:
                    act.activation(t1[3][:, :], t1[2][:, :], ACT.Exp).then_inc(f.r_act, 1)
            if L == 0:
                act.sem_inc(f.r_out, CREDIT)
                with act.Fori(0, B // 2) as i:
                    for bb in range(2):
                        act.wait_ge(f.r_ps, i * 2 + bb + 2 + CREDIT)
                        settle(act)
                        act.activation(gxT[:, :, bass.ds((i * 2 + bb) * S, S)],
                                       bank[bb][:, 0:ND * S].rearrange("p (k t) -> p k t", k=ND),
                                       ACT.Copy).then_inc(f.r_out, 1)
            if L == 2:
                for c in range(NCH):
                    act.wait_ge(f.r_ps, c + 2 + CREDIT)
                    act.activation(gateT[:, c * TOK:(c + 1) * TOK], bank[c][0:E, 0:TOK], ACT.Copy)\
                        .then_inc(f.r_out, 1)
            if not f.gated:
                act.wait_ge(loaded[f"b1{L}"], 16)

            def experts(i, n_e, first):
                steps = [(q, c, t) for q in range(n_e) for c in range(NCH) for t in range(NF)]
                s0 = first + i * (2 * NCH * NF)
                q0 = (first // NF) + i * (2 * NCH)
                for s, (q, c, t) in enumerate(steps):
                    w = f.tiles[t][1]
                    if f.gated:
                        act.wait_ge(f.hid, (s0 + s) * 2 + 1 + CREDIT)
                        act.wait_ge(f.mid, s0 + s - 1 + CREDIT)
                        act.activation(hg[0:w, s % 2, :], bank[s * 2 % 4][0:w, 0:TOK], ACT.Silu)\
                            .then_inc(f.act, 1)
                    else:
                        act.wait_ge(f.hid, s0 + s + 1 + CREDIT)
                        mid_free(act, f, n_e, s0, q0, s)
                        settle(act)
                        col = q * NF + t + (32 if L == 3 else 0)
                        bias = b1[0:w, bass.ds(i * (2 * NF) + col, 1)] if f.loop else b1[0:w, col:col + 1]
                        act.activation(mid[0:w, s % 2, :], bank[s % 4][0:w, 0:TOK], ACT.Relu, bias=bias)\
                            .then_inc(f.mid, 1)

            if f.loop:
                with act.Fori(0, f.loop) as i:
                    experts(i, 2, 0)
            if f.NE % 2:
                experts(0, 1, (f.NE - 1) * NCH * NF)

        def router(dve, f):
            L = f.L
            count = [0]

            def link(ins):
                count[0] += 1
                ins.then_inc(f.r_dve, 1)
                dve.wait_ge(f.r_dve, count[0])

            over = lambda a: a[:, :].unsqueeze(2).broadcast_to([S, B, E])
            gv = gate[:, :].rearrange("p (e b) -> p b e", b=B)

            def pick(scores, top, first):
                link(dve.tensor_reduce(top[:, :], scores, AX_X, ALU.max))
                link(dve.tensor_tensor(t8[4][:, :, :], scores, over(top), ALU.is_equal))
                link(dve.memset(t8[3][:, :, 0:1], 0.0))
                for e in range(1, E):
                    link(dve.tensor_tensor(t8[3][:, :, e:e + 1], t8[3][:, :, e - 1:e], t8[4][:, :, e - 1:e],
                                           ALU.add))
                link(dve.scalar_tensor_tensor(out=first, in0=t8[3][:, :, :], scalar=0.0, in1=t8[4][:, :, :],
                                              op0=ALU.is_equal, op1=ALU.mult))

            dve.wait_ge(f.r_ps, 1 + CREDIT)
            logits = bank[7][0:S, 0:B * E].rearrange("p (b e) -> p b e", e=E)
            if L == 0:
                link(dve.tensor_copy(lg[:, :, :], logits))
                pick(lg[:, :, :], t1[0], t8[2][:, :, :])
                f.n_act = count[0]
                link(dve.tensor_copy(gv[:, :, 0:E], t8[2][:, :, :]))
                link(dve.memset(gate[:, E * B:], 1.0))
                dve.wait_ge(f.r_act, 1)
                dve.sem_inc(f.r_in, CREDIT)
                with dve.Fori(0, B // 2) as i:
                    for bb in range(2):
                        dve.wait_ge(f.r_ps, i * 2 + bb + CREDIT)
                        dve.tensor_scalar(xn[:, bb, :], xd(i, bb), rstd[:, bass.ds(i * 2 + bb, 1)],
                                          nmr[:, bass.ds(i * 2 + bb, 1)], ALU.mult, ALU.add).then_inc(f.r_dve, 1)
                        dve.wait_ge(f.r_dve, i * 2 + bb + 1 + count[0])
                        dve.tensor_scalar(xn[:, bb, :], xn[:, bb, :], t1[1][:, bass.ds(i * 2 + bb, 1)], None,
                                          ALU.mult).then_inc(f.r_in, 1)
                return
            if L == 1:
                link(dve.tensor_copy(lg[:, :, :], logits))
                link(dve.tensor_reduce(t1[0][:, :], lg[:, :, :], AX_X, ALU.max))
                link(dve.tensor_tensor(t8[0][:, :, :], lg[:, :, :], over(t1[0]), ALU.subtract))
                f.n_act = count[0]
                dve.wait_ge(f.r_act, 1)
                link(dve.tensor_reduce(t1[1][:, :], t8[1][:, :, :], AX_X, ALU.add))
                link(dve.reciprocal(t1[2][:, :], t1[1][:, :]))
                link(dve.tensor_tensor(lg[:, :, :], t8[1][:, :, :], over(t1[2]), ALU.mult))
            else:
                dve.wait_ge(loaded["r2"], 32)
                link(dve.tensor_tensor(lg[:, :, :], logits, brB[:, :].unsqueeze(1).broadcast_to([S, B, E]),
                                       ALU.add))
            pick(lg[:, :, :], t1[0], t8[2][:, :, :])
            link(dve.scalar_tensor_tensor(out=t8[0][:, :, :], in0=t8[2][:, :, :], scalar=-BIG, in1=lg[:, :, :],
                                          op0=ALU.mult, op1=ALU.add))
            pick(t8[0][:, :, :], t1[1], t8[5][:, :, :])
            if L == 1:
                link(dve.tensor_tensor(t8[5][:, :, :], t8[5][:, :, :], t8[2][:, :, :], ALU.add))
                link(dve.tensor_tensor(gv[:, :, 0:E], t8[5][:, :, :], lg[:, :, :], ALU.mult))
                link(dve.memset(gate[:, E * B:], 1.0))
                return
            link(dve.tensor_tensor(t1[2][:, :], t1[1][:, :], t1[0][:, :], ALU.subtract))
            f.n_act = count[0]
            dve.wait_ge(f.r_act, 1)
            link(dve.tensor_scalar(t1[4][:, :], t1[3][:, :], 1.0, None, ALU.add))
            link(dve.reciprocal(t1[4][:, :], t1[4][:, :]))
            link(dve.tensor_tensor(t1[5][:, :], t1[3][:, :], t1[4][:, :], ALU.mult))
            link(dve.tensor_tensor(t8[2][:, :, :], t8[2][:, :, :], over(t1[4]), ALU.mult))
            link(dve.tensor_tensor(t8[5][:, :, :], t8[5][:, :, :], over(t1[5]), ALU.mult))
            link(dve.tensor_tensor(t8[5][:, :, :], t8[5][:, :, :], t8[2][:, :, :], ALU.add))
            f.n_gate = count[0]
            link(dve.tensor_copy(gv[:, :, 0:E], t8[5][:, :, :]))
            for b in range(B):
                if b % 2 == 0:
                    dve.wait_ge(f.r_ps, 1 + NCH + b // 2 + 1 + CREDIT)
                dve.tensor_tensor(xb(b), bank[4 + b // 2 % 4][0:S, b % 2 * D:(b % 2 + 1) * D], xb(b), ALU.add)\
                    .then_inc(f.r_in, 1)
            dve.wait_ge(f.r_in, B)

        def ffn_vector(dve, f):
            L, NF, NU = f.L, f.NF, f.NU
            dve.sem_inc(f.added, CREDIT)
            if f.gated:
                dve.sem_inc(f.mid, CREDIT)
            if L < 3:
                router(dve, f)

            def experts(i, n_e, first):
                steps = [(q, c, t) for q in range(n_e) for c in range(NCH) for t in range(NF)]
                s0 = first + i * (2 * NCH * NF)
                q0 = (first // NF) + i * (2 * NCH)
                for s, (q, c, t) in enumerate(steps):
                    w = f.tiles[t][1]
                    if f.gated:
                        dve.wait_ge(f.hid, (s0 + s) * 2 + 2 + CREDIT)
                        dve.wait_ge(f.act, s0 + s + 1 + CREDIT)
                        mid_free(dve, f, n_e, s0, q0, s)
                        dve.tensor_tensor(mid[0:w, s % 2, :], bank[(s * 2 + 1) % 4][0:w, 0:TOK], hg[0:w, s % 2, :],
                                          ALU.mult).then_inc(f.mid, 1)
                    if t != NF - 1:
                        continue
                    cc = q * NCH + c
                    dve.wait_ge(f.out, q0 + cc + 1 + CREDIT)
                    dve.wait_ge(f.added, q0 + cc + CREDIT)
                    for j in range(CHUNK):
                        b = c * CHUNK + j
                        src = bank[4 + c % 2 * 2 + j // 2][0:S, j % 2 * D:(j % 2 + 1) * D]
                        if L == 3:
                            ins = dve.tensor_tensor(gx3(b), src, gx3(b), ALU.add)
                        else:
                            col = q * B + b
                            g = gate[:, bass.ds(i * (2 * B) + col, 1)] if not first else \
                                gate[:, (f.NE - 1) * B + b:(f.NE - 1) * B + b + 1]
                            ins = dve.scalar_tensor_tensor(out=xb(b), in0=src, scalar=g, in1=xb(b),
                                                           op0=ALU.mult, op1=ALU.add)
                    ins.then_inc(f.added, 1)

            if f.loop:
                with dve.Fori(0, f.loop) as i:
                    experts(i, 2, 0)
            if f.NE % 2:
                experts(0, 1, (f.NE - 1) * NCH * NF)

        yv = V[0:S, :, :].rearrange("p b n -> p (b n)")[:, 0:B * D]
        gx3 = lambda b: yv[:, b * D:(b + 1) * D]

        for f in ffn:
            f.used = sem(f"l{f.L}f_mid_used")

        ffn[0].n_act = 1 + 11
        ffn[1].n_act = 3
        ffn[2].n_act = 1 + 11 + 1 + 11 + 1
        ffn[2].n_gate = ffn[2].n_act + 6

        @block.sync
        def _(sp):
            sp.dma_start(x[:, :].rearrange("p (b d) -> p b d", d=D), A["x"]).then_inc(loaded["x"], 16)
            for k, n in enumerate(("q", "k", "v", "o")):
                sp.dma_start(w_att(0, k), A[f"a0_w{n}"]).then_inc(loaded["w0"], 16)
            sp.dma_start(maski[:, :], A["mask0"]).then_inc(loaded["mask"], 16)
            sp.dma_start(maskb[:, :], A["mask3"].bitcast(U8).rearrange("(s k) -> s k", k=SK)).then_inc(loaded["mask"], 16)
            sp.dma_start(biasA[:, 0, :], A["a0_bq"]).then_inc(loaded["bias0"], 16)
            sp.dma_start(biasA[:, 1, :], A["a0_bk"]).then_inc(loaded["bias0"], 16)
            sp.dma_start(bvB[:, :], A["a0_bv"]).then_inc(loaded["bias0"], 16)
            sp.dma_start(boB[:, :], A["a0_bo"]).then_inc(loaded["bias0"], 16)
            sp.dma_start(wR[:, :, :], A["f0_r"]).then_inc(loaded["r0"], 16)
            for k, n in enumerate(("q", "k", "v", "o")):
                sp.dma_start(w_att(2, k), A[f"a2_w{n}"]).then_inc(loaded["w2"], 16)
            att_sync(sp, att[0])
            ffn_sync(sp, ffn[0])
            sp.wait_ge(stage_done, 3 * 2)
            for k, n in enumerate(("q", "k", "v")):
                sp.dma_start(w_att(1, k), A[f"a1_w{n}"]).then_inc(loaded["w1"], 16)
            sp.dma_start(biasA[:, 0, :], A["a1_bq"]).then_inc(loaded["bias1"], 16)
            sp.dma_start(biasA[:, 1, :], A["a1_bk"]).then_inc(loaded["bias1"], 16)
            sp.dma_start(bvB[:, :], A["a1_bv"]).then_inc(loaded["bias1"], 16)
            sp.dma_start(boB[:, :], A["a2_bo"]).then_inc(loaded["bo2"], 16)
            sp.wait_ge(stage_done, 3 * 4)
            sp.dma_start(wR[:, :, :], A["f1_r"]).then_inc(loaded["r1"], 16)
            att_sync(sp, att[1])
            sp.wait_ge(stage_done, 3 * 6)
            for k, n in enumerate(("q", "k", "v", "o")):
                sp.dma_start(w_att(3, k), A[f"a3_w{n}"]).then_inc(loaded["w3"], 16)
            ffn_sync(sp, ffn[1])
            sp.wait_ge(stage_done, 3 * 8)
            sp.dma_start(wR[:, :, :], A["f2_r"]).then_inc(loaded["r2"], 16)
            sp.dma_start(brB[:, :], A["f2_br"]).then_inc(loaded["r2"], 16)
            sp.dma_start(b1[:, 0:32], A["f2_b1"]).then_inc(loaded["b12"], 16)
            sp.dma_start(b2[:, :], A["f2_b2"]).then_inc(loaded["b2"], 16)
            att_sync(sp, att[2])
            sp.wait_ge(stage_done, 3 * 10)
            sp.dma_start(boB[:, :], A["f3_b2"]).then_inc(loaded["b23"], 16)
            ffn_sync(sp, ffn[2])
            sp.wait_ge(stage_done, 3 * 12)
            sp.dma_start(b1[:, 32:40], A["f3_b1"]).then_inc(loaded["b13"], 16)
            att_sync(sp, att[3])
            ffn_sync(sp, ffn[3])
            sp.wait_ge(stage_done, 3 * 14)
            sp.dma_start(gB[:, 0, :], A["f3_gamma"]).then_inc(loaded["gb"], 16)
            sp.dma_start(gB[:, 1, :], A["f3_beta"]).then_inc(loaded["gb"], 16)
            sp.wait_ge(fin, B + 1 + 4 * B)
            sp.dma_start(A["out"], x[:, :].rearrange("p (b d) -> p b d", d=D)).then_inc(stored, 16)
            sp.wait_ge(stored, 16)

        @block.gpsimd
        def _(pool):
            nc.gpsimd.memset(ident[:, :], 0.0).then_inc(consts, 1)
            nc.gpsimd.memset(epsc[:, :], EPS).then_inc(consts, 1)
            nc.gpsimd.memset(sel[16][:, :], -ATT[0]["scale"]).then_inc(consts, 1)
            nc.gpsimd.memset(sel[64][:, :], -ATT[2]["scale"]).then_inc(consts, 1)
            pool.wait_ge(consts, 4)
            nc.gpsimd.affine_select(out=ident[:, :], in_=ident[:, :], compare_op=ALU.not_equal, fill=1.0,
                                    base=0, pattern=[[-1, P]], channel_multiplier=1).then_inc(consts, 1)
            for dh, n in ((16, 8), (64, 2)):
                nc.gpsimd.affine_select(out=sel[dh][:, :], in_=sel[dh][:, :], compare_op=ALU.is_ge, fill=0.0,
                                        base=0, pattern=[[-dh, n]], channel_multiplier=1).then_inc(consts, 1)
            pool.wait_ge(consts, 7)
            for dh, n in ((16, 8), (64, 2)):
                nc.gpsimd.affine_select(out=sel[dh][:, :], in_=sel[dh][:, :], compare_op=ALU.is_ge, fill=0.0,
                                        base=dh - 1, pattern=[[dh, n]], channel_multiplier=-1)\
                    .then_inc(consts, 1)

        @block.tensor
        def _(pe):
            pe.wait_ge(consts, 9)
            pe.sem_inc(ln.ps, CREDIT)
            for L in range(4):
                for t in (att[L], ffn[L]):
                    n = 4 * L + (0 if t is att[L] else 2)
                    ln_tensor(pe, n // 2)
                    finish(pe, n)
                    (att_tensor if t is att[L] else ffn_tensor)(pe, t)
                    finish(pe, n + 1)

        @block.scalar
        def _(act):
            act.wait_ge(consts, 9)
            act.sem_inc(ln.xT, CREDIT)
            for L in range(4):
                for t in (att[L], ffn[L]):
                    n = 4 * L + (0 if t is att[L] else 2)
                    ln_scalar(act, n // 2)
                    finish(act, n)
                    (att_scalar if t is att[L] else ffn_scalar)(act, t)
                    finish(act, n + 1)
            ln_std(act, 8)

        @block.vector
        def _(dve):
            dve.wait_ge(consts, 9)
            dve.sem_inc(ln.xn, CREDIT)
            dve.wait_ge(loaded["x"], 16)
            for L in range(4):
                for t in (att[L], ffn[L]):
                    n = 4 * L + (0 if t is att[L] else 2)
                    ln_vector(dve, n // 2)
                    finish(dve, n)
                    if t is ffn[3]:
                        dve.wait_ge(loaded["b23"], 16)
                        for b in range(B):
                            dve.tensor_scalar(gx3(b), xb(b), rstd[:, b:b + 1], nmr[:, b:b + 1],
                                              ALU.mult, ALU.add).then_inc(fin, 1)
                        dve.wait_ge(fin, B)
                        dve.tensor_tensor(yv.rearrange("p (b d) -> p b d", d=D),
                                          yv.rearrange("p (b d) -> p b d", d=D),
                                          boB[0:S, :].unsqueeze(1).broadcast_to([S, B, D]), ALU.add)\
                            .then_inc(fin, 1)
                        dve.wait_ge(fin, B + 1)
                    (att_vector if t is att[L] else ffn_vector)(dve, t)
                    finish(dve, n + 1)
            ln_stats(dve, 8, gx3)
            dve.wait_ge(loaded["gb"], 32)
            done = B + 1
            for b in range(B):
                for ins in range(4):
                    y = gx3(b)
                    if ins == 0:
                        w = dve.tensor_scalar(y, y, rstd[:, b:b + 1], nmr[:, b:b + 1], ALU.mult, ALU.add)
                    elif ins == 1:
                        w = dve.tensor_tensor(y, y, gB[:, 0, :], ALU.mult)
                    elif ins == 2:
                        w = dve.tensor_tensor(y, y, gB[:, 1, :], ALU.add)
                    else:
                        w = dve.tensor_tensor(xb(b), xb(b), y, ALU.add)
                    w.then_inc(fin, 1)
                    done += 1
                    if ins < 3:
                        dve.wait_ge(fin, done)


def layout(inp):
    A = {}
    rows = lambda w: np.ascontiguousarray(w.reshape(-1, P, w.shape[-1]).transpose(1, 0, 2))
    cols = lambda v: np.ascontiguousarray(v.reshape(-1, P).T)
    every = lambda v, n: np.ascontiguousarray(np.broadcast_to(v, (n, v.shape[-1])))
    A["x"] = inp["x"].transpose(1, 0, 2)
    A["ctxT"] = inp["ctx_1024"].transpose(0, 2, 1).reshape(B, ND, P, SK).transpose(0, 2, 1, 3)
    A["mask0"] = inp["mask_1x1xSxS2_ik0"].reshape(S, SK)
    A["mask3"] = inp["mask_SxS2_bk0"].reshape(-1).view(np.int32)
    for n in "qkvo":
        A[f"a0_w{n}"] = rows(inp[f"L0_xattn_W_{n}"].T)
        A[f"a2_w{n}"] = rows(inp[f"L2_xattn_W{n}"].T)
        A[f"a3_w{n}"] = rows(inp[f"L3_xattn_W{n}"].T)
        if n != "o":
            A[f"a1_w{n}"] = rows(inp[f"L1_xattn_W{n}"])
    for L, u in ((0, "_"), (1, "")):
        A[f"a{L}_bq"] = cols(inp[f"L{L}_xattn_b{u}q"])
        A[f"a{L}_bk"] = cols(inp[f"L{L}_xattn_b{u}k"])
        A[f"a{L}_bv"] = every(inp[f"L{L}_xattn_b{u}v"], P)
    A["a0_bo"] = every(inp["L0_xattn_b_o"], P)
    A["a2_bo"] = every(inp["L2_xattn_bo"], P)
    A["f3_b2"] = every(inp["L3_ffn_b2"][0], P)

    def experts(w):
        e, r, n = w.shape
        t = -(-r // P)
        w = np.concatenate([w, np.zeros((e, t * P - r, n), w.dtype)], 1)
        return w.reshape(e, t, P, n).transpose(0, 2, 1, 3)

    A["f0_r"] = rows(inp["L0_ffn_router_DE"])
    A["f0_in0"] = experts(np.concatenate([inp["L0_ffn_w1_eDF"], inp["L0_ffn_ws1_DF"][None]]))
    A["f0_in1"] = experts(np.concatenate([inp["L0_ffn_w3_eDF"], inp["L0_ffn_ws3_DF"][None]]))
    A["f0_out"] = experts(np.concatenate([inp["L0_ffn_w2_eFD"], inp["L0_ffn_ws2_FD"][None]]))
    F = FFN[1]["F"]
    w1, w2, s1, s2 = (inp[f"L1_ffn_{n}"] for n in ("W1", "W2", "Ws1", "Ws2"))
    A["f1_r"] = rows(inp["L1_ffn_gate_w"].T)
    gate = np.concatenate([w1[:, F:], s1[2 * F:].reshape(2, F, D)])
    value = np.concatenate([w1[:, :F], s1[:2 * F].reshape(2, F, D)])
    out = np.concatenate([w2, s2.reshape(D, 2, F).transpose(1, 0, 2)])
    A["f1_in0"] = experts(gate.transpose(0, 2, 1))
    A["f1_in1"] = experts(value.transpose(0, 2, 1))
    A["f1_out"] = experts(out.transpose(0, 2, 1))
    A["f2_r"] = rows(inp["L2_ffn_Wr"])
    A["f2_br"] = every(inp["L2_ffn_br"], S)
    A["f2_in0"] = experts(inp["L2_ffn_W1"])
    A["f2_out"] = experts(inp["L2_ffn_W2"])
    A["f2_b1"] = cols(inp["L2_ffn_b1"].reshape(-1))
    A["f2_b2"] = inp["L2_ffn_b2"]
    A["f3_in0"] = experts(inp["L3_ffn_w1"][0:1])
    A["f3_out"] = experts(inp["L3_ffn_w2"][0:1])
    A["f3_b1"] = cols(inp["L3_ffn_b1"][0])
    A["f3_gamma"] = every(inp["L3_ffn_gamma"], S)
    A["f3_beta"] = every(inp["L3_ffn_beta"], S)
    return {k: np.ascontiguousarray(v) for k, v in A.items()}


def kernel(**inputs):
    import concourse.bacc as _bacc
    from concourse.bass_utils import run_bass_kernel_spmd as _run

    nc = _bacc.Bacc("TRN2", target_bir_lowering=False, num_devices=1)
    arrays = {f"in_{k}": v for k, v in layout({k: np.asarray(v) for k, v in inputs.items()}).items()}
    aps = {k[3:]: nc.dram_tensor(k, v.shape, mybir.dt.from_np(v.dtype), kind="ExternalInput").ap()
           for k, v in arrays.items()}
    aps["out"] = nc.dram_tensor("out_0", (B, S, D), F32, kind="ExternalOutput").ap().rearrange("b s d -> s b d")
    build(nc, aps)
    r = _run(nc, [arrays], core_ids=[0])
    return r.results[0]["out_0"]
```

```python
from contextlib import ExitStack

import concourse.bass as bass
import numpy as np
from concourse import mybir

F32 = mybir.dt.float32
I32 = mybir.dt.int32
U8 = mybir.dt.uint8
U32 = mybir.dt.uint32
ALU = mybir.AluOpType
ACT = mybir.ActivationFunctionType
AX_X = mybir.AxisListType.X

P = 128
B = 16
S = 112
SK = 375
KT = 125
NKT = SK // KT
D = 256
ND = D // P
E = 8
CHUNK = 4
NCH = B // CHUNK
TOK = CHUNK * S
CREDIT = 8
GENS = 64
EPS = 1e-5
BIG = 1e30

ATT = {
    0: dict(H=16, dh=16, scale=0.25, fill=1e30, bq=True, bk=True, bv=True, wo=True, bo=True),
    1: dict(H=1, dh=256, scale=1 / 16, fill=None, bq=True, bk=True, bv=True, wo=False, bo=False),
    2: dict(H=16, dh=64, scale=0.125, fill=None, bq=False, bk=False, bv=False, wo=True, bo=True),
    3: dict(H=16, dh=16, scale=0.25, fill=1e9, bq=False, bk=False, bv=False, wo=True, bo=False),
}
FFN = {
    0: dict(F=704, shared=1, K=1, gated=True),
    1: dict(F=192, shared=2, K=2, gated=True),
    2: dict(F=512, shared=0, K=2, gated=False),
    3: dict(F=1024, shared=1, K=0, gated=False),
}
ROWS = 2 * P
BLOCKS = [-(-(B * S * f["K"] // ROWS + E - 1) // 2) * 2 for f in FFN.values()]
MAXB = -(-B * S // ROWS)


def ftiles(F):
    return [(o, min(P, F - o)) for o in range(0, F, P)]


class Att:

    def __init__(self, L, sems, before):
        a = ATT[L]
        self.L, self.H, self.dh = L, a["H"], a["dh"]
        self.a = a
        self.W = self.H * self.dh
        self.NO = self.W // P
        self.per = max(1, P // self.dh)
        self.KH = max(1, self.dh // P)
        self.VH = max(1, self.W // 512)
        self.VW = self.W // self.VH
        self.masked = a["fill"] is not None
        self.plan = self.steps()
        self.gens = [s for s in self.plan if s[0] == "gen"]
        self.NG = len(self.gens)
        assert self.NG % 2 == 0
        self.gen_ready = sems["gen_ready"]
        self.scores = sems["scores"]
        self.maxed = sems["maxed"]
        self.probs = sems["probs"]
        self.pt_psum = sems["pt_psum"]
        self.pt_sbuf = sems["pt_sbuf"]
        self.pv = sems["pv"]
        self.norm = sems["norm"]
        self.chain = sems["chain"]
        self.ctx_landed = sems["ctx_landed"]
        self.gen_free = sems["gen_free"]
        self.h0 = before.h0 + B * before.H if before else CREDIT
        self.b0 = before.b0 + B // 2 * before.NG // 2 if before else CREDIT
        self.g0 = before.g0 + B // 2 * before.NG if before else GENS
        self.n0 = before.n0 + B if before else CREDIT
        self.c0 = before.c0 + 16 * B // 2 if before else 0
        self.prep = (5 if L == 0 else 6 if L == 3 else 0) + (1 if a["bo"] else 0)
        self.NC = 2 if self.masked else 1
        self.ch0 = before.ch0 + before.prep + B * before.NC if before else 0

    def steps(self):
        H = self.H
        proj = lambda bb: ([("gen", "q", bb, o, 0) for o in range(self.NO)]
                           + [("gen", "k", bb, o, 0) for o in range(self.NO)]
                           + [("gen", "v", bb, kt, h) for kt in range(NKT) for h in range(self.VH)])
        late = lambda bb: ([("gen", "t", bb, o, 0) for o in range(0, self.NO, 4)] + [("gen", "o", bb, 0, 0)]
                           if self.a["wo"] else [])
        plan = proj(0)
        nxt, done = proj(1), []
        for g in range(2 * H + 3):
            if g == H:
                plan += nxt
                nxt = []
            if g < 2 * H:
                plan.append(("scores", g))
            if 2 <= g < 2 * H + 2:
                plan.append(("turn", g - 2))
            if g >= 3:
                plan.append(("pv", g - 3))
                if (g - 3) % H == H - 1:
                    bb = (g - 3) // H
                    plan.append(("norm", bb))
                    done = late(bb)
            if 2 <= g < H and nxt:
                k = -(-len(nxt) // max(1, H - g - 1))
                plan += nxt[:k]
                nxt = nxt[k:]
            if done and ((g - 3) % H == 2 or g == 2 * H + 2):
                plan += done
                done = []
        out, n = [], 0
        for s in plan + done:
            if s[0] == "gen":
                s = s + (n,)
                n += 1
            out.append(s)
        return out

    def gen_index(self, kind, bb, o=0, h=0):
        return next(s[5] for s in self.gens if s[1:5] == (kind, bb, o, h))


class Ffn:

    def __init__(self, L, sem):
        f = FFN[L]
        self.L, self.gated, self.F = L, f["gated"], f["F"]
        self.NS, self.K, self.NB = f["shared"], f["K"], BLOCKS[L]
        self.tiles = ftiles(f["F"])
        self.NF = len(self.tiles)
        self.NU = 2 if self.gated else 1
        self.at_b1 = self.NU * ND * self.F
        self.at_out = self.at_b1 + (0 if self.gated else self.NF)
        self.at_b2 = self.at_out + self.NF * D
        self.size = self.at_b2 + (0 if self.gated else D)
        self.groups = [self.tiles[q:q + 2] for q in range(0, self.NF, 2)]
        self.G = len(self.groups)
        n = lambda s: sem(f"l{L}f_{s}")
        if self.NS:
            self.w_landed = n("shared_weights_landed")
            self.hid = n("shared_hidden_ready")
            self.mid = n("shared_mid_ready")
            self.act = n("shared_act_done") if self.gated else self.mid
            self.out = n("shared_out_ready")
            self.used = n("shared_mid_used")
            self.added = n("shared_out_added")
        if self.K:
            self.r_ps = n("router_psum")
            self.r_chain = n("router_chain")
            self.r_go = n("router_to_scalar")
            self.r_act = n("router_act")
            self.r_mask = n("router_choice")
            self.r_slots = n("router_slots")
            self.r_x = n("router_tokens")
            self.sorted = n("tokens_sorted")
            self.bw = [n(f"block_input_weights_landed{k}") for k in range(2)]
            self.bo = [n(f"block_output_weights_landed{k}") for k in range(2)]
            self.bx = [n(f"block_tokens_landed{k}") for k in range(2)]
            self.xT_ps = n("block_xT_psum")
            self.xT_sb = n("block_xT_sbuf")
            self.bhid = n("block_hidden_ready")
            self.bmid = n("block_mid_ready")
            self.bact = n("block_act_done") if self.gated else self.bmid
            self.bout = n("block_out_ready")
            self.yb = n("block_out_sbuf")
            self.y_store = [n(f"block_out_stored{k}") for k in range(2)]
            self.back = n("results_back")


class Ln:

    def __init__(self, sem):
        self.dve = sem("ln_dve")
        self.act = sem("ln_std")
        self.xn = sem("ln_xn")
        self.ps = sem("ln_psum")
        self.xT = sem("ln_xT")

    def at(self, k):
        return k * (2 * B + 2), k * B + CREDIT


def build(nc, A):
    ctx = ExitStack()
    with ctx:
        sb = lambda name, shape, dt=F32: ctx.enter_context(nc.sbuf_tensor(name, shape, dt))
        sem = lambda name: ctx.enter_context(nc.semaphore(name))
        bank = [ctx.enter_context(nc.psum_tensor(f"bank{k}", [P, 512], F32)) for k in range(8)]

        x = sb("x", [S, B * D])
        xnT = sb("xnT", [P, ND, B * S])
        ident = sb("ident", [P, P])
        sel = {16: sb("sel16", [P, 8]), 64: sb("sel64", [P, 2])}
        stats = sb("stats", [S, B, 6])
        mv = sb("mv", [S, B, 2])
        std = sb("std", [S, B])
        rstd = sb("rstd", [S, B])
        nmr = sb("nmr", [S, B])
        xn = sb("xn", [S, 2, D])
        epsc = sb("epsc", [P, 1])

        ctxT = sb("ctxT", [P, 2, ND, SK])
        kT = sb("kT", [P, 2, 8 * SK])
        V = sb("V", [KT, 2, NKT * 1024])
        qm = sb("qm", [P, 2, 16 * S])
        sm = sb("sm", [S, 2, SK])
        pr = sb("pr", [S, 2, SK])
        pT = sb("pT", [KT, 2, NKT * S])
        on = sb("on", [S, 1024])
        oT = sb("oT", [P, 8 * S])
        mx = sb("mx", [S, 2])
        sums = sb("sums", [S, 2, 16])
        rinv = sb("rinv", [S, 2, 16])
        maskf = sb("maskf", [S, SK])
        maski = sb("maski", [S, SK], I32)
        maskb = sb("maskb", [S, SK], U8)
        flag = sb("flag", [S, 2])
        fac = sb("fac", [S, 1])
        wA = sb("wA", [P, 4, ND * D])
        w2A = sb("w2A", [P, 4, 2048])
        biasA = sb("biasA", [P, 3, ND])
        bvB = sb("bvB", [P, D])
        boB = sb("boB", [P, D])

        wF = sb("wF", [P, 2, max(f["F"] * (ND * (1 + f["gated"]) + 2) for f in FFN.values()) + 264])
        hg = sb("hg", [P, 2, 512])
        mid = sb("mid", [P, 2, TOK])
        wR = sb("wR", [P, ND, E])
        brB = sb("brB", [S, E])
        t1 = [sb(f"t1_{k}", [S, B]) for k in range(8)]
        rowid = sb("rowid", [S, 2, B], U32)
        ebi = sb("ebi", [S, max(BLOCKS)], I32)
        tri = sb("tri", [S, S])
        ones = sb("ones", [S, S])
        ramp = sb("ramp", [S, max(BLOCKS)])
        rampi = sb("rampi", [S, max(BLOCKS)], I32)
        zero = mid[:, 0, 0:D]
        cflat = ctxT[:, :, :, :].rearrange("p b k t -> p (b k t)")
        xblk = cflat[:, 0:4 * D].rearrange("p (b s d) -> p b s d", b=2, s=2)
        tab = qm[0:S, :, :].rearrange("p b t -> p (b t)")
        tables = [tab[:, k * B * E:(k + 1) * B * E] for k in range(28)]
        kflat = kT[:, :, :].rearrange("p b n -> p (b n)")
        vflat = V[:, :, :].rearrange("p b n -> p (b n)")
        MIDW = 2 * max(len(ftiles(f["F"])) for f in FFN.values() if f["K"]) * P
        midr = kflat[:, 0:2 * MIDW].rearrange("p (b n) -> p b n", b=2)
        xTb = kflat[:, 2 * MIDW:2 * MIDW + 4 * P * ND].rearrange("p (b k t) -> p b k t", b=2, k=ND)
        yblk = kflat[:, 2 * MIDW + 4 * P * ND:2 * MIDW + 4 * P * ND + 4 * D]            .rearrange("p (b s d) -> p b s d", b=2, s=2)
        back = [kflat[0:S, 0:B * D], vflat[0:S, 0:B * D]]
        xna = vflat[0:S, 0:B * D]
        gB = on[:, 0:2 * D].rearrange("p (k d) -> p k d", d=D)

        consts = sem("constants_ready")
        loaded = {k: sem(f"loaded_{k}") for k in ["x", "w0", "w1", "w2", "w3", "mask", "bias0", "bias1", "bo2",
                                                  "r0", "r1", "r2", "gb"]}
        stage_done = sem("stage_done")
        stored = sem("stored")
        settled = sem("settled")
        names = dict(
            gen_ready="product_ready",
            scores="scores_ready",
            maxed="max_ready",
            probs="probs_ready",
            pt_psum="probsT_in_psum",
            pt_sbuf="probsT_in_sbuf",
            pv="pv_ready",
            norm="heads_normalised",
            chain="attention_chain",
        )
        att_sems = {k: sem(v) for k, v in names.items()}
        att_sems["ctx_landed"] = [sem(f"ctx_landed{k}") for k in range(2)]
        att_sems["gen_free"] = [sem(f"product_evacuated{k}") for k in range(2)]
        att = []
        for L in range(4):
            att.append(Att(L, att_sems, att[-1] if att else None))
        ffn = [Ffn(L, sem) for L in range(4)]
        ln = Ln(sem)
        fin = sem("final_chain")

        kTv = lambda p, NO: kT[:, p, 0:NO * SK].rearrange("p (o t) -> p o t", t=SK)
        Vv = lambda p, W: V[:, p, 0:NKT * W].rearrange("p (k w) -> p k w", w=W)
        qmv = qm[:, :, :].rearrange("p b (h t) -> p b h t", t=S)
        prv = pr
        pTv = pT[:, :, :].rearrange("p b (k t) -> p b k t", t=S)
        oTv = oT[:, :].rearrange("p (o t) -> p o t", t=S)
        xb = lambda b: x[:, b * D:(b + 1) * D]
        xd = lambda i, bb: x[:, bass.ds(i * (2 * D) + bb * D, D)]

        def w_att(L, k):
            if L == 2:
                return w2A[:, k, :].rearrange("p (k n) -> p k n", k=ND if k < 3 else 8)
            return wA[:, k, :].rearrange("p (k n) -> p k n", k=ND)

        def w_ffn(f, slot, off=0):
            n = ND * f.F
            up = [wF[:, slot, off + u * n:off + (u + 1) * n].rearrange("p (k f) -> p k f", k=ND)
                  for u in range(f.NU)]
            w2 = wF[:, slot, off + f.at_out:off + f.at_b2]
            return up, w2.rearrange("p (t n) -> p t n", n=D)

        xs = nc.dram_tensor("sorted_tokens", (max(BLOCKS) * ROWS, D), F32).ap()
        ys = nc.dram_tensor("sorted_results", (max(BLOCKS) * ROWS, D), F32).ap()
        cleared = sem("sorted_tokens_cleared")

        block = ctx.enter_context(nc.Block())

        def finish(eng, n):
            eng.drain().then_inc(stage_done, 1)
            eng.wait_ge(stage_done, 3 * (n + 1))

        def settle(eng):
            eng.sem_inc(settled, 1)

        def ln_stats(dve, k, of):
            at, _ = ln.at(k)
            for b in range(B):
                dve.bn_stats(stats[:, b, :], of(b)).then_inc(ln.dve, 1)
            for b in range(B):
                dve.wait_ge(ln.dve, at + b + 1)
                dve.bn_aggr(mv[:, b, :], stats[:, b, :]).then_inc(ln.dve, 1)
            dve.wait_ge(ln.act, k + 1)
            dve.reciprocal(rstd[:, :], std[:, :]).then_inc(ln.dve, 1)
            dve.wait_ge(ln.dve, at + 2 * B + 1)
            dve.scalar_tensor_tensor(out=nmr[:, :], in0=mv[:, :, 0], scalar=-1.0, in1=rstd[:, :],
                                     op0=ALU.mult, op1=ALU.mult).then_inc(ln.dve, 1)
            dve.wait_ge(ln.dve, at + 2 * B + 2)

        def ln_std(act, k):
            act.wait_ge(ln.dve, ln.at(k)[0] + 2 * B)
            act.activation(std[:, :], mv[:, :, 1], ACT.Sqrt, bias=epsc[0:S, :]).then_inc(ln.act, 1)

        def ln_vector(dve, k):
            ln_stats(dve, k, xb)
            _, at = ln.at(k)
            with dve.Fori(0, B // 2) as i:
                for bb in range(2):
                    dve.wait_ge(ln.ps, i * 2 + bb + at - 1)
                    dve.tensor_scalar(xn[:, bb, :], xd(i, bb), rstd[:, bass.ds(i * 2 + bb, 1)],
                                      nmr[:, bass.ds(i * 2 + bb, 1)], ALU.mult, ALU.add).then_inc(ln.xn, 1)

        def ln_scalar(act, k):
            ln_std(act, k)
            _, at = ln.at(k)
            with act.Fori(0, B // 2) as i:
                for bb in range(2):
                    act.wait_ge(ln.ps, i * 2 + bb + at + 1)
                    settle(act)
                    act.activation(xnT[:, :, bass.ds((i * 2 + bb) * S, S)],
                                   bank[bb][:, 0:ND * S].rearrange("p (k t) -> p k t", k=ND),
                                   ACT.Copy).then_inc(ln.xT, 1)

        def ln_tensor(pe, k):
            _, at = ln.at(k)
            with pe.Fori(0, B // 2) as i:
                for bb in range(2):
                    pe.wait_ge(ln.xn, i * 2 + bb + at + 1)
                    pe.wait_ge(ln.xT, i * 2 + bb + at - 1)
                    for c in range(ND):
                        t = pe.transpose(bank[bb][:, c * S:(c + 1) * S], xn[:, bb, c * P:(c + 1) * P],
                                         ident[0:S, 0:S])
                    t.then_inc(ln.ps, 1)

        def att_sync(sp, t):
            with sp.Fori(0, B // 2) as i:
                for bb in range(2):
                    last = t.gen_index("v", bb, NKT - 1, t.VH - 1)
                    sp.wait_ge(t.gen_ready, i * t.NG + last + 1 - t.NG + t.g0)
                    sp.dma_start(ctxT[:, bb, :, :],
                                 A["ctxT"][bass.ds(i * 2 + bb, 1), :, :, :].rearrange("a p k t -> (a p) k t"))\
                        .then_inc(t.ctx_landed[bb], 16)

        def att_tensor(pe, t):
            L, H, dh, per = t.L, t.H, t.dh, t.per
            w = [w_att(L, k) for k in range(4)]
            pe.wait_ge(loaded[f"w{L}"], 16 * (4 if t.a["wo"] else 3))
            with pe.Fori(0, B // 2) as i:
                def gen(kind, bb, o, h, n):
                    k = n % 2
                    dst = bank[6 + k]
                    pe.wait_ge(t.gen_free[k], i * (t.NG // 2) + n // 2 + t.b0)
                    if kind == "q":
                        for c in range(ND):
                            m = pe.matmul(dst[:, 0:S], w[0][:, c, o * P:(o + 1) * P],
                                          xnT[:, c, bass.ds((i * 2 + bb) * S, S)],
                                          start=(c == 0), stop=(c == ND - 1))
                    elif kind == "k":
                        if o == 0:
                            pe.wait_ge(t.ctx_landed[bb], i * 16 + 16 + t.c0)
                        for c in range(ND):
                            m = pe.matmul(dst[:, 0:SK], w[1][:, c, o * P:(o + 1) * P], ctxT[:, bb, c, :],
                                          start=(c == 0), stop=(c == ND - 1))
                    elif kind == "v":
                        for c in range(ND):
                            m = pe.matmul(dst[0:KT, 0:t.VW], ctxT[:, bb, c, o * KT:(o + 1) * KT],
                                          w[2][:, c, h * t.VW:(h + 1) * t.VW],
                                          start=(c == 0), stop=(c == ND - 1))
                    elif kind == "t":
                        if o == 0:
                            pe.wait_ge(t.norm, i * 2 + bb + 1 + t.n0)
                        for j in range(min(4, t.NO)):
                            m = pe.transpose(dst[:, j * S:(j + 1) * S], on[:, (o + j) * P:(o + j + 1) * P],
                                             ident[0:S, 0:S])
                    else:
                        last = t.gen_index("t", bb, (t.NO - 1) // 4 * 4)
                        pe.wait_ge(t.gen_free[last % 2], i * (t.NG // 2) + last // 2 + 1 + t.b0)
                        for j in range(t.NO):
                            m = pe.matmul(dst[0:S, 0:D], oTv[:, j, :], w[3][:, j, :],
                                          start=(j == 0), stop=(j == t.NO - 1))
                    m.then_inc(t.gen_ready, 1)

                for s in t.plan:
                    if s[0] == "gen":
                        gen(*s[1:])
                        continue
                    g = s[1]
                    if s[0] == "norm":
                        continue
                    bb, h = g // H, g % H
                    at = i * (2 * H) + t.h0
                    if s[0] == "scores":
                        if h == 0:
                            for o in range(t.NO - 2, t.NO):
                                n = t.gen_index("k", bb, o)
                                pe.wait_ge(t.gen_free[n % 2], i * (t.NG // 2) + n // 2 + 1 + t.b0)
                        pe.wait_ge(t.maxed if t.masked else t.probs, at + g - 1)
                        for c in range(t.KH):
                            m = pe.matmul(bank[g % 2][0:S, 0:SK], qmv[:, bb, h * t.KH + c, :],
                                          kTv(bb, t.NO)[:, h // per * t.KH + c, :],
                                          start=(c == 0), stop=(c == t.KH - 1))
                        m.then_inc(t.scores, 1)
                    elif s[0] == "turn":
                        pe.wait_ge(t.probs, at + g + 1)
                        pe.wait_ge(t.pt_sbuf, at + g - 1)
                        for k in range(NKT):
                            m = pe.transpose(bank[2 + g % 2][0:KT, k * S:(k + 1) * S],
                                             prv[:, g % 2, k * KT:(k + 1) * KT], ident[0:S, 0:S])
                        m.then_inc(t.pt_psum, 1)
                    else:
                        pe.wait_ge(t.pt_sbuf, at + g + 1)
                        if h == 0:
                            for n in range(2):
                                o, hh = divmod(NKT * t.VH - 1 - n, t.VH)
                                v = t.gen_index("v", bb, o, hh)
                                pe.wait_ge(t.gen_free[v % 2], i * (t.NG // 2) + v // 2 + 1 + t.b0)
                            pe.wait_ge(t.norm, i * 2 + bb + t.n0 - (0 if L == 2 else 1))
                        ob, col = (4 + h // 8, h % 8 * dh) if L == 2 else (4 + bb, h * dh)
                        for k in range(NKT):
                            m = pe.matmul(bank[ob][0:S, col:col + dh], pTv[:, g % 2, k, :],
                                          Vv(bb, t.W)[:, k, h * dh:(h + 1) * dh],
                                          start=(k == 0), stop=(k == NKT - 1))
                        m.then_inc(t.pv, 1)

        def att_vector(dve, t):
            L, H, dh, per = t.L, t.H, t.dh, t.per
            n_chain = t.ch0
            if t.masked:
                dve.wait_ge(loaded["mask"], 32)
                m = maski if L == 0 else maskb
                dve.tensor_scalar(maskf[:, :], m[:, :], 0.0, t.a["fill"], ALU.is_equal, ALU.mult)\
                    .then_inc(t.chain, 1)
                dve.tensor_scalar(sm[:, 0, :], m[:, :], 0.0, None, ALU.not_equal).then_inc(t.chain, 1)
                dve.wait_ge(t.chain, n_chain + 2)
                dve.tensor_reduce(flag[:, 0:1], sm[:, 0, :], AX_X, ALU.max).then_inc(t.chain, 1)
                dve.wait_ge(t.chain, n_chain + 3)
                if L == 0:
                    dve.reciprocal(flag[:, 1:2], flag[:, 0:1]).then_inc(t.chain, 1)
                else:
                    dve.tensor_scalar(flag[:, 1:2], flag[:, 0:1], 1e-9, None, ALU.max).then_inc(t.chain, 1)
                    dve.wait_ge(t.chain, n_chain + 4)
                    dve.reciprocal(flag[:, 1:2], flag[:, 1:2]).then_inc(t.chain, 1)
                n_chain += 4 if L == 0 else 5
                dve.wait_ge(t.chain, n_chain)
                dve.tensor_tensor(fac[:, :], flag[:, 0:1], flag[:, 1:2], ALU.mult).then_inc(t.chain, 1)
                n_chain += 1
                dve.wait_ge(t.chain, n_chain)
            if L == 1:
                dve.wait_ge(loaded["bias1"], 48)
            if t.a["bo"]:
                dve.wait_ge(loaded["bias0"] if L == 0 else loaded["bo2"], 16 * (4 if L == 0 else 1))
                dve.tensor_tensor(x[:, :].rearrange("p (b d) -> p b d", d=D),
                                  x[:, :].rearrange("p (b d) -> p b d", d=D),
                                  boB[0:S, :].unsqueeze(1).broadcast_to([S, B, D]), ALU.add)\
                    .then_inc(t.chain, 1)
                n_chain += 1
                dve.wait_ge(t.chain, n_chain)
            NC = t.NC
            assert n_chain == t.ch0 + t.prep
            qscale = -t.a["scale"]
            with dve.Fori(0, B // 2) as i:
                def gen(kind, bb, o, h, n):
                    k = n % 2
                    src = bank[6 + k]
                    if kind in ("k", "t") or (kind == "v" and not t.a["bv"]):
                        return
                    dve.wait_ge(t.gen_ready, i * t.NG + n + 1 + t.g0)
                    if kind == "q":
                        if H == 1:
                            ins = dve.tensor_scalar(qmv[:, bb, o, :], src[:, 0:S], biasA[:, 0, o:o + 1],
                                                    qscale, ALU.add, ALU.mult)
                        elif t.a["bq"]:
                            ins = dve.scalar_tensor_tensor(
                                out=qmv[:, bb, o * per:(o + 1) * per, :],
                                in0=src[:, 0:S].unsqueeze(1).broadcast_to([P, per, S]),
                                scalar=biasA[:, 0, o:o + 1],
                                in1=sel[dh][:, :].unsqueeze(2).broadcast_to([P, per, S]),
                                op0=ALU.add, op1=ALU.mult)
                        else:
                            ins = dve.tensor_tensor(
                                qmv[:, bb, o * per:(o + 1) * per, :],
                                src[:, 0:S].unsqueeze(1).broadcast_to([P, per, S]),
                                sel[dh][:, :].unsqueeze(2).broadcast_to([P, per, S]), ALU.mult)
                    elif kind == "v":
                        ins = dve.tensor_tensor(Vv(bb, t.W)[:, o, h * t.VW:(h + 1) * t.VW],
                                                src[0:KT, 0:t.VW], bvB[0:KT, :], ALU.add)
                    else:
                        ins = dve.tensor_tensor(xd(i, bb), src[0:S, 0:D], xd(i, bb), ALU.add)
                    ins.then_inc(t.gen_free[k], 1)

                for s in t.plan:
                    if s[0] == "gen":
                        gen(*s[1:])
                        continue
                    at = i * (2 * H) + t.h0
                    if s[0] == "scores":
                        g = s[1]
                        dve.wait_ge(t.scores, at + g + 1)
                        dve.wait_ge(t.probs, at + g - 1)
                        if t.masked:
                            settle(dve)
                            dve.tensor_tensor_reduce(sm[:, g % 2, :], bank[g % 2][0:S, 0:SK], maskf[:, :],
                                                     1.0, 3e38, ALU.add, ALU.min, mx[:, g % 2:g % 2 + 1])\
                                .then_inc(t.maxed, 1)
                        else:
                            dve.tensor_reduce(mx[:, g % 2:g % 2 + 1], bank[g % 2][0:S, 0:SK], AX_X, ALU.min)\
                                .then_inc(t.maxed, 1)
                    elif s[0] == "turn":
                        g = s[1]
                        dve.wait_ge(t.pt_psum, at + g + 1)
                        dve.wait_ge(t.pv, at + g - 1)
                        dve.tensor_copy(pT[:, g % 2, :], bank[2 + g % 2][0:KT, 0:NKT * S])\
                            .then_inc(t.pt_sbuf, 1)
                    elif s[0] == "norm":
                        bb = s[1]
                        c0 = i * (2 * NC) + bb * NC + n_chain
                        dve.wait_ge(t.pv, at + (bb + 1) * H)
                        dve.reciprocal(rinv[:, bb, 0:H], sums[:, bb, 0:H]).then_inc(t.chain, 1)
                        dve.wait_ge(t.chain, c0 + 1)
                        if t.masked:
                            dve.tensor_scalar(rinv[:, bb, 0:H], rinv[:, bb, 0:H], fac[:, 0:1], None, ALU.mult)\
                                .then_inc(t.chain, 1)
                            dve.wait_ge(t.chain, c0 + 2)
                        if L == 1:
                            dve.scalar_tensor_tensor(out=xd(i, bb), in0=bank[4 + bb][0:S, 0:D],
                                                     scalar=rinv[:, bb, 0:1], in1=xd(i, bb),
                                                     op0=ALU.mult, op1=ALU.add).then_inc(t.norm, 1)
                            continue
                        halves = 2 if L == 2 else 1
                        hh = H // halves
                        for q in range(halves):
                            ob = 4 + q if L == 2 else 4 + bb
                            ins = dve.tensor_tensor(
                                on[:, q * hh * dh:(q + 1) * hh * dh].rearrange("p (h d) -> p h d", d=dh),
                                bank[ob][0:S, 0:hh * dh].rearrange("p (h d) -> p h d", d=dh),
                                rinv[:, bb, q * hh:(q + 1) * hh].unsqueeze(2).broadcast_to([S, hh, dh]),
                                ALU.mult)
                        ins.then_inc(t.norm, 1)

        def att_scalar(act, t):
            H = t.H
            if t.a["bk"]:
                act.wait_ge(loaded[f"bias{t.L}"], 16 * (4 if t.L == 0 else 3))
            with act.Fori(0, B // 2) as i:
                for s in t.plan:
                    if s[0] == "gen":
                        _, kind, bb, o, h, n = s
                        if kind in ("q", "o") or (kind == "v" and t.a["bv"]):
                            continue
                        k = n % 2
                        src = bank[6 + k]
                        act.wait_ge(t.gen_ready, i * t.NG + n + 1 + t.g0)
                        if kind == "k":
                            if t.a["bk"]:
                                ins = act.activation(kTv(bb, t.NO)[:, o, :], src[:, 0:SK], ACT.Identity,
                                                     bias=biasA[:, 1, o:o + 1])
                            else:
                                ins = act.activation(kTv(bb, t.NO)[:, o, :], src[:, 0:SK], ACT.Copy)
                        elif kind == "v":
                            ins = act.activation(Vv(bb, t.W)[:, o, h * t.VW:(h + 1) * t.VW],
                                                 src[0:KT, 0:t.VW], ACT.Copy)
                        else:
                            m = min(4, t.NO)
                            ins = act.activation(oTv[:, o:o + m, :],
                                                 src[:, 0:m * S].rearrange("p (o t) -> p o t", t=S), ACT.Copy)
                        ins.then_inc(t.gen_free[k], 1)
                    elif s[0] == "scores":
                        g = s[1]
                        bb, h = g // H, g % H
                        at = i * (2 * H) + t.h0
                        act.wait_ge(t.maxed, at + g + 1)
                        act.wait_ge(t.pt_psum, at + g - 1)
                        if h == 0:
                            act.wait_ge(t.norm, i * 2 + bb - 1 + t.n0)
                        src = sm[:, g % 2, :] if t.masked else bank[g % 2][0:S, 0:SK]
                        act.activation(pr[:, g % 2, :], src, ACT.Exp, bias=mx[:, g % 2:g % 2 + 1], scale=-1.0,
                                       accum_out=sums[:, bb, h:h + 1]).then_inc(t.probs, 1)

        def route(dve, f):
            L, K, NB = f.L, f.K, f.NB
            n = [0]

            def link(ins, mark=None):
                if mark is not None:
                    ins.then_inc(mark, 1)
                    dve.wait_ge(mark, 1)
                else:
                    n[0] += 1
                    ins.then_inc(f.r_chain, 1)
                    dve.wait_ge(f.r_chain, n[0])

            tt, ts = dve.tensor_tensor, dve.tensor_scalar
            be = lambda k: tables[k].rearrange("p (b e) -> p b e", e=E)
            over = lambda a: a.unsqueeze(2).broadcast_to([S, B, E])
            lg, eq, before, rest, full, cum, tot, work = (be(k) for k in range(8))
            pick_of = [be(8), be(9)]
            both = be(10)
            small = lambda k, w: tables[11][:, k * 16:k * 16 + w]
            cnt, nb, end, base, cur = (small(k, E) for k in range(5))
            cmp1 = tab[:, 12 * 128:12 * 128 + E * MAXB].rearrange("p (e k) -> p e k", k=MAXB)
            cmp2 = tab[:, 13 * 128:13 * 128 + NB * E].rearrange("p (j e) -> p j e", e=E)
            eb = tab[:, 16 * 128:16 * 128 + NB]

            def pick(scores, top, first, top_mark=None, first_mark=None):
                link(dve.tensor_reduce(top, scores, AX_X, ALU.max), top_mark)
                link(tt(eq, scores, over(top), ALU.is_equal))
                link(dve.memset(before[:, :, 0:1], 0.0))
                for e in range(1, E):
                    link(tt(before[:, :, e:e + 1], before[:, :, e - 1:e], eq[:, :, e - 1:e], ALU.add))
                link(dve.scalar_tensor_tensor(out=first, in0=before, scalar=0.0, in1=eq,
                                              op0=ALU.is_equal, op1=ALU.mult), first_mark)

            dve.wait_ge(f.r_ps, 1)
            logits = bank[7][0:S, 0:B * E].rearrange("p (b e) -> p b e", e=E)
            if L == 2:
                dve.wait_ge(loaded["r2"], 32)
                link(tt(lg, logits, brB[:, :].unsqueeze(1).broadcast_to([S, B, E]), ALU.add))
            else:
                link(dve.tensor_copy(lg, logits))
            if L == 0:
                pick(lg, t1[0][:, :], pick_of[0], top_mark=f.r_go, first_mark=f.r_mask)
                chosen = pick_of[0]
            else:
                if L == 1:
                    link(dve.tensor_reduce(t1[2][:, :], lg, AX_X, ALU.max))
                    link(tt(work, lg, over(t1[2][:, :]), ALU.subtract), f.r_go)
                    dve.wait_ge(f.r_act, 1)
                    link(dve.tensor_reduce(t1[3][:, :], rest, AX_X, ALU.add))
                    link(dve.reciprocal(t1[4][:, :], t1[3][:, :]))
                    link(tt(lg, rest, over(t1[4][:, :]), ALU.mult))
                pick(lg, t1[0][:, :], pick_of[0])
                link(dve.scalar_tensor_tensor(out=rest, in0=pick_of[0], scalar=-BIG, in1=lg,
                                              op0=ALU.mult, op1=ALU.add))
                pick(rest, t1[1][:, :], pick_of[1])
                link(tt(both, pick_of[0], pick_of[1], ALU.add), f.r_mask)
                chosen = both
                if L == 2:
                    link(tt(t1[2][:, :], t1[1][:, :], t1[0][:, :], ALU.subtract), f.r_go)
            dve.wait_ge(f.r_ps, 2)
            link(dve.tensor_copy(tot, bank[1][0:S, 0:B * E].rearrange("p (b e) -> p b e", e=E)))
            link(dve.memset(cum[:, 0, :], 0.0))
            for b in range(1, B):
                link(tt(cum[:, b, :], cum[:, b - 1, :], tot[:, b - 1, :], ALU.add))
            link(tt(cnt, cum[:, B - 1, :], tot[:, B - 1, :], ALU.add))
            link(dve.scalar_tensor_tensor(out=cmp1, in0=ramp[:, 0:MAXB].unsqueeze(1).broadcast_to([S, E, MAXB]),
                                          scalar=float(ROWS), in1=cnt.unsqueeze(2).broadcast_to([S, E, MAXB]),
                                          op0=ALU.mult, op1=ALU.is_lt))
            link(dve.tensor_reduce(nb, cmp1, AX_X, ALU.add))
            link(dve.tensor_copy(end, nb))
            for e in range(1, E):
                link(tt(end[:, e:e + 1], end[:, e - 1:e], nb[:, e:e + 1], ALU.add))
            link(tt(cur, end, nb, ALU.subtract))
            link(ts(base, cur, float(ROWS), None, ALU.mult))
            link(tt(cmp2, end.unsqueeze(1).broadcast_to([S, NB, E]),
                    ramp[:, 0:NB].unsqueeze(2).broadcast_to([S, NB, E]), ALU.is_le))
            link(dve.tensor_reduce(eb, cmp2, AX_X, ALU.add))
            link(ts(eb, eb, float(E - 1), None, ALU.min))
            link(dve.tensor_copy(ebi[:, 0:NB], eb))
            link(tt(full, bank[0][0:S, 0:B * E].rearrange("p (b e) -> p b e", e=E), cum, ALU.add))
            link(tt(full, full, base.unsqueeze(1).broadcast_to([S, B, E]), ALU.add))
            for k in range(K):
                link(tt(work, full, pick_of[k], ALU.mult))
                link(dve.tensor_reduce(t1[6 + k][:, :], work, AX_X, ALU.add))
                link(dve.tensor_copy(rowid[:, k, :], t1[6 + k][:, :]), f.r_slots if k == K - 1 else None)
            scale, shift = rstd[:, :], nmr[:, :]
            dve.wait_ge(f.r_act, 1)
            if L == 0:
                link(tt(t1[2][:, :], rstd[:, :], t1[1][:, :], ALU.mult))
                link(tt(t1[3][:, :], nmr[:, :], t1[1][:, :], ALU.mult))
                scale, shift = t1[2][:, :], t1[3][:, :]
            for b in range(B):
                ts(xna[:, b * D:(b + 1) * D], xb(b), scale[:, b:b + 1], shift[:, b:b + 1], ALU.mult, ALU.add)\
                    .then_inc(f.r_x, 1)
            if L == 2:
                link(ts(t1[4][:, :], t1[3][:, :], 1.0, None, ALU.add))
                link(dve.reciprocal(t1[4][:, :], t1[4][:, :]))
                link(tt(t1[5][:, :], t1[3][:, :], t1[4][:, :], ALU.mult))

        def route_scalar(act, f):
            act.wait_ge(f.r_go, 1)
            if f.L == 0:
                act.activation(t1[1][:, :], t1[0][:, :], ACT.Sigmoid).then_inc(f.r_act, 1)
            elif f.L == 1:
                act.activation(tables[3], tables[7], ACT.Exp).then_inc(f.r_act, 1)
            else:
                act.activation(t1[3][:, :], t1[2][:, :], ACT.Exp).then_inc(f.r_act, 1)

        def route_tensor(pe, f):
            pe.wait_ge(loaded[f"r{f.L}"], 16 * (2 if f.L == 2 else 1))
            for b in range(B):
                for c in range(ND):
                    m = pe.matmul(bank[7][0:S, b * E:(b + 1) * E], xnT[:, c, b * S:(b + 1) * S], wR[:, c, :],
                                  start=(c == 0), stop=(c == ND - 1))
            m.then_inc(f.r_ps, 1)
            pe.wait_ge(f.r_mask, 1)
            chosen = tables[8] if f.K == 1 else tables[10]
            pe.matmul(bank[0][0:S, 0:B * E], tri[:, :], chosen, start=True, stop=True)
            pe.matmul(bank[1][0:S, 0:B * E], ones[:, :], chosen, start=True, stop=True).then_inc(f.r_ps, 1)
            pe.wait_ge(f.r_slots, 1)

        def shared_sync(sp, f):
            for q in range(f.NS):
                sp.dma_start(wF[:, 1, q * f.size:(q + 1) * f.size], A[f"f{f.L}_shared"][q])\
                    .then_inc(f.w_landed, 16)

        def shared_steps(f):
            return [(q, c, t) for q in range(f.NS) for c in range(NCH) for t in range(f.NF)]

        def shared_tensor(pe, f):
            NF, NU = f.NF, f.NU
            steps = shared_steps(f)
            pe.wait_ge(f.w_landed, 16 * f.NS)

            def hidden(s):
                q, c, t = steps[s]
                up, _ = w_ffn(f, 1, q * f.size)
                o, w = f.tiles[t]
                for u in range(NU):
                    if s * NU >= 4:
                        pe.wait_ge(f.mid if u == NU - 1 else f.act, s - 4 // NU + 1)
                    for k in range(ND):
                        m = pe.matmul(bank[(s * NU + u) % 4][0:w, 0:TOK], up[u][:, k, o:o + w],
                                      xnT[:, k, c * TOK:(c + 1) * TOK], start=(k == 0), stop=(k == ND - 1))
                    m.then_inc(f.hid, 1)

            hidden(0)
            for s, (q, c, t) in enumerate(steps):
                if s + 1 < len(steps):
                    hidden(s + 1)
                _, w2 = w_ffn(f, 1, q * f.size)
                w = f.tiles[t][1]
                cc = q * NCH + c
                if t == 0 and cc >= 2:
                    pe.wait_ge(f.added, cc - 1)
                pe.wait_ge(f.mid, s + 1)
                for j in range(CHUNK):
                    m = pe.matmul(bank[4 + c % 2 * 2 + j // 2][0:S, j % 2 * D:(j % 2 + 1) * D],
                                  mid[0:w, s % 2, j * S:(j + 1) * S], w2[0:w, t, :],
                                  start=(t == 0 and j % 2 == 0), stop=(t == NF - 1), skip_group_check=True)
                m.then_inc(f.out if t == NF - 1 else f.used, 1)
            pe.wait_ge(f.added, NCH * f.NS)

        def shared_mid_free(eng, f, s):
            if s < 2:
                return
            chunk, t = divmod(s - 2, f.NF)
            if t == f.NF - 1:
                eng.wait_ge(f.out, chunk + 1)
            else:
                eng.wait_ge(f.used, chunk * (f.NF - 1) + t + 1)

        def shared_scalar(act, f):
            act.wait_ge(cleared, 16)
            if not f.gated:
                act.wait_ge(f.w_landed, 16 * f.NS)
            for s, (q, c, t) in enumerate(shared_steps(f)):
                w = f.tiles[t][1]
                if f.gated:
                    act.wait_ge(f.hid, s * 2 + 1)
                    if s >= 2:
                        act.wait_ge(f.mid, s - 1)
                    act.activation(hg[0:w, s % 2, 0:TOK], bank[s * 2 % 4][0:w, 0:TOK], ACT.Silu)\
                        .then_inc(f.act, 1)
                else:
                    act.wait_ge(f.hid, s + 1)
                    shared_mid_free(act, f, s)
                    act.activation(mid[0:w, s % 2, :], bank[s % 4][0:w, 0:TOK], ACT.Relu,
                                   bias=wF[0:w, 1, f.at_b1 + t:f.at_b1 + t + 1]).then_inc(f.mid, 1)

        def shared_vector(dve, f, into):
            dve.wait_ge(cleared, 16)
            for s, (q, c, t) in enumerate(shared_steps(f)):
                w = f.tiles[t][1]
                if f.gated:
                    dve.wait_ge(f.hid, s * 2 + 2)
                    dve.wait_ge(f.act, s + 1)
                    shared_mid_free(dve, f, s)
                    dve.tensor_tensor(mid[0:w, s % 2, :], bank[(s * 2 + 1) % 4][0:w, 0:TOK],
                                      hg[0:w, s % 2, 0:TOK], ALU.mult).then_inc(f.mid, 1)
                if t != f.NF - 1:
                    continue
                cc = q * NCH + c
                dve.wait_ge(f.out, cc + 1)
                if cc:
                    dve.wait_ge(f.added, cc)
                for j in range(CHUNK):
                    b = c * CHUNK + j
                    ins = dve.tensor_tensor(into(b), bank[4 + c % 2 * 2 + j // 2][0:S, j % 2 * D:(j % 2 + 1) * D],
                                            into(b), ALU.add)
                ins.then_inc(f.added, 1)

        def rotated(eng, f, ahead, behind):
            ahead(0, 0)
            ahead(1, 1)
            behind(0, 0)
            ahead(2, 0)
            behind(1, 1)
            with eng.Fori(1, f.NB // 2 - 1) as i:
                ahead(i * 2 + 1, 1)
                behind(i * 2, 0)
                ahead(i * 2 + 2, 0)
                behind(i * 2 + 1, 1)
            ahead(f.NB - 1, 1)
            behind(f.NB - 2, 0)
            behind(f.NB - 1, 1)

        def sort_tokens(pool, f):
            pool.wait_ge(f.r_slots, 1)
            pool.wait_ge(cleared, 16)
            for b in range(B):
                pool.wait_ge(f.r_x, b + 1)
                for k in range(f.K):
                    pool.indirect_dma_start(xs[0:f.NB * ROWS, :], bass.IndirectOffsetOnAxis(ap=rowid[:, k, b:b + 1], axis=0),
                                            xna[:, b * D:(b + 1) * D], None).then_inc(f.sorted, 16)

        def blocks_sync(sp, f):
            rows = f.at_out

            def load(n, p):
                expert = sp.value_load(ebi[0:1, bass.ds(n, 1)], min_val=0, max_val=E - 1)
                packed = A[f"f{f.L}_routed"][bass.ds(expert, 1)].rearrange("e p n -> (e p) n")
                first = isinstance(n, int)
                if not first:
                    sp.wait_ge(f.xT_ps, n - 1 + CREDIT)
                sp.dma_start(xblk[:, p, :, :], xs[bass.ds(n * ROWS, ROWS), :].rearrange("(s p) d -> p s d", p=P))\
                    .then_inc(f.bx[p], 16)
                if not first:
                    sp.wait_ge(f.bmid, (n - 1) * f.G + CREDIT)
                sp.dma_start(wF[:, p, 0:rows], packed[:, 0:rows]).then_inc(f.bw[p], 16)
                if not first:
                    sp.wait_ge(f.yb, n - 1 + CREDIT)
                sp.dma_start(wF[:, p, rows:f.size], packed[:, rows:f.size]).then_inc(f.bo[p], 16)

            sp.wait_ge(f.r_slots, 1)
            sp.wait_ge(f.sorted, 16 * B * f.K)
            load(0, 0)
            if f.NS:
                sp.wait_ge(f.out, NCH * f.NS)
            load(1, 1)
            with sp.Fori(1, f.NB // 2) as i:
                load(i * 2, 0)
                load(i * 2 + 1, 1)

        def half_of(f, p, q):
            return (p * f.G + q) % 2

        def blocks_tensor(pe, f):
            NU, G = f.NU, f.G

            def turn(n, p):
                pe.wait_ge(f.bx[p], landed(n, p))
                for k in range(ND):
                    for s in range(2):
                        m = pe.transpose(bank[p][:, (k * 2 + s) * P:(k * 2 + s + 1) * P],
                                         xblk[:, p, s, k * P:(k + 1) * P], ident[:, :])
                m.then_inc(f.xT_ps, 1)

            def hidden(n, p):
                up, _ = w_ffn(f, p)
                pe.wait_ge(f.bw[p], landed(n, p))
                pe.wait_ge(f.xT_sb, n + 1 + CREDIT)
                for q, tiles in enumerate(f.groups):
                    m = n * G + q
                    for u in range(NU):
                        pe.wait_ge(f.bmid if u == NU - 1 else f.bact, m - 1 + CREDIT)
                        for j, (o, w) in enumerate(tiles):
                            for k in range(ND):
                                ins = pe.matmul(bank[2 + 2 * half_of(f, p, q) + u][0:w, j * ROWS:(j + 1) * ROWS],
                                                up[u][:, k, o:o + w], xTb[:, p, k, :],
                                                start=(k == 0), stop=(k == ND - 1))
                        ins.then_inc(f.bhid, 1)

            def ahead(n, p):
                hidden(n, p)
                if not (isinstance(n, int) and n == f.NB - 1):
                    turn(n + 1, 1 - p)

            def behind(n, p):
                _, w2 = w_ffn(f, p)
                pe.wait_ge(f.bo[p], landed(n, p))
                pe.wait_ge(f.bmid, (n + 1) * G + CREDIT)
                pe.wait_ge(f.yb, n - 1 + CREDIT)
                for s in range(2):
                    for t, (o, w) in enumerate(f.tiles):
                        at = t * ROWS + s * P
                        ins = pe.matmul(bank[6 + p][:, s * D:(s + 1) * D], midr[0:w, p, at:at + P], w2[0:w, t, :],
                                        start=(t == 0), stop=(t == f.NF - 1))
                ins.then_inc(f.bout, 1)

            turn(0, 0)
            rotated(pe, f, ahead, behind)

        def landed(n, p):
            return (n - p) * 8 + 16

        def blocks_scalar(act, f):
            G = f.G

            def xT(n, p):
                act.wait_ge(f.xT_ps, n + 1 + CREDIT)
                act.activation(xTb[:, p, :, :], bank[p][:, :].rearrange("p (k t) -> p k t", k=ND),
                               ACT.Copy).then_inc(f.xT_sb, 1)

            def step(n, p, last=False):
                for q, tiles in enumerate(f.groups):
                    m = n * G + q
                    half = half_of(f, p, q)
                    src = bank[2 + 2 * half]
                    if f.gated:
                        act.wait_ge(f.bhid, m * 2 + 1 + CREDIT)
                        act.wait_ge(f.bmid, m - 1 + CREDIT)
                        for j0, j1, w in runs(tiles):
                            ins = act.activation(hg[0:w, half, j0 * ROWS:j1 * ROWS],
                                                 src[0:w, j0 * ROWS:j1 * ROWS], ACT.Silu)
                        ins.then_inc(f.bact, 1)
                    else:
                        act.wait_ge(f.bhid, m + 1 + CREDIT)
                        act.wait_ge(f.bout, n - 1 + CREDIT)
                        for j in range(len(tiles)):
                            t = q * 2 + j
                            ins = act.activation(midr[:, p, t * ROWS:(t + 1) * ROWS],
                                                 src[:, j * ROWS:(j + 1) * ROWS], ACT.Relu,
                                                 bias=wF[:, p, f.at_b1 + t:f.at_b1 + t + 1])
                        ins.then_inc(f.bmid, 1)
                if not last:
                    xT(n + 1, 1 - p)

            xT(0, 0)
            with act.Fori(0, f.NB // 2 - 1) as i:
                step(i * 2, 0)
                step(i * 2 + 1, 1)
            step(f.NB - 2, 0)
            step(f.NB - 1, 1, last=True)

        def runs(tiles):
            full = sum(w == P for _, w in tiles)
            return [(0, full, P)] * (full > 0) + [(j, j + 1, tiles[j][1]) for j in range(full, len(tiles))]

        def blocks_vector(dve, f):
            G = f.G

            def ahead(n, p):
                if not f.gated:
                    return
                for q, tiles in enumerate(f.groups):
                    m = n * G + q
                    half = half_of(f, p, q)
                    dve.wait_ge(f.bhid, m * 2 + 2 + CREDIT)
                    dve.wait_ge(f.bact, m + 1 + CREDIT)
                    dve.wait_ge(f.bout, n - 1 + CREDIT)
                    for j0, j1, w in runs(tiles):
                        ins = dve.tensor_tensor(midr[0:w, p, (q * 2 + j0) * ROWS:(q * 2 + j1) * ROWS],
                                                bank[3 + 2 * half][0:w, j0 * ROWS:j1 * ROWS],
                                                hg[0:w, half, j0 * ROWS:j1 * ROWS], ALU.mult)
                    ins.then_inc(f.bmid, 1)

            def behind(n, p):
                dve.wait_ge(f.bout, n + 1 + CREDIT)
                if not isinstance(n, int) or n >= 2:
                    dve.wait_ge(f.y_store[p], landed(n, p) - 16)
                y = bank[6 + p][:, :].rearrange("p (s d) -> p s d", d=D)
                if f.gated:
                    ins = dve.tensor_copy(yblk[:, p, :, :], y)
                else:
                    ins = dve.tensor_tensor(yblk[:, p, :, :], y, wF[:, p, f.at_b2:f.at_b2 + D]
                                            .unsqueeze(1).broadcast_to([P, 2, D]), ALU.add)
                ins.then_inc(f.yb, 1)

            rotated(dve, f, ahead, behind)

        def store_blocks(pool, f):
            with pool.Fori(0, f.NB // 2) as i:
                for p in range(2):
                    pool.wait_ge(f.yb, i * 2 + p + 1 + CREDIT)
                    settle(pool)
                    pool.dma_start(ys[bass.ds((i * 2 + p) * ROWS, ROWS), :].rearrange("(s p) d -> p s d", p=P),
                                   yblk[:, p, :, :]).then_inc(f.y_store[p], 16)
            for p in range(2):
                pool.wait_ge(f.y_store[p], 8 * f.NB)
            for b in range(B):
                for k in range(f.K):
                    pool.indirect_dma_start(back[k][:, b * D:(b + 1) * D], None, ys[0:f.NB * ROWS, :],
                                            bass.IndirectOffsetOnAxis(ap=rowid[:, k, b:b + 1], axis=0))\
                        .then_inc(f.back, 16)

        def collect(dve, f):
            dve.wait_ge(f.back, 16 * B * f.K)
            n = 0
            for k in range(f.K):
                for b in range(B):
                    src = back[k][:, b * D:(b + 1) * D]
                    if f.L == 0:
                        dve.tensor_tensor(xb(b), src, xb(b), ALU.add)
                    else:
                        g = t1[k] if f.L == 1 else t1[4 + k]
                        if k:
                            dve.wait_ge(f.r_slots, 1 + b + 1)
                        ins = dve.scalar_tensor_tensor(out=xb(b), in0=src, scalar=g[:, b:b + 1], in1=xb(b),
                                                       op0=ALU.mult, op1=ALU.add)
                        if not k:
                            ins.then_inc(f.r_slots, 1)

        def ffn_tensor(pe, f):
            if f.K:
                pe.sem_inc(f.xT_ps, CREDIT)
                pe.sem_inc(f.bhid, CREDIT)
                pe.sem_inc(f.bout, CREDIT)
                route_tensor(pe, f)
            if f.NS:
                shared_tensor(pe, f)
            if f.K:
                blocks_tensor(pe, f)

        def ffn_scalar(act, f):
            if f.K:
                act.sem_inc(f.xT_sb, CREDIT)
                act.sem_inc(f.bact, CREDIT)
                route_scalar(act, f)
            if f.NS:
                shared_scalar(act, f)
            if f.K:
                blocks_scalar(act, f)

        def ffn_vector(dve, f):
            if f.K:
                dve.sem_inc(f.yb, CREDIT)
                if f.gated:
                    dve.sem_inc(f.bmid, CREDIT)
                route(dve, f)
            if f.NS:
                shared_vector(dve, f, xb if f.L < 3 else gx3)
            if f.K:
                blocks_vector(dve, f)
                collect(dve, f)

        yv = V[0:S, :, :].rearrange("p b n -> p (b n)")[:, 0:B * D]
        gx3 = lambda b: yv[:, b * D:(b + 1) * D]

        @block.sync
        def _(sp):
            sp.dma_start(x[:, :].rearrange("p (b d) -> p b d", d=D), A["x"]).then_inc(loaded["x"], 16)
            for k, n in enumerate(("q", "k", "v", "o")):
                sp.dma_start(w_att(0, k), A[f"a0_w{n}"]).then_inc(loaded["w0"], 16)
            sp.dma_start(maski[:, :], A["mask0"]).then_inc(loaded["mask"], 16)
            sp.dma_start(maskb[:, :], A["mask3"].bitcast(U8).rearrange("(s k) -> s k", k=SK))\
                .then_inc(loaded["mask"], 16)
            sp.dma_start(biasA[:, 0, :], A["a0_bq"]).then_inc(loaded["bias0"], 16)
            sp.dma_start(biasA[:, 1, :], A["a0_bk"]).then_inc(loaded["bias0"], 16)
            sp.dma_start(bvB[:, :], A["a0_bv"]).then_inc(loaded["bias0"], 16)
            sp.dma_start(boB[:, :], A["a0_bo"]).then_inc(loaded["bias0"], 16)
            sp.dma_start(wR[:, :, :], A["f0_r"]).then_inc(loaded["r0"], 16)
            for k, n in enumerate(("q", "k", "v", "o")):
                sp.dma_start(w_att(2, k), A[f"a2_w{n}"]).then_inc(loaded["w2"], 16)
            sp.wait_ge(consts, 15)
            sp.dma_start(xs[:, :].rearrange("(j p) d -> p j d", p=P),
                         zero.unsqueeze(1).broadcast_to([P, max(BLOCKS) * ROWS // P, D])).then_inc(cleared, 16)
            shared_sync(sp, ffn[0])
            att_sync(sp, att[0])
            sp.wait_ge(stage_done, 3 * 2)
            for k, n in enumerate(("q", "k", "v")):
                sp.dma_start(w_att(1, k), A[f"a1_w{n}"]).then_inc(loaded["w1"], 16)
            sp.dma_start(biasA[:, 0, :], A["a1_bq"]).then_inc(loaded["bias1"], 16)
            sp.dma_start(biasA[:, 1, :], A["a1_bk"]).then_inc(loaded["bias1"], 16)
            sp.dma_start(bvB[:, :], A["a1_bv"]).then_inc(loaded["bias1"], 16)
            sp.dma_start(boB[:, :], A["a2_bo"]).then_inc(loaded["bo2"], 16)
            blocks_sync(sp, ffn[0])
            sp.wait_ge(stage_done, 3 * 4)
            sp.dma_start(wR[:, :, :], A["f1_r"]).then_inc(loaded["r1"], 16)
            shared_sync(sp, ffn[1])
            att_sync(sp, att[1])
            sp.wait_ge(stage_done, 3 * 6)
            for k, n in enumerate(("q", "k", "v", "o")):
                sp.dma_start(w_att(3, k), A[f"a3_w{n}"]).then_inc(loaded["w3"], 16)
            blocks_sync(sp, ffn[1])
            sp.wait_ge(stage_done, 3 * 8)
            sp.dma_start(wR[:, :, :], A["f2_r"]).then_inc(loaded["r2"], 16)
            sp.dma_start(brB[:, :], A["f2_br"]).then_inc(loaded["r2"], 16)
            att_sync(sp, att[2])
            blocks_sync(sp, ffn[2])
            sp.wait_ge(stage_done, 3 * 12)
            shared_sync(sp, ffn[3])
            att_sync(sp, att[3])
            sp.wait_ge(stage_done, 3 * 14)
            sp.dma_start(gB[:, 0, :], A["f3_gamma"]).then_inc(loaded["gb"], 16)
            sp.dma_start(gB[:, 1, :], A["f3_beta"]).then_inc(loaded["gb"], 16)
            sp.wait_ge(cleared, 16)
            sp.wait_ge(fin, B + 1 + 4 * B)
            sp.dma_start(A["out"], x[:, :].rearrange("p (b d) -> p b d", d=D)).then_inc(stored, 16)
            sp.wait_ge(stored, 16)

        @block.gpsimd
        def _(pool):
            nc.gpsimd.memset(zero, 0.0).then_inc(consts, 1)
            nc.gpsimd.memset(ident[:, :], 0.0).then_inc(consts, 1)
            nc.gpsimd.memset(epsc[:, :], EPS).then_inc(consts, 1)
            nc.gpsimd.memset(sel[16][:, :], -ATT[0]["scale"]).then_inc(consts, 1)
            nc.gpsimd.memset(sel[64][:, :], -ATT[2]["scale"]).then_inc(consts, 1)
            nc.gpsimd.memset(ones[:, :], 1.0).then_inc(consts, 1)
            nc.gpsimd.memset(tri[:, :], 1.0).then_inc(consts, 1)
            nc.gpsimd.iota(rampi[:, :], pattern=[[1, max(BLOCKS)]], base=0, channel_multiplier=0)\
                .then_inc(consts, 1)
            pool.wait_ge(consts, 8)
            nc.gpsimd.tensor_copy(ramp[:, :], rampi[:, :]).then_inc(consts, 1)
            nc.gpsimd.affine_select(out=ident[:, :], in_=ident[:, :], compare_op=ALU.not_equal, fill=1.0,
                                    base=0, pattern=[[-1, P]], channel_multiplier=1).then_inc(consts, 1)
            nc.gpsimd.affine_select(out=tri[:, :], in_=tri[:, :], compare_op=ALU.is_ge, fill=0.0,
                                    base=-1, pattern=[[1, S]], channel_multiplier=-1).then_inc(consts, 1)
            for dh, n in ((16, 8), (64, 2)):
                nc.gpsimd.affine_select(out=sel[dh][:, :], in_=sel[dh][:, :], compare_op=ALU.is_ge, fill=0.0,
                                        base=0, pattern=[[-dh, n]], channel_multiplier=1).then_inc(consts, 1)
            pool.wait_ge(consts, 13)
            for dh, n in ((16, 8), (64, 2)):
                nc.gpsimd.affine_select(out=sel[dh][:, :], in_=sel[dh][:, :], compare_op=ALU.is_ge, fill=0.0,
                                        base=dh - 1, pattern=[[dh, n]], channel_multiplier=-1)\
                    .then_inc(consts, 1)
            for f in ffn[:3]:
                sort_tokens(pool, f)
                store_blocks(pool, f)

        @block.tensor
        def _(pe):
            pe.wait_ge(consts, 15)
            pe.sem_inc(ln.ps, CREDIT)
            pe.sem_inc(att[0].gen_ready, GENS)
            for q in (att[0].scores, att[0].pt_psum, att[0].pv):
                pe.sem_inc(q, CREDIT)
            for L in range(4):
                for t in (att[L], ffn[L]):
                    n = 4 * L + (0 if t is att[L] else 2)
                    ln_tensor(pe, n // 2)
                    finish(pe, n)
                    (att_tensor if t is att[L] else ffn_tensor)(pe, t)
                    finish(pe, n + 1)

        @block.scalar
        def _(act):
            act.wait_ge(consts, 15)
            act.sem_inc(ln.xT, CREDIT)
            act.sem_inc(att[0].probs, CREDIT)
            for L in range(4):
                for t in (att[L], ffn[L]):
                    n = 4 * L + (0 if t is att[L] else 2)
                    ln_scalar(act, n // 2)
                    finish(act, n)
                    (att_scalar if t is att[L] else ffn_scalar)(act, t)
                    finish(act, n + 1)
            ln_std(act, 8)

        @block.vector
        def _(dve):
            dve.wait_ge(consts, 15)
            dve.sem_inc(ln.xn, CREDIT)
            for q in (att[0].maxed, att[0].pt_sbuf, att[0].norm, *att[0].gen_free):
                dve.sem_inc(q, CREDIT)
            dve.wait_ge(loaded["x"], 16)
            for L in range(4):
                for t in (att[L], ffn[L]):
                    n = 4 * L + (0 if t is att[L] else 2)
                    ln_vector(dve, n // 2)
                    finish(dve, n)
                    if t is ffn[3]:
                        dve.wait_ge(t.w_landed, 16)
                        for b in range(B):
                            dve.tensor_scalar(gx3(b), xb(b), rstd[:, b:b + 1], nmr[:, b:b + 1],
                                              ALU.mult, ALU.add).then_inc(fin, 1)
                        dve.wait_ge(fin, B)
                        dve.tensor_tensor(yv.rearrange("p (b d) -> p b d", d=D),
                                          yv.rearrange("p (b d) -> p b d", d=D),
                                          wF[0:S, 1, t.at_b2:t.at_b2 + D].unsqueeze(1).broadcast_to([S, B, D]),
                                          ALU.add).then_inc(fin, 1)
                        dve.wait_ge(fin, B + 1)
                    (att_vector if t is att[L] else ffn_vector)(dve, t)
                    finish(dve, n + 1)
            ln_stats(dve, 8, gx3)
            dve.wait_ge(loaded["gb"], 32)
            done = B + 1
            for b in range(B):
                y = gx3(b)
                for k in range(4):
                    if k == 0:
                        ins = dve.tensor_scalar(y, y, rstd[:, b:b + 1], nmr[:, b:b + 1], ALU.mult, ALU.add)
                    elif k == 1:
                        ins = dve.tensor_tensor(y, y, gB[:, 0, :], ALU.mult)
                    elif k == 2:
                        ins = dve.tensor_tensor(y, y, gB[:, 1, :], ALU.add)
                    else:
                        ins = dve.tensor_tensor(xb(b), xb(b), y, ALU.add)
                    ins.then_inc(fin, 1)
                    done += 1
                    if k < 3:
                        dve.wait_ge(fin, done)


def layout(inp):
    A = {}
    rows = lambda w: np.ascontiguousarray(w.reshape(-1, P, w.shape[-1]).transpose(1, 0, 2))
    cols = lambda v: np.ascontiguousarray(v.reshape(-1, P).T)
    every = lambda v, n: np.ascontiguousarray(np.broadcast_to(v, (n, v.shape[-1])))
    A["x"] = inp["x"].transpose(1, 0, 2)
    A["ctxT"] = inp["ctx_1024"].transpose(0, 2, 1).reshape(B, ND, P, SK).transpose(0, 2, 1, 3)
    A["mask0"] = inp["mask_1x1xSxS2_ik0"].reshape(S, SK)
    A["mask3"] = inp["mask_SxS2_bk0"].reshape(-1).view(np.int32)
    for n in "qkvo":
        A[f"a0_w{n}"] = rows(inp[f"L0_xattn_W_{n}"].T)
        A[f"a2_w{n}"] = rows(inp[f"L2_xattn_W{n}"].T)
        A[f"a3_w{n}"] = rows(inp[f"L3_xattn_W{n}"].T)
        if n != "o":
            A[f"a1_w{n}"] = rows(inp[f"L1_xattn_W{n}"])
    for L, u in ((0, "_"), (1, "")):
        A[f"a{L}_bq"] = cols(inp[f"L{L}_xattn_b{u}q"])
        A[f"a{L}_bk"] = cols(inp[f"L{L}_xattn_b{u}k"])
        A[f"a{L}_bv"] = every(inp[f"L{L}_xattn_b{u}v"], P)
    A["a0_bo"] = every(inp["L0_xattn_b_o"], P)
    A["a2_bo"] = every(inp["L2_xattn_bo"], P)

    def tiled(w):
        e, r, n = w.shape
        t = -(-r // P)
        w = np.concatenate([w, np.zeros((e, t * P - r, n), w.dtype)], 1)
        return w.reshape(e, t, P, n).transpose(0, 2, 1, 3).reshape(e, P, t * n)

    pack = lambda *parts: np.concatenate(parts, 2)
    biases = lambda b1, b2: (b1.reshape(len(b1), -1, P).transpose(0, 2, 1),
                             np.broadcast_to(b2[:, None], (len(b2), P, D)))
    A["f0_r"] = rows(inp["L0_ffn_router_DE"])
    A["f0_routed"] = pack(*(tiled(inp[f"L0_ffn_{n}"]) for n in ("w1_eDF", "w3_eDF", "w2_eFD")))
    A["f0_shared"] = pack(*(tiled(inp[f"L0_ffn_{n}"][None]) for n in ("ws1_DF", "ws3_DF", "ws2_FD")))
    F = FFN[1]["F"]
    w1, w2, s1, s2 = (inp[f"L1_ffn_{n}"] for n in ("W1", "W2", "Ws1", "Ws2"))
    A["f1_r"] = rows(inp["L1_ffn_gate_w"].T)
    swap = lambda w: tiled(w.transpose(0, 2, 1))
    A["f1_routed"] = pack(swap(w1[:, F:]), swap(w1[:, :F]), swap(w2))
    A["f1_shared"] = pack(swap(s1[2 * F:].reshape(2, F, D)), swap(s1[:2 * F].reshape(2, F, D)),
                          tiled(s2.T.reshape(2, F, D)))
    A["f2_r"] = rows(inp["L2_ffn_Wr"])
    A["f2_br"] = every(inp["L2_ffn_br"], S)
    b1, b2 = biases(inp["L2_ffn_b1"], inp["L2_ffn_b2"])
    A["f2_routed"] = pack(tiled(inp["L2_ffn_W1"]), b1, tiled(inp["L2_ffn_W2"]), b2)
    b1, b2 = biases(inp["L3_ffn_b1"][:1], inp["L3_ffn_b2"][:1])
    A["f3_shared"] = pack(tiled(inp["L3_ffn_w1"][:1]), b1, tiled(inp["L3_ffn_w2"][:1]), b2)
    A["f3_gamma"] = every(inp["L3_ffn_gamma"], S)
    A["f3_beta"] = every(inp["L3_ffn_beta"], S)
    return {k: np.ascontiguousarray(v) for k, v in A.items()}


def kernel(**inputs):
    import concourse.bacc as _bacc
    from concourse.bass_utils import run_bass_kernel_spmd as _run

    nc = _bacc.Bacc("TRN2", target_bir_lowering=False, num_devices=1)
    arrays = {f"in_{k}": v for k, v in layout({k: np.asarray(v) for k, v in inputs.items()}).items()}
    aps = {k[3:]: nc.dram_tensor(k, v.shape, mybir.dt.from_np(v.dtype), kind="ExternalInput").ap()
           for k, v in arrays.items()}
    aps["out"] = nc.dram_tensor("out_0", (B, S, D), F32, kind="ExternalOutput").ap().rearrange("b s d -> s b d")
    build(nc, aps)
    r = _run(nc, [arrays], core_ids=[0])
    return r.results[0]["out_0"]
```

```python
from contextlib import ExitStack

import concourse.bass as bass
import numpy as np
from concourse import mybir

F32 = mybir.dt.float32
F32R = mybir.dt.float32r
I32 = mybir.dt.int32
U8 = mybir.dt.uint8
U32 = mybir.dt.uint32
ALU = mybir.AluOpType
ACT = mybir.ActivationFunctionType
AX_X = mybir.AxisListType.X

P = 128
B = 16
S = 112
SK = 375
KT = 125
NKT = SK // KT
SKE = SK + SK % 2
D = 256
ND = D // P
E = 8
CHUNK = 4
NCH = B // CHUNK
TOK = CHUNK * S
CREDIT = 8
GENS = 64
WIDE = 64
EPS = 1e-5
BIG = 1e30

ATT = {
    0: dict(H=16, dh=16, scale=0.25, fill=1e30, bq=True, bk=True, bv=True, wo=True, bo=True),
    1: dict(H=1, dh=256, scale=1 / 16, fill=None, bq=True, bk=True, bv=True, wo=False, bo=False),
    2: dict(H=16, dh=64, scale=0.125, fill=None, bq=False, bk=False, bv=False, wo=True, bo=True),
    3: dict(H=16, dh=16, scale=0.25, fill=1e9, bq=False, bk=False, bv=False, wo=True, bo=False),
}
FFN = {
    0: dict(F=704, shared=1, K=1, gated=True),
    1: dict(F=192, shared=2, K=2, gated=True),
    2: dict(F=512, shared=0, K=2, gated=False),
    3: dict(F=1024, shared=1, K=0, gated=False),
}
ROWS = 2 * P
BLOCKS = [-(-(B * S * f["K"] // ROWS + E - 1) // 2) * 2 for f in FFN.values()]
MAXB = -(-B * S // ROWS)


def ftiles(F):
    return [(o, min(P, F - o)) for o in range(0, F, P)]


class Att:

    def __init__(self, L, sems, before):
        a = ATT[L]
        self.L, self.H, self.dh = L, a["H"], a["dh"]
        self.a = a
        self.W = self.H * self.dh
        self.NO = self.W // P
        self.per = max(1, P // self.dh)
        self.KH = max(1, self.dh // P)
        self.VH = max(1, self.W // 512)
        self.VW = self.W // self.VH
        self.masked = a["fill"] is not None
        self.stack = self.dh == 16
        self.halves = self.W == 1024
        proj = self.proj(0)
        self.NP = sum(s[0] == "gen" for s in proj) if self.stack else 0
        self.ahead = self.numbered(proj, 0) if self.stack else []
        self.plan = self.steps()
        self.last_plan = self.steps(last=True) if self.stack else None
        self.gens = [s for s in self.plan if s[0] == "gen"]
        self.NG = len(self.gens)
        assert self.NG % 2 == 0
        self.gen_ready = sems["gen_ready"]
        self.scores = sems["scores"]
        self.maxed = sems["maxed"]
        self.probs = sems["probs"]
        self.pt_psum = sems["pt_psum"]
        self.pt_sbuf = sems["pt_sbuf"]
        self.pv = sems["pv"]
        self.norm = sems["norm"]
        self.chain = sems["chain"]
        self.ctx_landed = sems["ctx_landed"]
        self.gen_free = sems["gen_free"]
        if self.halves:
            self.halved = sems["halved"]
        if self.stack:
            self.spilled = sems[f"spilled{L}"]
            self.split = sems[f"split{L}"]
            self.stacked, self.stacked8 = sems[f"stacked{L}"], sems[f"stacked8{L}"]
        self.h0 = before.h0 + B * before.H if before else CREDIT
        self.b0 = before.b0 + B // 2 * before.NG // 2 if before else CREDIT
        self.g0 = before.g0 + B // 2 * before.NG if before else GENS
        self.n0 = before.n0 + B if before else CREDIT
        self.c0 = before.c0 + 16 * B // 2 if before else 0
        self.prep = (6 if L == 0 else 7 if L == 3 else 0) + (1 if a["bo"] else 0)
        self.NC = 2 if self.masked else 1
        self.ch0 = before.ch0 + before.prep + B * before.NC if before else 0

    def proj(self, bb):
        qk = [("gen", kind, bb, o, 0) for kind in "qk" for o in range(self.NO)]
        if self.stack:
            qk = qk[0:3] + [("split", bb, 0)] + qk[3:4] + [("split", bb, 1), ("split", bb, 2)]
        return (qk
                + [("gen", "v", bb, kt, h) for kt in range(NKT) for h in range(self.VH)])

    @staticmethod
    def numbered(steps, n):
        out = []
        for s in steps:
            if s[0] == "gen":
                s = s + (n,)
                n += 1
            out.append(s)
        return out

    def steps(self, last=False):
        H = self.H
        late = lambda bb: ([("gen", "t", bb, o, 0) for o in range(0, self.NO, 4)] + [("gen", "o", bb, 0, 0)]
                           if self.a["wo"] else [])
        plan = [] if self.stack else self.proj(0)
        if self.halves:
            plan = [("ctx", 0)] + plan + [("ctx", 1)]
        nxt, done = self.proj(1), []
        for g in range(2 * H + 3):
            if g == H:
                plan += nxt
                nxt = self.proj(2) if self.stack and not last else []
            if g < 2 * H:
                plan.append(("scores", g))
            if 2 <= g < 2 * H + 2:
                plan.append(("turn", g - 2))
            if g >= 3:
                plan.append(("pv", g - 3))
                if (g - 3) % H == H - 1:
                    bb = (g - 3) // H
                    plan.append(("norm", bb))
                    done = late(bb)
            if self.stack:
                k = 1
                while k < len(nxt) and nxt[k - 1][0] == "split":
                    k += 1
                if g > H and nxt and nxt[0][1] == "v":
                    k = {2 * H: 1, 2 * H + 2: 3}.get(g, 0)
                plan += nxt[:k]
                nxt = nxt[k:]
            elif 2 <= g < H:
                k = -(-len(nxt) // max(1, H - g - 1))
                plan += nxt[:k]
                nxt = nxt[k:]
            if done and ((g - 3) % H == 2 or g == 2 * H + 2):
                plan += done
                done = []
        return self.numbered(plan + done, self.NP)

    def gen_index(self, kind, bb, o=0, h=0, plan=None):
        if self.stack and bb == 0 and kind in "qkv":
            return self.gen_index(kind, 2, o, h) - self.NG
        return next(s[5] for s in plan or self.plan if s[0:5] == ("gen", kind, bb, o, h))

    def run(self, eng, body):
        if self.stack:
            with eng.Fori(0, B // 2 - 1) as i:
                body(i, self.plan)
            body(B // 2 - 1, self.last_plan)
        else:
            with eng.Fori(0, B // 2) as i:
                body(i, self.plan)


class Ffn:

    def __init__(self, L, sem):
        f = FFN[L]
        self.L, self.gated, self.F = L, f["gated"], f["F"]
        self.NS, self.K, self.NB = f["shared"], f["K"], BLOCKS[L]
        self.tiles = ftiles(f["F"])
        self.NF = len(self.tiles)
        self.NU = 2 if self.gated else 1
        self.at_b1 = self.NU * ND * self.F
        self.at_out = self.at_b1 + (0 if self.gated else self.NF)
        self.at_b2 = self.at_out + self.NF * D
        self.size = self.at_b2 + (0 if self.gated else D)
        self.groups = [self.tiles[q:q + 2] for q in range(0, self.NF, 2)]
        self.G = len(self.groups)
        n = lambda s: sem(f"l{L}f_{s}")
        if self.NS:
            self.early = NCH * self.NS if not self.K else NCH if self.NS > 1 else NCH - 1
            self.w_landed = n("shared_weights_landed")
            self.hid = n("shared_hidden_ready")
            self.mid = n("shared_mid_ready")
            self.act = n("shared_act_done") if self.gated else self.mid
            self.out = n("shared_out_ready")
            self.used = n("shared_mid_used")
            self.added = n("shared_out_added")
        if self.K:
            self.r_ps = n("router_psum")
            self.r_chain = n("router_chain")
            self.r_go = n("router_to_scalar")
            self.r_act = n("router_act")
            self.r_mask = n("router_choice")
            self.r_slots = n("router_slots")
            self.r_x = n("router_tokens")
            self.sorted = n("tokens_sorted")
            self.bw = [n(f"block_input_weights_landed{k}") for k in range(2)]
            self.bo = [n(f"block_output_weights_landed{k}") for k in range(2)]
            self.bx = [n(f"block_tokens_landed{k}") for k in range(2)]
            self.xT_ps = n("block_xT_psum")
            self.xT_sb = n("block_xT_sbuf")
            self.bhid = n("block_hidden_ready")
            self.bmid = n("block_mid_ready")
            self.bact = n("block_act_done") if self.gated else self.bmid
            self.bout = n("block_out_ready")
            self.yb = n("block_out_sbuf")
            self.y_store = [n(f"block_out_stored{k}") for k in range(2)]
            self.back = [n(f"results_back{k}") for k in range(NCH)]


class Ln:

    def __init__(self, sem):
        self.dve = sem("ln_dve")
        self.act = sem("ln_std")
        self.xn = sem("ln_xn")
        self.ps = sem("ln_psum")
        self.xT = sem("ln_xT")

    def at(self, k):
        return k * (2 * B + 2), k * B // 2 + CREDIT


def build(nc, A):
    ctx = ExitStack()
    with ctx:
        sb = lambda name, shape, dt=F32: ctx.enter_context(nc.sbuf_tensor(name, shape, dt))
        sem = lambda name: ctx.enter_context(nc.semaphore(name))
        bank = [ctx.enter_context(nc.psum_tensor(f"bank{k}", [P, 512], F32)) for k in range(8)]

        x = sb("x", [S, B * D])
        xnT = sb("xnT", [P, ND, B * S])
        ident = sb("ident", [P, P])
        sel = {16: sb("sel16", [P, 8]), 64: sb("sel64", [P, 2])}
        stats = sb("stats", [S, B, 6])
        mv = sb("mv", [S, B, 2])
        std = sb("std", [S, B])
        rstd = sb("rstd", [S, B])
        nmr = sb("nmr", [S, B])
        xn = sb("xn", [S, 2, 2, D])
        epsc = sb("epsc", [P, 1])

        ctxT = sb("ctxT", [P, 2, ND, SKE])
        with nc.sbuf_tensor("kS", [P, 2, 8 * SKE], F32) as kS, nc.sbuf_tensor("qS", [P, 2, 16 * S], F32) as qS:
            pass
        kT = sb("kT", [P, 2, 8 * SKE])
        qm = sb("qm", [P, 2, 16 * S])
        V = sb("V", [KT, 2, NKT * 1024])
        sm = sb("sm", [S, 2, SK])
        pr = sb("pr", [S, 2, SK])
        pT = sb("pT", [KT, 2, NKT * S])
        on = sb("on", [S, 1024])
        oT = sb("oT", [P, max(8 * S, 2 * 512)])
        mx = sb("mx", [S, 2])
        sums = sb("sums", [S, 2, 16])
        rinv = sb("rinv", [S, 2, 16])
        maskf = sb("maskf", [S, SK])
        maski = sb("maski", [S, SK], I32)
        maskb = sb("maskb", [S, SK], U8)
        flag = sb("flag", [S, 2])
        fac = sb("fac", [S, 1])
        with nc.sbuf_tensor("ctx_halves", [P, 2, ND, SKE], F32R) as ctxH:
            pass
        wA = sb("wA", [P, 4, ND * D])
        w2A = sb("w2A", [P, 4, 2048])
        sel2 = sb("sel2", [P, 2])
        wflat = w2A[:, :, :].rearrange("p k n -> p (k n)")
        keys = wflat[:, 0:6 * SKE].rearrange("p (k o t) -> p k o t", k=3, o=2)
        queries = wflat[:, 6 * SKE:6 * SKE + 12 * S].rearrange("p (k o t) -> p k o t", k=3, o=2)
        STACK = 32
        NSTACK = P // STACK
        STACK_DMAS = [2 * NSTACK * 16, NSTACK * 16]
        biasA = sb("biasA", [P, 3, ND])
        bvB = sb("bvB", [P, D])
        boB = sb("boB", [P, D])

        with nc.sbuf_tensor("weight_halves", [P, 2, 2, ND * 1024], F32R) as wH:
            pass
        wF = sb("wF", [P, 2, max(f["F"] * (ND * (1 + f["gated"]) + 2) for f in FFN.values()) + 264])
        hg = oT[:, 0:2 * 512].rearrange("p (b n) -> p b n", b=2)
        mid = sb("mid", [P, 2, TOK])
        wR = sb("wR", [P, ND, E])
        brB = sb("brB", [S, E])
        t1 = [sb(f"t1_{k}", [S, B]) for k in range(8)]
        rowid = sb("rowid", [S, 2, B], U32)
        ebi = sb("ebi", [S, max(BLOCKS)], I32)
        tri = sb("tri", [S, S])
        ones = sb("ones", [S, S])
        ramp = sb("ramp", [S, max(BLOCKS)])
        down = sb("down", [S, E])
        rampi = sb("rampi", [S, max(BLOCKS)], I32)
        zero = mid[:, 0, 0:D]
        cflat = ctxT[:, :, :, :].rearrange("p b k t -> p (b k t)")
        xblk = cflat[:, 0:4 * D].rearrange("p (b s d) -> p b s d", b=2, s=2)
        tab = qm[0:S, :, :].rearrange("p b t -> p (b t)")
        tables = [tab[:, k * B * E:(k + 1) * B * E] for k in range(28)]
        kflat = kT[:, :, :].rearrange("p b n -> p (b n)")
        vflat = V[:, :, :].rearrange("p b n -> p (b n)")
        MIDW = 2 * max(len(ftiles(f["F"])) for f in FFN.values() if f["K"]) * P
        midr = kflat[:, 0:2 * MIDW].rearrange("p (b n) -> p b n", b=2)
        xTb = kflat[:, 2 * MIDW:2 * MIDW + 4 * P * ND].rearrange("p (b k t) -> p b k t", b=2, k=ND)
        yblk = kflat[:, 2 * MIDW + 4 * P * ND:2 * MIDW + 4 * P * ND + 4 * D]            .rearrange("p (b s d) -> p b s d", b=2, s=2)
        back = [kflat[0:S, 0:B * D], vflat[0:S, 0:B * D]]
        xna = vflat[0:S, 0:B * D]
        gB = on[:, 0:2 * D].rearrange("p (k d) -> p k d", d=D)

        consts = sem("constants_ready")
        loaded = {k: sem(f"loaded_{k}") for k in ["x", "w0", "w1", "w2", "w3", "mask", "bias0", "bias1", "bo2",
                                                  "r0", "r1", "r2", "gb"]}
        stage_done = sem("stage_done")
        stored = sem("stored")
        settled = sem("settled")
        names = dict(
            gen_ready="product_ready",
            scores="scores_ready",
            maxed="max_ready",
            probs="probs_ready",
            pt_psum="probsT_in_psum",
            pt_sbuf="probsT_in_sbuf",
            pv="pv_ready",
            norm="heads_normalised",
            chain="attention_chain",
        )
        att_sems = {k: sem(v) for k, v in names.items()}
        att_sems["ctx_landed"] = [sem(f"ctx_landed{k}") for k in range(2)]
        att_sems["gen_free"] = [sem(f"product_evacuated{k}") for k in range(2)]
        for L in (0, 3):
            att_sems[f"spilled{L}"] = [sem(f"l{L}a_spilled{k}") for k in range(3)]
            att_sems[f"stacked8{L}"] = [sem(f"l{L}a_stacked8{k}") for k in range(2)]
            att_sems[f"split{L}"] = sem(f"l{L}a_halves")
            att_sems[f"stacked{L}"] = [sem(f"l{L}a_stacked{k}") for k in range(2)]
        att_sems["halved"] = sem("l2a_halved")
        att = []
        for L in range(4):
            att.append(Att(L, att_sems, att[-1] if att else None))
        ffn = [Ffn(L, sem) for L in range(4)]
        ln = Ln(sem)
        fin = sem("final_chain")

        kTv = lambda p, NO: kT[:, p, 0:NO * SK].rearrange("p (o t) -> p o t", t=SK)
        Vv = lambda p, W: V[:, p, 0:NKT * W].rearrange("p (k w) -> p k w", w=W)
        qmv = qm[:, :, :].rearrange("p b (h t) -> p b h t", t=S)
        prv = pr
        pTv = pT[:, :, :].rearrange("p b (k t) -> p b k t", t=S)
        oTv = oT[:, 0:8 * S].rearrange("p (o t) -> p o t", t=S)
        xb = lambda b: x[:, b * D:(b + 1) * D]
        xd = lambda i, bb: x[:, bass.ds(i * (2 * D) + bb * D, D)]

        def w_att(L, k):
            if L == 2:
                return w2A[:, k, :].rearrange("p (k n) -> p k n", k=ND if k < 3 else 8)
            return wA[:, k, :].rearrange("p (k n) -> p k n", k=ND)

        def w_ffn(f, slot, off=0):
            n = ND * f.F
            up = [wF[:, slot, off + u * n:off + (u + 1) * n].rearrange("p (k f) -> p k f", k=ND)
                  for u in range(f.NU)]
            w2 = wF[:, slot, off + f.at_out:off + f.at_b2]
            return up, w2.rearrange("p (t n) -> p t n", n=D)

        khalves = [nc.dram_tensor(f"key_halves{o}", (2, P, SKE), F32).ap() for o in range(2)]
        qhalves = nc.dram_tensor("query_halves", (2, 2 * P, 2 * S), F32).ap()
        xs = nc.dram_tensor("sorted_tokens", (max(BLOCKS) * ROWS, D), F32).ap()
        ys = nc.dram_tensor("sorted_results", (max(BLOCKS) * ROWS, D), F32).ap()
        cleared = sem("sorted_tokens_cleared")

        block = ctx.enter_context(nc.Block())

        def finish(eng, n):
            eng.drain().then_inc(stage_done, 1)
            eng.wait_ge(stage_done, 3 * (n + 1))

        def settle(eng):
            eng.sem_inc(settled, 1)

        def ln_stats(dve, k, of):
            at, _ = ln.at(k)
            for b in range(0 if k in (2, 4, 6) else B):
                dve.bn_stats(stats[:, b, :], of(b)).then_inc(ln.dve, 1)
            for b in range(B):
                dve.wait_ge(ln.dve, at + b + 1)
                dve.bn_aggr(mv[:, b, :], stats[:, b, :]).then_inc(ln.dve, 1)
            dve.wait_ge(ln.act, k + 1)
            dve.reciprocal(rstd[:, :], std[:, :]).then_inc(ln.dve, 1)
            dve.wait_ge(ln.dve, at + 2 * B + 1)
            dve.scalar_tensor_tensor(out=nmr[:, :], in0=mv[:, :, 0], scalar=-1.0, in1=rstd[:, :],
                                     op0=ALU.mult, op1=ALU.mult).then_inc(ln.dve, 1)
            dve.wait_ge(ln.dve, at + 2 * B + 2)

        def ln_std(act, k):
            act.wait_ge(ln.dve, ln.at(k)[0] + 2 * B)
            act.activation(std[:, :], mv[:, :, 1], ACT.Sqrt, bias=epsc[0:S, :]).then_inc(ln.act, 1)

        def ln_vector(dve, k):
            ln_stats(dve, k, xb)
            _, at = ln.at(k)
            with dve.Fori(0, B // 4) as i:
                for p in range(2):
                    dve.wait_ge(ln.ps, i * 2 + p + at - 1)
                    for bb in range(2):
                        b = i * 4 + p * 2 + bb
                        ins = dve.tensor_scalar(xn[:, p, bb, :], x[:, bass.ds(i * (4 * D) + (p * 2 + bb) * D, D)],
                                                rstd[:, bass.ds(b, 1)], nmr[:, bass.ds(b, 1)], ALU.mult, ALU.add)
                    ins.then_inc(ln.xn, 1)

        def ln_scalar(act, k):
            ln_std(act, k)
            _, at = ln.at(k)
            with act.Fori(0, B // 4) as i:
                for p in range(2):
                    act.wait_ge(ln.ps, i * 2 + p + at + 1)
                    settle(act)
                    act.activation(xnT[:, :, bass.ds((i * 4 + p * 2) * S, 2 * S)],
                                   bank[p][:, 0:ND * 2 * S].rearrange("p (k t) -> p k t", k=ND),
                                   ACT.Copy).then_inc(ln.xT, 1)

        def ln_tensor(pe, k):
            _, at = ln.at(k)
            with pe.Fori(0, B // 4) as i:
                for p in range(2):
                    pe.wait_ge(ln.xn, i * 2 + p + at + 1)
                    pe.wait_ge(ln.xT, i * 2 + p + at - 1)
                    for c in range(ND):
                        for bb in range(2):
                            t = pe.transpose(bank[p][:, (c * 2 + bb) * S:(c * 2 + bb + 1) * S],
                                             xn[:, p, bb, c * P:(c + 1) * P], ident[0:S, 0:S])
                    t.then_inc(ln.ps, 1)

        def att_sync(sp, t):
            with sp.Fori(0, B // 2) as i:
                for bb in range(2):
                    last = t.gen_index("v", bb, NKT - 1, t.VH - 1)
                    sp.wait_ge(t.gen_ready, i * t.NG + last + 1 - t.NG + t.g0)
                    sp.dma_start(ctxT[:, bb, :, :],
                                 A["ctxT"][bass.ds(i * 2 + bb, 1), :, :, :].rearrange("a p k t -> (a p) k t"))\
                        .then_inc(t.ctx_landed[bb], 16)

        def att_tensor(pe, t):
            L, H, dh, per = t.L, t.H, t.dh, t.per
            w = [w_att(L, k) for k in range(4)]
            pe.wait_ge(loaded[f"w{L}"], 16 * (4 if t.a["wo"] else 3))
            def body(i, plan):
                def gen(kind, bb, o, h, n):
                    k = n % 2
                    dst = bank[6 + k]
                    pe.wait_ge(t.gen_free[k], i * (t.NG // 2) + n // 2 + t.b0)
                    if kind == "q":
                        for c in range(ND):
                            m = pe.matmul(dst[:, 0:S], w[0][:, c, o * P:(o + 1) * P],
                                          xnT[:, c, bass.ds((i * 2 + bb) * S, S)],
                                          start=(c == 0), stop=(c == ND - 1))
                    elif t.halves and kind in "kv":
                        if o == 0 and kind == "k":
                            pe.wait_ge(t.halved, i * 4 + bb * 2 + 6)
                        for c in range(ND):
                            for wh, ch in ((0, 0), (0, 1), (1, 0)):
                                flags = dict(start=(c + wh + ch == 0), stop=(c == ND - 1 and wh == 1))
                                if kind == "k":
                                    m = pe.matmul(dst[:, 0:SKE],
                                                  wH[:, 0, wh, c * t.W + o * P:c * t.W + (o + 1) * P],
                                                  ctxH[:, ch, c, :], **flags)
                                else:
                                    m = pe.matmul(dst[0:KT + 1, 0:t.VW], ctxH[:, ch, c, o * KT:(o + 1) * KT + 1],
                                                  wH[:, 1, wh, c * t.W + h * t.VW:c * t.W + (h + 1) * t.VW],
                                                  **flags)
                    elif kind == "k":
                        if o == 0:
                            pe.wait_ge(t.ctx_landed[bb % 2], (i + bb // 2) * 16 + 16 + t.c0)
                        for c in range(ND):
                            m = pe.matmul(dst[:, 0:SK], w[1][:, c, o * P:(o + 1) * P], ctxT[:, bb % 2, c, 0:SK],
                                          start=(c == 0), stop=(c == ND - 1))
                    elif kind == "v":
                        for c in range(ND):
                            m = pe.matmul(dst[0:KT, 0:t.VW], ctxT[:, bb % 2, c, o * KT:(o + 1) * KT],
                                          w[2][:, c, h * t.VW:(h + 1) * t.VW],
                                          start=(c == 0), stop=(c == ND - 1))
                    elif kind == "t":
                        if o == 0:
                            pe.wait_ge(t.norm, i * 2 + bb + 1 + t.n0)
                        for j in range(min(4, t.NO)):
                            m = pe.transpose(dst[:, j * S:(j + 1) * S], on[:, (o + j) * P:(o + j + 1) * P],
                                             ident[0:S, 0:S])
                    else:
                        last = t.gen_index("t", bb, (t.NO - 1) // 4 * 4, plan=plan)
                        pe.wait_ge(t.gen_free[last % 2], i * (t.NG // 2) + last // 2 + 1 + t.b0)
                        for j in range(t.NO):
                            m = pe.matmul(dst[0:S, 0:D], oTv[:, j, :], w[3][:, j, :],
                                          start=(j == 0), stop=(j == t.NO - 1))
                    m.then_inc(t.gen_ready, 1)

                for s in plan:
                    if s[0] == "gen":
                        gen(*s[1:])
                        continue
                    g = s[1]
                    if s[0] in ("norm", "split", "ctx"):
                        continue
                    bb, h = g // H, g % H
                    at = i * (2 * H) + t.h0
                    if s[0] == "scores":
                        if h == 8 and t.stack:
                            pe.wait_ge(t.stacked8[bb], i * STACK_DMAS[1] + STACK_DMAS[1])
                        if h == 0 and t.stack:
                            pe.wait_ge(t.stacked[bb], i * STACK_DMAS[0] + STACK_DMAS[0])
                        elif h == 0:
                            for o in range(t.NO - 2, t.NO):
                                n = t.gen_index("k", bb, o)
                                pe.wait_ge(t.gen_free[n % 2], i * (t.NG // 2) + n // 2 + 1 + t.b0)
                        pe.wait_ge(t.maxed if t.masked else t.probs, at + g - 1)
                        if t.stack:
                            m = pe.matmul(bank[g % 2][0:S, 0:SKE], qS[:, bb, h * S:(h + 1) * S].bitcast(F32R),
                                          kS[:, bb, h // 2 * SKE:(h // 2 + 1) * SKE].bitcast(F32R),
                                          start=True, stop=True)
                        for c in range(0 if t.stack else t.KH):
                            m = pe.matmul(bank[g % 2][0:S, 0:SK], qmv[:, bb, h * t.KH + c, :],
                                          kTv(bb, t.NO)[:, h // per * t.KH + c, :],
                                          start=(c == 0), stop=(c == t.KH - 1))
                        m.then_inc(t.scores, 1)
                    elif s[0] == "turn":
                        pe.wait_ge(t.probs, at + g + 1)
                        pe.wait_ge(t.pt_sbuf, at + g - 1)
                        for k in range(NKT):
                            m = pe.transpose(bank[2 + g % 2][0:KT, k * S:(k + 1) * S],
                                             prv[:, g % 2, k * KT:(k + 1) * KT], ident[0:S, 0:S])
                        m.then_inc(t.pt_psum, 1)
                    else:
                        pe.wait_ge(t.pt_sbuf, at + g + 1)
                        if h == 0:
                            for n in range(2):
                                o, hh = divmod(NKT * t.VH - 1 - n, t.VH)
                                v = t.gen_index("v", bb, o, hh)
                                pe.wait_ge(t.gen_free[v % 2], i * (t.NG // 2) + v // 2 + 1 + t.b0)
                            pe.wait_ge(t.norm, i * 2 + bb + t.n0 - (0 if L == 2 else 1))
                        ob, col = (4 + h // 8, h % 8 * dh) if L == 2 else (4 + bb, h * dh)
                        wide = min(WIDE, t.W - h * dh) if t.stack else dh
                        for k in range(NKT):
                            m = pe.matmul(bank[ob][0:S, col:col + wide], pTv[:, g % 2, k, :],
                                          Vv(bb, t.W)[:, k, h * dh:h * dh + wide],
                                          start=(k == 0), stop=(k == NKT - 1))
                        m.then_inc(t.pv, 1)

            if t.stack:
                body(0, t.ahead)
                for k in range(2):
                    pe.wait_ge(t.gen_free[k], t.b0 + (t.NP + 1 - k) // 2)
            t.run(pe, body)

        def att_vector(dve, t):
            L, H, dh, per = t.L, t.H, t.dh, t.per
            n_chain = t.ch0
            if t.masked:
                dve.wait_ge(loaded["mask"], 32)
                m = maski if L == 0 else maskb
                dve.tensor_scalar(maskf[:, :], m[:, :], 0.0, t.a["fill"], ALU.is_equal, ALU.mult)\
                    .then_inc(t.chain, 1)
                dve.tensor_scalar(sm[:, 0, :], m[:, :], 0.0, None, ALU.not_equal).then_inc(t.chain, 1)
                dve.wait_ge(t.chain, n_chain + 2)
                dve.tensor_reduce(flag[:, 0:1], sm[:, 0, :], AX_X, ALU.max).then_inc(t.chain, 1)
                dve.wait_ge(t.chain, n_chain + 3)
                if L == 0:
                    dve.reciprocal(flag[:, 1:2], flag[:, 0:1]).then_inc(t.chain, 1)
                else:
                    dve.tensor_scalar(flag[:, 1:2], flag[:, 0:1], 1e-9, None, ALU.max).then_inc(t.chain, 1)
                    dve.wait_ge(t.chain, n_chain + 4)
                    dve.reciprocal(flag[:, 1:2], flag[:, 1:2]).then_inc(t.chain, 1)
                n_chain += 4 if L == 0 else 5
                dve.wait_ge(t.chain, n_chain)
                dve.tensor_tensor(fac[:, :], flag[:, 0:1], flag[:, 1:2], ALU.mult).then_inc(t.chain, 1)
                n_chain += 1
                dve.wait_ge(t.chain, n_chain)
            if L == 1:
                dve.wait_ge(loaded["bias1"], 48)
            if t.a["bo"]:
                dve.wait_ge(loaded["bias0"] if L == 0 else loaded["bo2"], 16 * (4 if L == 0 else 1))
                dve.tensor_tensor(x[:, :].rearrange("p (b d) -> p b d", d=D),
                                  x[:, :].rearrange("p (b d) -> p b d", d=D),
                                  boB[0:S, :].unsqueeze(1).broadcast_to([S, B, D]), ALU.add)\
                    .then_inc(t.chain, 1)
                n_chain += 1
                dve.wait_ge(t.chain, n_chain)
            if t.stack:
                dve.memset(keys[:, 0, :, SK:SKE], 0.0).then_inc(t.chain, 1)
                n_chain += 1
                dve.wait_ge(t.chain, n_chain)
            NC = t.NC
            assert n_chain == t.ch0 + t.prep
            qscale = -t.a["scale"]

            def halve(upper, lower, of, n):
                dve.tensor_copy(upper, of).then_inc(t.halved, 1)
                dve.wait_ge(t.halved, n + 1)
                dve.tensor_tensor(lower, of, upper.bitcast(F32), ALU.subtract).then_inc(t.halved, 1)

            def halve_context(i, bb):
                dve.wait_ge(t.ctx_landed[bb], i * 16 + 16 + t.c0)
                n = t.gen_index("v", 1 - bb, NKT - 1, t.VH - 1) + 1 - (0 if bb else t.NG)
                dve.wait_ge(t.gen_ready, i * t.NG + n + t.g0)
                halve(ctxH[:, 0], ctxH[:, 1], ctxT[:, bb, :, :], i * 4 + bb * 2 + 4)

            if t.halves:
                dve.wait_ge(loaded["w2"], 64)
                for n in range(2):
                    halve(wH[:, n, 0, :], wH[:, n, 1, :], w2A[:, 1 + n, :], n * 2)


            def split(i, bb, plan, part):
                a = queries if part == 0 else keys[:, :, part - 1:part, :]
                kind, o = ("q", 1) if part == 0 else ("k", part - 1)
                if plan is t.ahead:
                    m = next(s[-1] for s in plan if s[0:4] == ("gen", kind, 0, o))
                else:
                    m = t.gen_index(kind, bb, o, plan=plan)
                dve.wait_ge(t.gen_free[m % 2], i * (t.NG // 2) + m // 2 + 1 + t.b0)
                if part == 0:
                    m -= 1
                    dve.wait_ge(t.gen_free[m % 2], i * (t.NG // 2) + m // 2 + 1 + t.b0)
                at = i * 12 + bb * 6 + part * 2
                if part and bb:
                    former, n = (t.stacked8, STACK_DMAS[1]) if part == 2 else (t.stacked, STACK_DMAS[0])
                    dve.wait_ge(former[bb - 1], i * n + n)
                dve.tensor_copy(a[:, 1].bitcast(F32R), a[:, 0]).then_inc(t.split, 1)
                dve.wait_ge(t.split, at + 1)
                dve.tensor_tensor(a[:, 2].bitcast(F32R), a[:, 0], a[:, 1], ALU.subtract).then_inc(t.split, 1)

            def body(i, plan):
                def gen(kind, bb, o, h, n):
                    k = n % 2
                    src = bank[6 + k]
                    if kind in ("k", "t") or (kind == "v" and not t.a["bv"]):
                        return
                    dve.wait_ge(t.gen_ready, i * t.NG + n + 1 + t.g0)
                    if kind == "q" and t.stack:
                        if bb:
                            dve.wait_ge(t.stacked[bb - 1], i * STACK_DMAS[0] + STACK_DMAS[0])
                        out = queries[:, 0, o, :].rearrange("p (e s) -> p e s", e=2)
                        q2 = src[:, 0:S].unsqueeze(1).broadcast_to([P, 2, S])
                        by_parity = sel2[:, :].unsqueeze(2).broadcast_to([P, 2, S])
                        if t.a["bq"]:
                            ins = dve.scalar_tensor_tensor(out=out, in0=q2, scalar=biasA[:, 0, o:o + 1],
                                                           in1=by_parity, op0=ALU.add, op1=ALU.mult)
                        else:
                            ins = dve.tensor_tensor(out, q2, by_parity, ALU.mult)
                    elif kind == "q":
                        if H == 1:
                            ins = dve.tensor_scalar(qmv[:, bb, o, :], src[:, 0:S], biasA[:, 0, o:o + 1],
                                                    qscale, ALU.add, ALU.mult)
                        else:
                            ins = dve.tensor_tensor(
                                qmv[:, bb, o * per:(o + 1) * per, :],
                                src[:, 0:S].unsqueeze(1).broadcast_to([P, per, S]),
                                sel[dh][:, :].unsqueeze(2).broadcast_to([P, per, S]), ALU.mult)
                    elif kind == "v":
                        ins = dve.tensor_tensor(Vv(bb % 2, t.W)[:, o, h * t.VW:(h + 1) * t.VW],
                                                src[0:KT, 0:t.VW], bvB[0:KT, :], ALU.add)
                    else:
                        ins = dve.tensor_tensor(xd(i, bb), src[0:S, 0:D], xd(i, bb), ALU.add)
                    ins.then_inc(t.gen_free[k], 1)

                for s in plan:
                    if s[0] == "gen":
                        gen(*s[1:])
                        continue
                    at = i * (2 * H) + t.h0
                    if s[0] == "scores":
                        g = s[1]
                        dve.wait_ge(t.scores, at + g + 1)
                        dve.wait_ge(t.probs, at + g - 1)
                        if t.masked:
                            settle(dve)
                            dve.tensor_tensor_reduce(sm[:, g % 2, :], bank[g % 2][0:S, 0:SK], maskf[:, :],
                                                     1.0, 3e38, ALU.add, ALU.min, mx[:, g % 2:g % 2 + 1])\
                                .then_inc(t.maxed, 1)
                        else:
                            dve.tensor_reduce(mx[:, g % 2:g % 2 + 1], bank[g % 2][0:S, 0:SK], AX_X, ALU.min)\
                                .then_inc(t.maxed, 1)
                    elif s[0] == "turn" and not t.stack:
                        g = s[1]
                        dve.wait_ge(t.pt_psum, at + g + 1)
                        dve.wait_ge(t.pv, at + g - 1)
                        dve.tensor_copy(pT[:, g % 2, :], bank[2 + g % 2][0:KT, 0:NKT * S])\
                            .then_inc(t.pt_sbuf, 1)
                    elif s[0] == "ctx":
                        halve_context(i, s[1])
                    elif s[0] == "split":
                        split(i, s[1], plan, s[2])
                    elif s[0] == "norm":
                        bb = s[1]
                        c0 = i * (2 * NC) + bb * NC + n_chain
                        dve.wait_ge(t.pv, at + (bb + 1) * H)
                        dve.reciprocal(rinv[:, bb, 0:H], sums[:, bb, 0:H]).then_inc(t.chain, 1)
                        dve.wait_ge(t.chain, c0 + 1)
                        if t.masked:
                            dve.tensor_scalar(rinv[:, bb, 0:H], rinv[:, bb, 0:H], fac[:, 0:1], None, ALU.mult)\
                                .then_inc(t.chain, 1)
                            dve.wait_ge(t.chain, c0 + 2)
                        if L == 1:
                            dve.scalar_tensor_tensor(out=xd(i, bb), in0=bank[4 + bb][0:S, 0:D],
                                                     scalar=rinv[:, bb, 0:1], in1=xd(i, bb),
                                                     op0=ALU.mult, op1=ALU.add).then_inc(t.norm, 1)
                            continue
                        halves = 2 if L == 2 else 1
                        hh = H // halves
                        for q in range(halves):
                            ob = 4 + q if L == 2 else 4 + bb
                            ins = dve.tensor_tensor(
                                on[:, q * hh * dh:(q + 1) * hh * dh].rearrange("p (h d) -> p h d", d=dh),
                                bank[ob][0:S, 0:hh * dh].rearrange("p (h d) -> p h d", d=dh),
                                rinv[:, bb, q * hh:(q + 1) * hh].unsqueeze(2).broadcast_to([S, hh, dh]),
                                ALU.mult)
                        ins.then_inc(t.norm, 1)

            if t.stack:
                body(0, t.ahead)
            t.run(dve, body)

        def att_scalar(act, t):
            H = t.H
            if t.a["bk"]:
                act.wait_ge(loaded[f"bias{t.L}"], 16 * (4 if t.L == 0 else 3))

            def exponentials(i, g):
                bb, h = g // H, g % H
                at = i * (2 * H) + t.h0
                act.wait_ge(t.maxed, at + g + 1)
                act.wait_ge(t.pt_psum, at + g - 1)
                if h == 0:
                    act.wait_ge(t.norm, i * 2 + bb - 1 + t.n0)
                src = sm[:, g % 2, :] if t.masked else bank[g % 2][0:S, 0:SK]
                act.activation(pr[:, g % 2, :], src, ACT.Exp, bias=mx[:, g % 2:g % 2 + 1], scale=-1.0,
                               accum_out=sums[:, bb, h:h + 1]).then_inc(t.probs, 1)

            def body(i, plan):
                for s in plan:
                    if s[0] == "gen":
                        _, kind, bb, o, h, n = s
                        if kind in ("q", "o") or (kind == "v" and t.a["bv"]):
                            continue
                        k = n % 2
                        src = bank[6 + k]
                        act.wait_ge(t.gen_ready, i * t.NG + n + 1 + t.g0)
                        if kind == "k":
                            out = keys[:, 0, o, 0:SK] if t.stack else kTv(bb, t.NO)[:, o, :]
                            if t.stack and bb:
                                former, n = (t.stacked8, STACK_DMAS[1]) if o else (t.stacked, STACK_DMAS[0])
                                act.wait_ge(former[bb - 1], i * n + n)
                            if t.a["bk"]:
                                ins = act.activation(out, src[:, 0:SK], ACT.Identity,
                                                     bias=biasA[:, 1, o:o + 1])
                            else:
                                ins = act.activation(out, src[:, 0:SK], ACT.Copy)
                        elif kind == "v":
                            ins = act.activation(Vv(bb % 2, t.W)[:, o, h * t.VW:(h + 1) * t.VW],
                                                 src[0:KT, 0:t.VW], ACT.Copy)
                        else:
                            m = min(4, t.NO)
                            ins = act.activation(oTv[:, o:o + m, :],
                                                 src[:, 0:m * S].rearrange("p (o t) -> p o t", t=S), ACT.Copy)
                        ins.then_inc(t.gen_free[k], 1)
                    elif s[0] == "scores":
                        if not t.stack or s[1] < 2:
                            exponentials(i, s[1])
                    elif s[0] == "turn" and t.stack:
                        g = s[1]
                        at = i * (2 * H) + t.h0
                        act.wait_ge(t.pt_psum, at + g + 1)
                        act.wait_ge(t.pv, at + g - 1)
                        act.activation(pT[:, g % 2, :], bank[2 + g % 2][0:KT, 0:NKT * S], ACT.Copy)\
                            .then_inc(t.pt_sbuf, 1)
                        if g + 2 < 2 * H:
                            exponentials(i, g + 2)

            if t.stack:
                body(0, t.ahead)
            t.run(act, body)

        def stack_sync(sp, t):
            def batch(b, bb):
                spill = lambda a: a.rearrange("h (o p) t -> p h o t", p=P)
                pairs = "(g r) t -> r g t"
                to_k = kS[:, bb, :].rearrange("p (g t) -> p g t", t=SKE)
                to_q = qS[:, bb, :].rearrange("p (g t) -> p g t", t=2 * S)
                sp.wait_ge(t.split, b * 6 + 2)
                settle(sp)
                sp.dma_start(spill(qhalves), queries[:, 1:3]).then_inc(t.spilled[0], 16)
                for o in range(2):
                    sp.wait_ge(t.split, b * 6 + 4 + o * 2)
                    settle(sp)
                    sp.dma_start(spill(khalves[o]), keys[:, 1:3, o:o + 1, :]).then_inc(t.spilled[1 + o], 16)
                    if o == 0:
                        if not (isinstance(b, int) and b == 0):
                            sp.wait_ge(t.scores, b * t.H - t.H + t.h0)
                            settle(sp)
                        sp.wait_ge(t.spilled[0], b * 16 + 16)
                        settle(sp)
                        for part in range(NSTACK):
                            sp.dma_start(to_q[part * STACK:(part + 1) * STACK],
                                         qhalves[part // 2].rearrange(pairs, r=STACK)).then_inc(t.stacked[bb], 16)
                    sp.wait_ge(t.spilled[1 + o], b * 16 + 16)
                    settle(sp)
                    for part in range(NSTACK):
                        sp.dma_start(to_k[part * STACK:(part + 1) * STACK, o * NSTACK:(o + 1) * NSTACK, :],
                                     khalves[o][part % 2].rearrange(pairs, r=STACK))\
                            .then_inc(t.stacked8[bb] if o else t.stacked[bb], 16)

            def context(b, bb):
                sp.dma_start(ctxT[:, bb, :, :], A["ctxT"][bass.ds(b, 1), :, :, :].rearrange("a p k t -> (a p) k t"))\
                    .then_inc(t.ctx_landed[bb], 16)

            values = lambda bb: t.gen_index("v", bb, NKT - 1) + 1 + t.g0
            context(0, 0)
            context(1, 1)
            batch(0, 0)
            sp.wait_ge(t.gen_ready, t.NP + t.g0)
            settle(sp)
            context(2, 0)
            with sp.Fori(0, B // 2 - 2) as i:
                batch(i * 2 + 1, 1)
                sp.wait_ge(t.gen_ready, i * t.NG + values(1))
                settle(sp)
                context(i * 2 + 3, 1)
                batch(i * 2 + 2, 0)
                sp.wait_ge(t.gen_ready, i * t.NG + values(2))
                settle(sp)
                context(i * 2 + 4, 0)
            batch(B - 3, 1)
            sp.wait_ge(t.gen_ready, (B // 2 - 2) * t.NG + values(1))
            settle(sp)
            context(B - 1, 1)
            batch(B - 2, 0)
            batch(B - 1, 1)

        def route(dve, f):
            L, K, NB = f.L, f.K, f.NB
            n = [0]

            def link(ins, mark=None):
                if mark is not None:
                    ins.then_inc(mark, 1)
                    dve.wait_ge(mark, 1)
                else:
                    n[0] += 1
                    ins.then_inc(f.r_chain, 1)
                    dve.wait_ge(f.r_chain, n[0])

            tt, ts = dve.tensor_tensor, dve.tensor_scalar
            be = lambda k: tables[k].rearrange("p (b e) -> p b e", e=E)
            over = lambda a: a.unsqueeze(2).broadcast_to([S, B, E])
            lg, eq, before, rest, full, cum, tot, work = (be(k) for k in range(8))
            pick_of = [be(8), be(9)]
            both = be(10)
            small = lambda k, w: tables[11][:, k * 16:k * 16 + w]
            cnt, nb, end, base, cur = (small(k, E) for k in range(5))
            cmp1 = tab[:, 12 * 128:12 * 128 + E * MAXB].rearrange("p (e k) -> p e k", k=MAXB)
            cmp2 = tab[:, 13 * 128:13 * 128 + NB * E].rearrange("p (j e) -> p j e", e=E)
            eb = tab[:, 16 * 128:16 * 128 + NB]

            def pick(scores, top, first, top_mark=None, first_mark=None):
                link(dve.tensor_reduce(top, scores, AX_X, ALU.max), top_mark)
                link(tt(eq, scores, over(top), ALU.is_equal))
                link(tt(eq, eq, down[:, :].unsqueeze(1).broadcast_to([S, B, E]), ALU.mult))
                link(dve.tensor_reduce(t1[5][:, :], eq, AX_X, ALU.max))
                link(tt(first, eq, over(t1[5][:, :]), ALU.is_equal), first_mark)

            dve.wait_ge(f.r_ps, 1)
            logits = bank[7][0:S, 0:B * E].rearrange("p (b e) -> p b e", e=E)
            if L == 2:
                dve.wait_ge(loaded["r2"], 32)
                link(tt(lg, logits, brB[:, :].unsqueeze(1).broadcast_to([S, B, E]), ALU.add))
            else:
                link(dve.tensor_copy(lg, logits))
            if L == 0:
                pick(lg, t1[0][:, :], pick_of[0], top_mark=f.r_go, first_mark=f.r_mask)
                chosen = pick_of[0]
            else:
                if L == 1:
                    link(dve.tensor_reduce(t1[2][:, :], lg, AX_X, ALU.max))
                    link(tt(work, lg, over(t1[2][:, :]), ALU.subtract), f.r_go)
                    dve.wait_ge(f.r_act, 1)
                    link(dve.tensor_reduce(t1[3][:, :], rest, AX_X, ALU.add))
                    link(dve.reciprocal(t1[4][:, :], t1[3][:, :]))
                    link(tt(lg, rest, over(t1[4][:, :]), ALU.mult))
                pick(lg, t1[0][:, :], pick_of[0])
                link(dve.scalar_tensor_tensor(out=rest, in0=pick_of[0], scalar=-BIG, in1=lg,
                                              op0=ALU.mult, op1=ALU.add))
                pick(rest, t1[1][:, :], pick_of[1])
                link(tt(both, pick_of[0], pick_of[1], ALU.add), f.r_mask)
                chosen = both
                if L == 2:
                    link(tt(t1[2][:, :], t1[1][:, :], t1[0][:, :], ALU.subtract), f.r_go)
            dve.wait_ge(f.r_ps, 2)
            link(dve.tensor_copy(tot, bank[1][0:S, 0:B * E].rearrange("p (b e) -> p b e", e=E)))
            src, into = tot, [before, rest, before, cum]
            for d, dst in zip((1, 2, 4, 8), into):
                tt(dst[:, d:, :], src[:, d:, :], src[:, :B - d, :], ALU.add)
                link(dve.tensor_copy(dst[:, :d, :], src[:, :d, :]))
                src = dst
            link(dve.tensor_copy(cnt, cum[:, B - 1, :]))
            link(tt(cum, cum, tot, ALU.subtract))
            link(dve.scalar_tensor_tensor(out=cmp1, in0=ramp[:, 0:MAXB].unsqueeze(1).broadcast_to([S, E, MAXB]),
                                          scalar=float(ROWS), in1=cnt.unsqueeze(2).broadcast_to([S, E, MAXB]),
                                          op0=ALU.mult, op1=ALU.is_lt))
            link(dve.tensor_reduce(nb, cmp1, AX_X, ALU.add))
            link(dve.tensor_copy(end, nb))
            for e in range(1, E):
                link(tt(end[:, e:e + 1], end[:, e - 1:e], nb[:, e:e + 1], ALU.add))
            link(tt(cur, end, nb, ALU.subtract))
            link(ts(base, cur, float(ROWS), None, ALU.mult))
            link(tt(cmp2, end.unsqueeze(1).broadcast_to([S, NB, E]),
                    ramp[:, 0:NB].unsqueeze(2).broadcast_to([S, NB, E]), ALU.is_le))
            link(dve.tensor_reduce(eb, cmp2, AX_X, ALU.add))
            link(ts(eb, eb, float(E - 1), None, ALU.min))
            link(dve.tensor_copy(ebi[:, 0:NB], eb))
            link(tt(full, bank[0][0:S, 0:B * E].rearrange("p (b e) -> p b e", e=E), cum, ALU.add))
            link(tt(full, full, base.unsqueeze(1).broadcast_to([S, B, E]), ALU.add))
            for k in range(K):
                link(tt(work, full, pick_of[k], ALU.mult))
                link(dve.tensor_reduce(t1[6 + k][:, :], work, AX_X, ALU.add))
                link(dve.tensor_copy(rowid[:, k, :], t1[6 + k][:, :]), f.r_slots if k == K - 1 else None)
            scale, shift = rstd[:, :], nmr[:, :]
            dve.wait_ge(f.r_act, 1)
            if L == 0:
                link(tt(t1[2][:, :], rstd[:, :], t1[1][:, :], ALU.mult))
                link(tt(t1[3][:, :], nmr[:, :], t1[1][:, :], ALU.mult))
                scale, shift = t1[2][:, :], t1[3][:, :]
            for b in range(B):
                ts(xna[:, b * D:(b + 1) * D], xb(b), scale[:, b:b + 1], shift[:, b:b + 1], ALU.mult, ALU.add)\
                    .then_inc(f.r_x, 1)
            if L == 2:
                link(ts(t1[4][:, :], t1[3][:, :], 1.0, None, ALU.add))
                link(dve.reciprocal(t1[4][:, :], t1[4][:, :]))
                link(tt(t1[5][:, :], t1[3][:, :], t1[4][:, :], ALU.mult))

        def route_scalar(act, f):
            act.wait_ge(f.r_go, 1)
            if f.L == 0:
                act.activation(t1[1][:, :], t1[0][:, :], ACT.Sigmoid).then_inc(f.r_act, 1)
            elif f.L == 1:
                act.activation(tables[3], tables[7], ACT.Exp).then_inc(f.r_act, 1)
            else:
                act.activation(t1[3][:, :], t1[2][:, :], ACT.Exp).then_inc(f.r_act, 1)

        def route_tensor(pe, f):
            pe.wait_ge(loaded[f"r{f.L}"], 16 * (2 if f.L == 2 else 1))
            for b in range(B):
                for c in range(ND):
                    m = pe.matmul(bank[7][0:S, b * E:(b + 1) * E], xnT[:, c, b * S:(b + 1) * S], wR[:, c, :],
                                  start=(c == 0), stop=(c == ND - 1))
            m.then_inc(f.r_ps, 1)
            pe.wait_ge(f.r_mask, 1)
            chosen = tables[8] if f.K == 1 else tables[10]
            pe.matmul(bank[0][0:S, 0:B * E], tri[:, :], chosen, start=True, stop=True)
            pe.matmul(bank[1][0:S, 0:B * E], ones[:, :], chosen, start=True, stop=True).then_inc(f.r_ps, 1)
            pe.wait_ge(f.r_slots, 1)

        def shared_sync(sp, f, late=False):
            if late:
                sp.wait_ge(f.yb, f.NB - 1 + CREDIT)
            sp.dma_start(wF[:, 0 if late else 1, 0:f.size], A[f"f{f.L}_shared"][f.NS - 1 if late else 0])\
                .then_inc(f.w_landed, 16)

        def shared_steps(f, late):
            steps = [(q, c, t) for q in range(f.NS) for c in range(NCH) for t in range(f.NF)]
            cut = f.early * f.NF
            return [(s, *steps[s]) for s in (range(cut, len(steps)) if late else range(cut))]

        def shared_tensor(pe, f, late=False):
            NF, NU = f.NF, f.NU
            slot = 0 if late else 1
            up, w2 = w_ffn(f, slot)
            pe.wait_ge(f.w_landed, 32 if late else 16)
            if late:
                pe.wait_ge(f.yb, f.NB + CREDIT)

            def hidden(s, q, c, t):
                o, w = f.tiles[t]
                for u in range(NU):
                    if s * NU >= 4:
                        pe.wait_ge(f.mid if u == NU - 1 else f.act, s - 4 // NU + 1)
                    for k in range(ND):
                        m = pe.matmul(bank[(s * NU + u) % 4][0:w, 0:TOK], up[u][:, k, o:o + w],
                                      xnT[:, k, c * TOK:(c + 1) * TOK], start=(k == 0), stop=(k == ND - 1))
                    m.then_inc(f.hid, 1)

            steps = shared_steps(f, late)
            hidden(*steps[0])
            for n, (s, q, c, t) in enumerate(steps):
                if n + 1 < len(steps):
                    hidden(*steps[n + 1])
                w = f.tiles[t][1]
                cc = q * NCH + c
                if t == 0 and cc >= 2:
                    pe.wait_ge(f.added, cc - 1)
                pe.wait_ge(f.mid, s + 1)
                for j in range(CHUNK):
                    m = pe.matmul(bank[4 + c % 2 * 2 + j // 2][0:S, j % 2 * D:(j % 2 + 1) * D],
                                  mid[0:w, s % 2, j * S:(j + 1) * S], w2[0:w, t, :],
                                  start=(t == 0 and j % 2 == 0), stop=(t == NF - 1), skip_group_check=True)
                m.then_inc(f.out if t == NF - 1 else f.used, 1)
            if not late:
                pe.wait_ge(f.added, f.early)

        def shared_mid_free(eng, f, s):
            if s < 2:
                return
            chunk, t = divmod(s - 2, f.NF)
            if t == f.NF - 1:
                eng.wait_ge(f.out, chunk + 1)
            else:
                eng.wait_ge(f.used, chunk * (f.NF - 1) + t + 1)

        def shared_scalar(act, f, late=False):
            act.wait_ge(cleared, 16)
            if not f.gated:
                act.wait_ge(f.w_landed, 16)
            if late:
                act.wait_ge(f.bmid, f.NB * f.G + CREDIT)
            for s, q, c, t in shared_steps(f, late):
                w = f.tiles[t][1]
                if f.gated:
                    act.wait_ge(f.hid, s * 2 + 1)
                    if s >= 2:
                        act.wait_ge(f.mid, s - 1)
                    act.activation(hg[0:w, s % 2, 0:TOK], bank[s * 2 % 4][0:w, 0:TOK], ACT.Silu)\
                        .then_inc(f.act, 1)
                else:
                    act.wait_ge(f.hid, s + 1)
                    shared_mid_free(act, f, s)
                    act.activation(mid[0:w, s % 2, :], bank[s % 4][0:w, 0:TOK], ACT.Relu,
                                   bias=wF[0:w, 1, f.at_b1 + t:f.at_b1 + t + 1]).then_inc(f.mid, 1)

        def shared_vector(dve, f, into, late=False):
            dve.wait_ge(cleared, 16)
            for s, q, c, t in shared_steps(f, late):
                w = f.tiles[t][1]
                if f.gated:
                    dve.wait_ge(f.hid, s * 2 + 2)
                    dve.wait_ge(f.act, s + 1)
                    shared_mid_free(dve, f, s)
                    dve.tensor_tensor(mid[0:w, s % 2, :], bank[(s * 2 + 1) % 4][0:w, 0:TOK],
                                      hg[0:w, s % 2, 0:TOK], ALU.mult).then_inc(f.mid, 1)
                if t != f.NF - 1:
                    continue
                cc = q * NCH + c
                dve.wait_ge(f.out, cc + 1)
                if cc:
                    dve.wait_ge(f.added, cc)
                for j in range(CHUNK):
                    b = c * CHUNK + j
                    ins = dve.tensor_tensor(into(b), bank[4 + c % 2 * 2 + j // 2][0:S, j % 2 * D:(j % 2 + 1) * D],
                                            into(b), ALU.add)
                ins.then_inc(f.added, 1)

        def rotated(eng, f, ahead, behind):
            ahead(0, 0)
            ahead(1, 1)
            behind(0, 0)
            ahead(2, 0)
            behind(1, 1)
            with eng.Fori(1, f.NB // 2 - 1) as i:
                ahead(i * 2 + 1, 1)
                behind(i * 2, 0)
                ahead(i * 2 + 2, 0)
                behind(i * 2 + 1, 1)
            ahead(f.NB - 1, 1)
            behind(f.NB - 2, 0)
            behind(f.NB - 1, 1)

        def sort_tokens(pool, f):
            pool.wait_ge(f.r_slots, 1)
            pool.wait_ge(cleared, 16)
            for b in range(B):
                pool.wait_ge(f.r_x, b + 1)
                for k in range(f.K):
                    pool.indirect_dma_start(xs[0:f.NB * ROWS, :], bass.IndirectOffsetOnAxis(ap=rowid[:, k, b:b + 1], axis=0),
                                            xna[:, b * D:(b + 1) * D], None).then_inc(f.sorted, 16)

        def blocks_sync(sp, f):
            rows = f.at_out

            def load(n, p):
                expert = sp.value_load(ebi[0:1, bass.ds(n, 1)], min_val=0, max_val=E - 1)
                packed = A[f"f{f.L}_routed"][bass.ds(expert, 1)].rearrange("e p n -> (e p) n")
                first = isinstance(n, int)
                if not first:
                    sp.wait_ge(f.xT_ps, n - 1 + CREDIT)
                sp.dma_start(xblk[:, p, :, :], xs[bass.ds(n * ROWS, ROWS), :].rearrange("(s p) d -> p s d", p=P))\
                    .then_inc(f.bx[p], 16)
                if not first:
                    sp.wait_ge(f.bmid, (n - 1) * f.G + CREDIT)
                sp.dma_start(wF[:, p, 0:rows], packed[:, 0:rows]).then_inc(f.bw[p], 16)
                if not first:
                    sp.wait_ge(f.yb, n - 1 + CREDIT)
                sp.dma_start(wF[:, p, rows:f.size], packed[:, rows:f.size]).then_inc(f.bo[p], 16)

            sp.wait_ge(f.r_slots, 1)
            sp.wait_ge(f.sorted, 16 * B * f.K)
            load(0, 0)
            if f.NS:
                sp.wait_ge(f.out, f.early)
            load(1, 1)
            with sp.Fori(1, f.NB // 2) as i:
                load(i * 2, 0)
                load(i * 2 + 1, 1)
            if f.NS:
                shared_sync(sp, f, late=True)

        def half_of(f, p, q):
            return (p * f.G + q) % 2

        def blocks_tensor(pe, f):
            NU, G = f.NU, f.G

            def turn(n, p):
                pe.wait_ge(f.bx[p], landed(n, p))
                for k in range(ND):
                    for s in range(2):
                        m = pe.transpose(bank[p][:, (k * 2 + s) * P:(k * 2 + s + 1) * P],
                                         xblk[:, p, s, k * P:(k + 1) * P], ident[:, :])
                m.then_inc(f.xT_ps, 1)

            def hidden(n, p):
                up, _ = w_ffn(f, p)
                pe.wait_ge(f.bw[p], landed(n, p))
                pe.wait_ge(f.xT_sb, n + 1 + CREDIT)
                for q, tiles in enumerate(f.groups):
                    m = n * G + q
                    for u in range(NU):
                        pe.wait_ge(f.bmid if u == NU - 1 else f.bact, m - 1 + CREDIT)
                        for j, (o, w) in enumerate(tiles):
                            for k in range(ND):
                                ins = pe.matmul(bank[2 + 2 * half_of(f, p, q) + u][0:w, j * ROWS:(j + 1) * ROWS],
                                                up[u][:, k, o:o + w], xTb[:, p, k, :],
                                                start=(k == 0), stop=(k == ND - 1))
                        ins.then_inc(f.bhid, 1)

            def ahead(n, p):
                hidden(n, p)
                if not (isinstance(n, int) and n == f.NB - 1):
                    turn(n + 1, 1 - p)

            def behind(n, p):
                _, w2 = w_ffn(f, p)
                pe.wait_ge(f.bo[p], landed(n, p))
                pe.wait_ge(f.bmid, (n + 1) * G + CREDIT)
                pe.wait_ge(f.yb, n - 1 + CREDIT)
                for s in range(2):
                    for t, (o, w) in enumerate(f.tiles):
                        at = t * ROWS + s * P
                        ins = pe.matmul(bank[6 + p][:, s * D:(s + 1) * D], midr[0:w, p, at:at + P], w2[0:w, t, :],
                                        start=(t == 0), stop=(t == f.NF - 1))
                ins.then_inc(f.bout, 1)

            turn(0, 0)
            rotated(pe, f, ahead, behind)

        def landed(n, p):
            return (n - p) * 8 + 16

        def blocks_scalar(act, f):
            G = f.G

            def xT(n, p):
                act.wait_ge(f.xT_ps, n + 1 + CREDIT)
                act.activation(xTb[:, p, :, :], bank[p][:, :].rearrange("p (k t) -> p k t", k=ND),
                               ACT.Copy).then_inc(f.xT_sb, 1)

            def step(n, p, last=False):
                for q, tiles in enumerate(f.groups):
                    m = n * G + q
                    half = half_of(f, p, q)
                    src = bank[2 + 2 * half]
                    if f.gated:
                        act.wait_ge(f.bhid, m * 2 + 1 + CREDIT)
                        act.wait_ge(f.bmid, m - 1 + CREDIT)
                        for j0, j1, w in runs(tiles):
                            ins = act.activation(hg[0:w, half, j0 * ROWS:j1 * ROWS],
                                                 src[0:w, j0 * ROWS:j1 * ROWS], ACT.Silu)
                        ins.then_inc(f.bact, 1)
                    else:
                        act.wait_ge(f.bhid, m + 1 + CREDIT)
                        act.wait_ge(f.bout, n - 1 + CREDIT)
                        for j in range(len(tiles)):
                            t = q * 2 + j
                            ins = act.activation(midr[:, p, t * ROWS:(t + 1) * ROWS],
                                                 src[:, j * ROWS:(j + 1) * ROWS], ACT.Relu,
                                                 bias=wF[:, p, f.at_b1 + t:f.at_b1 + t + 1])
                        ins.then_inc(f.bmid, 1)
                if not last:
                    xT(n + 1, 1 - p)

            xT(0, 0)
            with act.Fori(0, f.NB // 2 - 1) as i:
                step(i * 2, 0)
                step(i * 2 + 1, 1)
            step(f.NB - 2, 0)
            step(f.NB - 1, 1, last=True)

        def runs(tiles):
            full = sum(w == P for _, w in tiles)
            return [(0, full, P)] * (full > 0) + [(j, j + 1, tiles[j][1]) for j in range(full, len(tiles))]

        def blocks_vector(dve, f):
            G = f.G

            def ahead(n, p):
                if not f.gated:
                    return
                for q, tiles in enumerate(f.groups):
                    m = n * G + q
                    half = half_of(f, p, q)
                    dve.wait_ge(f.bhid, m * 2 + 2 + CREDIT)
                    dve.wait_ge(f.bact, m + 1 + CREDIT)
                    dve.wait_ge(f.bout, n - 1 + CREDIT)
                    for j0, j1, w in runs(tiles):
                        ins = dve.tensor_tensor(midr[0:w, p, (q * 2 + j0) * ROWS:(q * 2 + j1) * ROWS],
                                                bank[3 + 2 * half][0:w, j0 * ROWS:j1 * ROWS],
                                                hg[0:w, half, j0 * ROWS:j1 * ROWS], ALU.mult)
                    ins.then_inc(f.bmid, 1)

            def behind(n, p):
                dve.wait_ge(f.bout, n + 1 + CREDIT)
                if not isinstance(n, int) or n >= 2:
                    dve.wait_ge(f.y_store[p], landed(n, p) - 16)
                y = bank[6 + p][:, :].rearrange("p (s d) -> p s d", d=D)
                if f.gated:
                    ins = dve.tensor_copy(yblk[:, p, :, :], y)
                else:
                    ins = dve.tensor_tensor(yblk[:, p, :, :], y, wF[:, p, f.at_b2:f.at_b2 + D]
                                            .unsqueeze(1).broadcast_to([P, 2, D]), ALU.add)
                ins.then_inc(f.yb, 1)

            rotated(dve, f, ahead, behind)

        def store_blocks(pool, f):
            with pool.Fori(0, f.NB // 2) as i:
                for p in range(2):
                    pool.wait_ge(f.yb, i * 2 + p + 1 + CREDIT)
                    settle(pool)
                    pool.dma_start(ys[bass.ds((i * 2 + p) * ROWS, ROWS), :].rearrange("(s p) d -> p s d", p=P),
                                   yblk[:, p, :, :]).then_inc(f.y_store[p], 16)
            for p in range(2):
                pool.wait_ge(f.y_store[p], 8 * f.NB)
            for b in range(B):
                for k in range(f.K):
                    pool.indirect_dma_start(back[k][:, b * D:(b + 1) * D], None, ys[0:f.NB * ROWS, :],
                                            bass.IndirectOffsetOnAxis(ap=rowid[:, k, b:b + 1], axis=0))\
                        .then_inc(f.back[b // CHUNK], 16)

        def collect(dve, f):
            if f.NS:
                dve.wait_ge(f.added, NCH * f.NS)
            done = 1
            for c in range(NCH):
                dve.wait_ge(f.back[c], 16 * CHUNK * f.K)
                for k in range(f.K):
                    for b in range(c * CHUNK, (c + 1) * CHUNK):
                        src = back[k][:, b * D:(b + 1) * D]
                        if k:
                            dve.wait_ge(f.r_slots, done - CHUNK + 1)
                        if f.L == 0:
                            ins = dve.tensor_tensor(xb(b), src, xb(b), ALU.add)
                        else:
                            g = t1[k] if f.L == 1 else t1[4 + k]
                            ins = dve.scalar_tensor_tensor(out=xb(b), in0=src, scalar=g[:, b:b + 1], in1=xb(b),
                                                           op0=ALU.mult, op1=ALU.add)
                        ins.then_inc(f.r_slots, 1)
                        done += 1
                for j in range(CHUNK):
                    b = c * CHUNK + j
                    dve.wait_ge(f.r_slots, done - CHUNK + 1 + j)
                    dve.bn_stats(stats[:, b, :], xb(b)).then_inc(ln.dve, 1)

        def ffn_tensor(pe, f):
            if f.K:
                pe.sem_inc(f.xT_ps, CREDIT)
                pe.sem_inc(f.bhid, CREDIT)
                pe.sem_inc(f.bout, CREDIT)
                route_tensor(pe, f)
            if f.NS:
                shared_tensor(pe, f)
            if f.K:
                blocks_tensor(pe, f)
            if f.NS and f.K:
                shared_tensor(pe, f, late=True)

        def ffn_scalar(act, f):
            if f.K:
                act.sem_inc(f.xT_sb, CREDIT)
                act.sem_inc(f.bact, CREDIT)
                route_scalar(act, f)
            if f.NS:
                shared_scalar(act, f)
            if f.K:
                blocks_scalar(act, f)
            if f.NS and f.K:
                shared_scalar(act, f, late=True)

        def ffn_vector(dve, f):
            if f.K:
                dve.sem_inc(f.yb, CREDIT)
                if f.gated:
                    dve.sem_inc(f.bmid, CREDIT)
                route(dve, f)
            if f.NS:
                shared_vector(dve, f, xb if f.L < 3 else gx3)
            if f.K:
                blocks_vector(dve, f)
                if f.NS:
                    shared_vector(dve, f, xb, late=True)
                collect(dve, f)

        yv = V[0:S, :, :].rearrange("p b n -> p (b n)")[:, 0:B * D]
        gx3 = lambda b: yv[:, b * D:(b + 1) * D]

        @block.sync
        def _(sp):
            sp.dma_start(x[:, :].rearrange("p (b d) -> p b d", d=D), A["x"]).then_inc(loaded["x"], 16)
            for k, n in enumerate(("q", "k", "v", "o")):
                sp.dma_start(w_att(0, k), A[f"a0_w{n}"]).then_inc(loaded["w0"], 16)
            sp.dma_start(maski[:, :], A["mask0"]).then_inc(loaded["mask"], 16)
            sp.dma_start(maskb[:, :], A["mask3"].bitcast(U8).rearrange("(s k) -> s k", k=SK))\
                .then_inc(loaded["mask"], 16)
            sp.dma_start(biasA[:, 0, :], A["a0_bq"]).then_inc(loaded["bias0"], 16)
            sp.dma_start(biasA[:, 1, :], A["a0_bk"]).then_inc(loaded["bias0"], 16)
            sp.dma_start(bvB[:, :], A["a0_bv"]).then_inc(loaded["bias0"], 16)
            sp.dma_start(boB[:, :], A["a0_bo"]).then_inc(loaded["bias0"], 16)
            sp.dma_start(wR[:, :, :], A["f0_r"]).then_inc(loaded["r0"], 16)
            sp.wait_ge(consts, 16)
            sp.dma_start(xs[:, :].rearrange("(j p) d -> p j d", p=P),
                         zero.unsqueeze(1).broadcast_to([P, max(BLOCKS) * ROWS // P, D])).then_inc(cleared, 16)
            shared_sync(sp, ffn[0])
            stack_sync(sp, att[0])
            sp.wait_ge(stage_done, 3 * 2)
            for k, n in enumerate(("q", "k", "v", "o")):
                sp.dma_start(w_att(2, k), A[f"a2_w{n}"]).then_inc(loaded["w2"], 16)
            for k, n in enumerate(("q", "k", "v")):
                sp.dma_start(w_att(1, k), A[f"a1_w{n}"]).then_inc(loaded["w1"], 16)
            sp.dma_start(biasA[:, 0, :], A["a1_bq"]).then_inc(loaded["bias1"], 16)
            sp.dma_start(biasA[:, 1, :], A["a1_bk"]).then_inc(loaded["bias1"], 16)
            sp.dma_start(bvB[:, :], A["a1_bv"]).then_inc(loaded["bias1"], 16)
            sp.dma_start(boB[:, :], A["a2_bo"]).then_inc(loaded["bo2"], 16)
            blocks_sync(sp, ffn[0])
            sp.wait_ge(stage_done, 3 * 4)
            sp.dma_start(wR[:, :, :], A["f1_r"]).then_inc(loaded["r1"], 16)
            shared_sync(sp, ffn[1])
            att_sync(sp, att[1])
            blocks_sync(sp, ffn[1])
            sp.wait_ge(stage_done, 3 * 8)
            sp.dma_start(wR[:, :, :], A["f2_r"]).then_inc(loaded["r2"], 16)
            sp.dma_start(brB[:, :], A["f2_br"]).then_inc(loaded["r2"], 16)
            att_sync(sp, att[2])
            sp.wait_ge(stage_done, 3 * 10)
            for k, n in enumerate(("q", "k", "v", "o")):
                sp.dma_start(w_att(3, k), A[f"a3_w{n}"]).then_inc(loaded["w3"], 16)
            blocks_sync(sp, ffn[2])
            sp.wait_ge(stage_done, 3 * 12)
            shared_sync(sp, ffn[3])
            stack_sync(sp, att[3])
            sp.wait_ge(stage_done, 3 * 14)
            sp.dma_start(gB[:, 0, :], A["f3_gamma"]).then_inc(loaded["gb"], 16)
            sp.dma_start(gB[:, 1, :], A["f3_beta"]).then_inc(loaded["gb"], 16)
            sp.wait_ge(cleared, 16)
            sp.wait_ge(fin, B + 1 + 4 * B)
            sp.dma_start(A["out"], x[:, :].rearrange("p (b d) -> p b d", d=D)).then_inc(stored, 16)
            sp.wait_ge(stored, 16)

        @block.gpsimd
        def _(pool):
            nc.gpsimd.memset(zero, 0.0).then_inc(consts, 1)
            nc.gpsimd.memset(ident[:, :], 0.0).then_inc(consts, 1)
            nc.gpsimd.memset(epsc[:, :], EPS).then_inc(consts, 1)
            nc.gpsimd.memset(sel[16][:, :], -ATT[0]["scale"]).then_inc(consts, 1)
            nc.gpsimd.memset(sel[64][:, :], -ATT[2]["scale"]).then_inc(consts, 1)
            nc.gpsimd.memset(ones[:, :], 1.0).then_inc(consts, 1)
            nc.gpsimd.memset(tri[:, :], 1.0).then_inc(consts, 1)
            nc.gpsimd.iota(rampi[:, :], pattern=[[1, max(BLOCKS)]], base=0, channel_multiplier=0)\
                .then_inc(consts, 1)
            pool.wait_ge(consts, 8)
            nc.gpsimd.tensor_copy(ramp[:, :], rampi[:, :]).then_inc(consts, 1)
            nc.gpsimd.tensor_scalar(down[:, :], rampi[:, 0:E], -1.0, float(E), ALU.mult, ALU.add)\
                .then_inc(consts, 1)
            nc.gpsimd.affine_select(out=ident[:, :], in_=ident[:, :], compare_op=ALU.not_equal, fill=1.0,
                                    base=0, pattern=[[-1, P]], channel_multiplier=1).then_inc(consts, 1)
            nc.gpsimd.affine_select(out=tri[:, :], in_=tri[:, :], compare_op=ALU.is_ge, fill=0.0,
                                    base=-1, pattern=[[1, S]], channel_multiplier=-1).then_inc(consts, 1)
            for dh, n in ((16, 8), (64, 2)):
                nc.gpsimd.affine_select(out=sel[dh][:, :], in_=sel[dh][:, :], compare_op=ALU.is_ge, fill=0.0,
                                        base=0, pattern=[[-dh, n]], channel_multiplier=1).then_inc(consts, 1)
            pool.wait_ge(consts, 14)
            for dh, n in ((16, 8), (64, 2)):
                nc.gpsimd.affine_select(out=sel[dh][:, :], in_=sel[dh][:, :], compare_op=ALU.is_ge, fill=0.0,
                                        base=dh - 1, pattern=[[dh, n]], channel_multiplier=-1)\
                    .then_inc(consts, 1)
            for f in ffn[:3]:
                sort_tokens(pool, f)
                store_blocks(pool, f)

        @block.tensor
        def _(pe):
            pe.wait_ge(consts, 16)
            pe.sem_inc(ln.ps, CREDIT)
            pe.sem_inc(att[0].gen_ready, GENS)
            for q in (att[0].scores, att[0].pt_psum, att[0].pv):
                pe.sem_inc(q, CREDIT)
            for L in range(4):
                for t in (att[L], ffn[L]):
                    n = 4 * L + (0 if t is att[L] else 2)
                    ln_tensor(pe, n // 2)
                    finish(pe, n)
                    (att_tensor if t is att[L] else ffn_tensor)(pe, t)
                    finish(pe, n + 1)

        @block.scalar
        def _(act):
            act.wait_ge(consts, 16)
            act.sem_inc(ln.xT, CREDIT)
            act.sem_inc(att[0].probs, CREDIT)
            for L in range(4):
                for t in (att[L], ffn[L]):
                    n = 4 * L + (0 if t is att[L] else 2)
                    ln_scalar(act, n // 2)
                    finish(act, n)
                    (att_scalar if t is att[L] else ffn_scalar)(act, t)
                    finish(act, n + 1)
            ln_std(act, 8)

        @block.vector
        def _(dve):
            dve.wait_ge(consts, 16)
            dve.tensor_reduce(sel2[:, :], sel[16][:, :].rearrange("p (j e) -> p e j", e=2), AX_X, ALU.add)\
                .then_inc(consts, 1)
            dve.wait_ge(consts, 17)
            dve.sem_inc(ln.xn, CREDIT)
            for q in (att[0].maxed, att[0].pt_sbuf, att[0].norm, *att[0].gen_free):
                dve.sem_inc(q, CREDIT)
            dve.wait_ge(loaded["x"], 16)
            for L in range(4):
                for t in (att[L], ffn[L]):
                    n = 4 * L + (0 if t is att[L] else 2)
                    ln_vector(dve, n // 2)
                    finish(dve, n)
                    if t is ffn[3]:
                        dve.wait_ge(t.w_landed, 16)
                        for b in range(B):
                            dve.tensor_scalar(gx3(b), xb(b), rstd[:, b:b + 1], nmr[:, b:b + 1],
                                              ALU.mult, ALU.add).then_inc(fin, 1)
                        dve.wait_ge(fin, B)
                        dve.tensor_tensor(yv.rearrange("p (b d) -> p b d", d=D),
                                          yv.rearrange("p (b d) -> p b d", d=D),
                                          wF[0:S, 1, t.at_b2:t.at_b2 + D].unsqueeze(1).broadcast_to([S, B, D]),
                                          ALU.add).then_inc(fin, 1)
                        dve.wait_ge(fin, B + 1)
                    (att_vector if t is att[L] else ffn_vector)(dve, t)
                    finish(dve, n + 1)
            ln_stats(dve, 8, gx3)
            dve.wait_ge(loaded["gb"], 32)
            done = B + 1
            for b in range(B):
                y = gx3(b)
                for k in range(4):
                    if k == 0:
                        ins = dve.tensor_scalar(y, y, rstd[:, b:b + 1], nmr[:, b:b + 1], ALU.mult, ALU.add)
                    elif k == 1:
                        ins = dve.tensor_tensor(y, y, gB[:, 0, :], ALU.mult)
                    elif k == 2:
                        ins = dve.tensor_tensor(y, y, gB[:, 1, :], ALU.add)
                    else:
                        ins = dve.tensor_tensor(xb(b), xb(b), y, ALU.add)
                    ins.then_inc(fin, 1)
                    done += 1
                    if k < 3:
                        dve.wait_ge(fin, done)


def layout(inp):
    A = {}
    rows = lambda w: np.ascontiguousarray(w.reshape(-1, P, w.shape[-1]).transpose(1, 0, 2))
    cols = lambda v: np.ascontiguousarray(v.reshape(-1, P).T)
    every = lambda v, n: np.ascontiguousarray(np.broadcast_to(v, (n, v.shape[-1])))
    A["x"] = inp["x"].transpose(1, 0, 2)
    A["ctxT"] = np.pad(inp["ctx_1024"].transpose(0, 2, 1).reshape(B, ND, P, SK).transpose(0, 2, 1, 3),
                       ((0, 0), (0, 0), (0, 0), (0, SKE - SK)))
    A["mask0"] = inp["mask_1x1xSxS2_ik0"].reshape(S, SK)
    A["mask3"] = inp["mask_SxS2_bk0"].reshape(-1).view(np.int32)
    for n in "qkvo":
        A[f"a0_w{n}"] = rows(inp[f"L0_xattn_W_{n}"].T)
        A[f"a2_w{n}"] = rows(inp[f"L2_xattn_W{n}"].T)
        A[f"a3_w{n}"] = rows(inp[f"L3_xattn_W{n}"].T)
        if n != "o":
            A[f"a1_w{n}"] = rows(inp[f"L1_xattn_W{n}"])
    for L, u in ((0, "_"), (1, "")):
        A[f"a{L}_bq"] = cols(inp[f"L{L}_xattn_b{u}q"])
        A[f"a{L}_bk"] = cols(inp[f"L{L}_xattn_b{u}k"])
        A[f"a{L}_bv"] = every(inp[f"L{L}_xattn_b{u}v"], P)
    A["a0_bo"] = every(inp["L0_xattn_b_o"], P)
    A["a2_bo"] = every(inp["L2_xattn_bo"], P)

    def tiled(w):
        e, r, n = w.shape
        t = -(-r // P)
        w = np.concatenate([w, np.zeros((e, t * P - r, n), w.dtype)], 1)
        return w.reshape(e, t, P, n).transpose(0, 2, 1, 3).reshape(e, P, t * n)

    pack = lambda *parts: np.concatenate(parts, 2)
    biases = lambda b1, b2: (b1.reshape(len(b1), -1, P).transpose(0, 2, 1),
                             np.broadcast_to(b2[:, None], (len(b2), P, D)))
    A["f0_r"] = rows(inp["L0_ffn_router_DE"])
    A["f0_routed"] = pack(*(tiled(inp[f"L0_ffn_{n}"]) for n in ("w1_eDF", "w3_eDF", "w2_eFD")))
    A["f0_shared"] = pack(*(tiled(inp[f"L0_ffn_{n}"][None]) for n in ("ws1_DF", "ws3_DF", "ws2_FD")))
    F = FFN[1]["F"]
    w1, w2, s1, s2 = (inp[f"L1_ffn_{n}"] for n in ("W1", "W2", "Ws1", "Ws2"))
    A["f1_r"] = rows(inp["L1_ffn_gate_w"].T)
    swap = lambda w: tiled(w.transpose(0, 2, 1))
    A["f1_routed"] = pack(swap(w1[:, F:]), swap(w1[:, :F]), swap(w2))
    A["f1_shared"] = pack(swap(s1[2 * F:].reshape(2, F, D)), swap(s1[:2 * F].reshape(2, F, D)),
                          tiled(s2.T.reshape(2, F, D)))
    A["f2_r"] = rows(inp["L2_ffn_Wr"])
    A["f2_br"] = every(inp["L2_ffn_br"], S)
    b1, b2 = biases(inp["L2_ffn_b1"], inp["L2_ffn_b2"])
    A["f2_routed"] = pack(tiled(inp["L2_ffn_W1"]), b1, tiled(inp["L2_ffn_W2"]), b2)
    b1, b2 = biases(inp["L3_ffn_b1"][:1], inp["L3_ffn_b2"][:1])
    A["f3_shared"] = pack(tiled(inp["L3_ffn_w1"][:1]), b1, tiled(inp["L3_ffn_w2"][:1]), b2)
    A["f3_gamma"] = every(inp["L3_ffn_gamma"], S)
    A["f3_beta"] = every(inp["L3_ffn_beta"], S)
    return {k: np.ascontiguousarray(v) for k, v in A.items()}


def kernel(**inputs):
    import concourse.bacc as _bacc
    from concourse.bass_utils import run_bass_kernel_spmd as _run

    nc = _bacc.Bacc("TRN2", target_bir_lowering=False, num_devices=1)
    arrays = {f"in_{k}": v for k, v in layout({k: np.asarray(v) for k, v in inputs.items()}).items()}
    aps = {k[3:]: nc.dram_tensor(k, v.shape, mybir.dt.from_np(v.dtype), kind="ExternalInput").ap()
           for k, v in arrays.items()}
    aps["out"] = nc.dram_tensor("out_0", (B, S, D), F32, kind="ExternalOutput").ap().rearrange("b s d -> s b d")
    build(nc, aps)
    r = _run(nc, [arrays], core_ids=[0])
    return r.results[0]["out_0"]
```
